# Optimizing a Trainium2 kernel written in Bass

```python
import numpy as np
import jax
import jax.numpy as jnp

def _softmax(x, axis=-1):
    return jax.nn.softmax(x, axis=axis)

def _gelu(x):
    return jax.nn.gelu(x, approximate=True)

def _silu(x):
    return jax.nn.silu(x)

def _sigmoid(x):
    return jax.nn.sigmoid(x)

def _layernorm(x, axis=-1, eps=1e-05):
    m = jnp.mean(x, axis=axis, keepdims=True)
    v = jnp.var(x, axis=axis, keepdims=True)
    return (x - m) / jnp.sqrt(v + eps)

def _scatter_add(tgt, idx, src, axis=0):
    return tgt.at[idx].add(src)

def _segment_sum(src, seg, n):
    return jax.ops.segment_sum(src, seg, n)
kernel_name = 'mk_adaln_d1_jaxref_r8_b07b06'

def setup_inputs(seed: int=0):
    np.random.seed(seed)
    _w = jnp.asarray

    def _L0_attn_setup():
        import jax, jax.numpy as jnp
        import numpy as np
        B_SZ, L_SEQ, D_MODEL, D_STATE = (4, 256, 128, 16)

        def _ssm_scan(u, A_log, B_param, C_param, log_dt):
            L = u.shape[1]
            dt = jnp.clip(jnp.exp(log_dt), 0.0001, 1.0)
            A_bar = jnp.exp(-jnp.exp(A_log) * dt[:, None])
            A_bar = jnp.clip(A_bar, 1e-08, 1.0 - 1e-08)
            log_A = jnp.log(A_bar)
            t_idx = jnp.arange(L, dtype=jnp.float32)
            A_powers = jnp.exp(t_idx[:, None, None] * log_A[None, :, :])
            cb_dt = C_param * B_param * dt[:, None]
            kernel = jnp.einsum('ldn,dn->ld', A_powers, cb_dt)
            n_fft = 2 * L
            Kf = jnp.fft.rfft(kernel, n=n_fft, axis=0)
            Uf = jnp.fft.rfft(u, n=n_fft, axis=1)
            y = jnp.fft.irfft(Uf * Kf[None], n=n_fft, axis=1)[:, :L]
            return y.astype(u.dtype)
        key = jax.random.key(seed)
        ks = jax.random.split(key, 6)
        x = jax.random.normal(ks[0], (B_SZ, L_SEQ, D_MODEL), jnp.float32)
        A_log = jnp.clip(jnp.log(jnp.arange(1, D_STATE + 1, dtype=jnp.float32)), -7.0, None)
        A_log = jnp.broadcast_to(A_log[None, :], (D_MODEL, D_STATE)).astype(jnp.float32)
        B_param = 0.02 * jax.random.normal(ks[1], (D_MODEL, D_STATE), jnp.float32)
        C_param = 0.02 * jax.random.normal(ks[2], (D_MODEL, D_STATE), jnp.float32)
        log_dt = 0.01 * jax.random.normal(ks[3], (D_MODEL,), jnp.float32) - 4.0
        in_w = jax.random.normal(ks[4], (2 * D_MODEL, D_MODEL), jnp.float32) / np.sqrt(D_MODEL).astype(np.float32)
        in_b = jnp.zeros((2 * D_MODEL,), jnp.float32)
        out_w = jax.random.normal(ks[5], (D_MODEL, D_MODEL), jnp.float32) / np.sqrt(D_MODEL).astype(np.float32)
        out_b = jnp.zeros((D_MODEL,), jnp.float32)
        ln_g = jnp.ones((D_MODEL,), jnp.float32)
        ln_b = jnp.zeros((D_MODEL,), jnp.float32)
        return {'x': x, 'A_log': A_log, 'B_param': B_param, 'C_param': C_param, 'log_dt': log_dt, 'in_w': in_w, 'in_b': in_b, 'out_w': out_w, 'out_b': out_b, 'ln_g': ln_g, 'ln_b': ln_b}
    _L0_attn_in = _L0_attn_setup()

    def _L0_ffn_setup():
        import jax, jax.numpy as jnp
        import numpy as np
        B, S, D, H, E = (8, 256, 128, 512, 8)
        CAPACITY_FACTOR = 2.0
        LN_EPS = 1e-05

        def _layernorm(x, g, b):
            mu = jnp.mean(x, axis=-1, keepdims=True)
            var = jnp.mean(jnp.square(x - mu), axis=-1, keepdims=True)
            return (x - mu) * jax.lax.rsqrt(var + LN_EPS) * g + b
        if __name__ == '__main__':
            out = reference(**setup_inputs())
            print(out.shape, out.dtype)
        key = jax.random.key(seed)
        ks = jax.random.split(key, 6)
        s = 0.02
        return {'x': jax.random.normal(ks[0], (B, S, D), jnp.float32), 'W_proj': jax.random.normal(ks[1], (D, D), jnp.float32) * s, 'b_proj': jnp.zeros((D,), jnp.float32), 'W_gate': jax.random.normal(ks[2], (D, E), jnp.float32) * s, 'W1': jax.random.normal(ks[3], (E, D, H), jnp.float32) * s, 'b1': jnp.zeros((E, H), jnp.float32), 'ln1_g': jnp.ones((E, H), jnp.float32), 'ln1_b': jnp.zeros((E, H), jnp.float32), 'W2': jax.random.normal(ks[4], (E, H, D), jnp.float32) * s, 'b2': jnp.zeros((E, D), jnp.float32), 'ln_g': jnp.ones((D,), jnp.float32), 'ln_b': jnp.zeros((D,), jnp.float32)}
    _L0_ffn_in = _L0_ffn_setup()
    _L0_c = _w((lambda *s: np.random.randn(*s).astype(np.float32) * 0.05)(4, 128))
    _L0_wmod = _w((lambda *s: np.random.randn(*s).astype(np.float32) * 0.05)(128, 6 * 128) * 128 ** (-0.5))
    _d = {'L0_attn_x': _L0_attn_in['x'], 'L0_attn_A_log': _L0_attn_in['A_log'], 'L0_attn_B_param': _L0_attn_in['B_param'], 'L0_attn_C_param': _L0_attn_in['C_param'], 'L0_attn_log_dt': _L0_attn_in['log_dt'], 'L0_attn_in_w': _L0_attn_in['in_w'], 'L0_attn_in_b': _L0_attn_in['in_b'], 'L0_attn_out_w': _L0_attn_in['out_w'], 'L0_attn_out_b': _L0_attn_in['out_b'], 'L0_attn_ln_g': _L0_attn_in['ln_g'], 'L0_attn_ln_b': _L0_attn_in['ln_b'], 'L0_ffn_W_proj': _L0_ffn_in['W_proj'], 'L0_ffn_b_proj': _L0_ffn_in['b_proj'], 'L0_ffn_W_gate': _L0_ffn_in['W_gate'], 'L0_ffn_W1': _L0_ffn_in['W1'], 'L0_ffn_b1': _L0_ffn_in['b1'], 'L0_ffn_ln1_g': _L0_ffn_in['ln1_g'], 'L0_ffn_ln1_b': _L0_ffn_in['ln1_b'], 'L0_ffn_W2': _L0_ffn_in['W2'], 'L0_ffn_b2': _L0_ffn_in['b2'], 'L0_ffn_ln_g': _L0_ffn_in['ln_g'], 'L0_ffn_ln_b': _L0_ffn_in['ln_b'], 'L0_c': _L0_c, 'L0_wmod': _L0_wmod}
    _x0 = _d['L0_attn_x']
    _d['L0_attn_x'] = jax.random.normal(jax.random.fold_in(jax.random.key(seed), 1), (4, 1024, 128), dtype=_x0.dtype)
    del _x0
    return _d

def reference(L0_attn_x, L0_attn_A_log, L0_attn_B_param, L0_attn_C_param, L0_attn_log_dt, L0_attn_in_w, L0_attn_in_b, L0_attn_out_w, L0_attn_out_b, L0_attn_ln_g, L0_attn_ln_b, L0_ffn_W_proj, L0_ffn_b_proj, L0_ffn_W_gate, L0_ffn_W1, L0_ffn_b1, L0_ffn_ln1_g, L0_ffn_ln1_b, L0_ffn_W2, L0_ffn_b2, L0_ffn_ln_g, L0_ffn_ln_b, L0_c, L0_wmod):

    def _L0_attn_ref(x, A_log, B_param, C_param, log_dt, in_w, in_b, out_w, out_b, ln_g, ln_b):
        import jax, jax.numpy as jnp
        import numpy as np
        B_SZ, L_SEQ, D_MODEL, D_STATE = (4, 256, 128, 16)

        def _ssm_scan(u, A_log, B_param, C_param, log_dt):
            L = u.shape[1]
            dt = jnp.clip(jnp.exp(log_dt), 0.0001, 1.0)
            A_bar = jnp.exp(-jnp.exp(A_log) * dt[:, None])
            A_bar = jnp.clip(A_bar, 1e-08, 1.0 - 1e-08)
            log_A = jnp.log(A_bar)
            t_idx = jnp.arange(L, dtype=jnp.float32)
            A_powers = jnp.exp(t_idx[:, None, None] * log_A[None, :, :])
            cb_dt = C_param * B_param * dt[:, None]
            kernel = jnp.einsum('ldn,dn->ld', A_powers, cb_dt)
            n_fft = 2 * L
            Kf = jnp.fft.rfft(kernel, n=n_fft, axis=0)
            Uf = jnp.fft.rfft(u, n=n_fft, axis=1)
            y = jnp.fft.irfft(Uf * Kf[None], n=n_fft, axis=1)[:, :L]
            return y.astype(u.dtype)
        x = x.astype(jnp.float32)
        residual = x
        mu = jnp.mean(x, axis=-1, keepdims=True)
        var = jnp.mean(jnp.square(x - mu), axis=-1, keepdims=True)
        xn = (x - mu) * jax.lax.rsqrt(var + 1e-05) * ln_g + ln_b
        xz = xn @ in_w.T + in_b
        x_proj, z = (xz[..., :D_MODEL], xz[..., D_MODEL:])
        z = jax.nn.silu(z)
        y = _ssm_scan(x_proj, A_log, B_param, C_param, log_dt)
        y = y * z
        y = y @ out_w.T + out_b
        return jnp.clip(y + residual, -10.0, 10.0)

    def _L0_ffn_ref(x, W_proj, b_proj, W_gate, W1, b1, ln1_g, ln1_b, W2, b2, ln_g, ln_b):
        import jax, jax.numpy as jnp
        import numpy as np
        B, S, D, H, E = (8, 256, 128, 512, 8)
        CAPACITY_FACTOR = 2.0
        LN_EPS = 1e-05

        def _layernorm(x, g, b):
            mu = jnp.mean(x, axis=-1, keepdims=True)
            var = jnp.mean(jnp.square(x - mu), axis=-1, keepdims=True)
            return (x - mu) * jax.lax.rsqrt(var + LN_EPS) * g + b
        if __name__ == '__main__':
            out = reference(**setup_inputs())
            print(out.shape, out.dtype)
        b_, s_, d_ = x.shape
        N = b_ * s_
        capacity = max(int(CAPACITY_FACTOR * N / E), 1)
        x_flat = (jnp.einsum('bsd,de->bse', x, W_proj) + b_proj).reshape(N, d_)
        router_logits = x_flat @ W_gate
        routing_weights = jax.nn.softmax(router_logits, axis=-1)
        ew, ei = jax.lax.top_k(routing_weights, 1)
        ew = ew / jnp.sum(ew, axis=-1, keepdims=True)
        tok_weight = ew[:, 0]
        tok_expert = ei[:, 0]
        assigned = tok_expert[None, :] == jnp.arange(E)[:, None]
        masked = jnp.where(assigned, tok_weight[None, :], -1.0)
        top_scores, top_idx = jax.lax.top_k(masked, capacity)
        valid = top_scores > 0.0
        tok = x_flat[top_idx]
        h = jnp.einsum('ecd,edh->ech', tok, W1) + b1[:, None, :]
        h = _layernorm(h, ln1_g[:, None, :], ln1_b[:, None, :])
        h = jax.nn.gelu(h, approximate=False)
        out_e = jnp.einsum('ech,ehd->ecd', h, W2) + b2[:, None, :]
        w = jnp.where(valid, top_scores, 0.0)[..., None]
        weighted = out_e * w
        outputs = jnp.zeros((N, d_), x.dtype).at[top_idx.reshape(-1)].add(weighted.reshape(-1, d_))
        final = _layernorm(outputs.reshape(b_, s_, d_), ln_g, ln_b)
        return final
    x = L0_attn_x
    mod = (_silu(L0_c) @ L0_wmod).reshape(L0_c.shape[0], 6, 1, -1)
    sa, ca, ga, sb, cb, gb = (mod[:, 0], mod[:, 1], mod[:, 2], mod[:, 3], mod[:, 4], mod[:, 5])
    ga = (2 * (ga >= 0) - 1) * jnp.maximum(jnp.abs(ga), 0.25)
    gb = (2 * (gb >= 0) - 1) * jnp.maximum(jnp.abs(gb), 0.25)
    h = _layernorm(x, axis=-1) * (1 + ca) + sa
    x = x + ga * _L0_attn_ref(h, L0_attn_A_log, L0_attn_B_param, L0_attn_C_param, L0_attn_log_dt, L0_attn_in_w, L0_attn_in_b, L0_attn_out_w, L0_attn_out_b, L0_attn_ln_g, L0_attn_ln_b)
    h = _layernorm(x, axis=-1) * (1 + cb) + sb
    x = x + gb * _L0_ffn_ref(h, L0_ffn_W_proj, L0_ffn_b_proj, L0_ffn_W_gate, L0_ffn_W1, L0_ffn_b1, L0_ffn_ln1_g, L0_ffn_ln1_b, L0_ffn_W2, L0_ffn_b2, L0_ffn_ln_g, L0_ffn_ln_b)
    return x

_drawn_inputs = setup_inputs


def setup_inputs(seed=0):
    import zlib

    import numpy as np

    out = dict(_drawn_inputs(seed))
    spreads = {'L0_attn_in_b': (0.0, 0.8),
     'L0_attn_out_b': (0.0, 0.1),
     'L0_attn_ln_g': (1.0, 0.6),
     'L0_attn_ln_b': (0.0, 0.8),
     'L0_ffn_b_proj': (0.0, 0.1),
     'L0_ffn_b1': (0.0, 0.1),
     'L0_ffn_ln1_g': (1.0, 0.2),
     'L0_ffn_ln1_b': (0.0, 0.359),
     'L0_ffn_b2': (0.0, 0.1),
     'L0_ffn_ln_g': (1.0, 0.2),
     'L0_ffn_ln_b': (0.0, 0.357)}
    factors = {'L0_attn_A_log': 8.0,
     'L0_attn_B_param': 8.0,
     'L0_attn_C_param': 8.0,
     'L0_attn_log_dt': 8.0,
     'L0_attn_in_w': 8.0,
     'L0_attn_out_w': 8.0}
    for name, (base, spread) in spreads.items():
        noise = np.random.default_rng([zlib.crc32(name.encode()), seed]).standard_normal(out[name].shape)
        drawn = base * np.exp(spread * noise) if base else spread * noise
        out[name] = jnp.asarray(drawn.astype(out[name].dtype))
    for name, factor in factors.items():
        out[name] = (out[name] * factor).astype(out[name].dtype)
    return out
```

```python
import concourse.bass as bass
from concourse import mybir
from contextlib import ExitStack

FP32 = mybir.dt.float32
BF16 = mybir.dt.bfloat16
I32 = mybir.dt.int32
ALU = mybir.AluOpType
ACT = mybir.ActivationFunctionType
AX = mybir.AxisListType

P = 128
B, L, D = 4, 1024, 128
NS = 16
IC = L // P
NT = B * IC
N = B * L
E, H = 8, 512
KC = H // P
CAPACITY = int(2.0 * N / E)
MAX_TILES = N // P + E - 1
QD = 32
JQ = P // QD
LN_EPS = 1e-5
LOG_LO = -18.420680743952367
PJ = D + E
RING = 3
AHEAD = 5
TRING = 6


class Steps:

    def __init__(self, eng, sem):
        self.eng, self.sem, self.base, self.n = eng, sem, 0, 0

    def mark(self, ins):
        ins.then_inc(self.sem, 1)
        self.n += 1

    def settle(self):
        self.eng.wait_ge(self.sem, self.base + self.n)

    def enter(self, i, per):
        self.start, self.per = self.base + self.n, per
        self.base, self.n = self.start + i * per, 0

    def leave(self, rounds):
        assert self.n == self.per, (self.n, self.per)
        self.base, self.n = self.start + rounds * self.per, 0


def adaln_program(nc, x, A_log, B_param, C_param, log_dt, in_w, in_b, out_w, out_b, ln_g, ln_b,
                  W_proj, b_proj, W_gate, W1, b1, ln1_g, ln1_b, W2, b2, f_ln_g, f_ln_b, c, wmod, out):
    k_pad = nc.dram_tensor("k_pad", [D, 2 * P], FP32, kind="Internal").ap()
    la_rows = nc.dram_tensor("la_rows", [D, NS], FP32, kind="Internal").ap()
    xf_rows = nc.dram_tensor("xf_rows", [N, D], FP32, kind="Internal").ap()
    y_rows = nc.dram_tensor("y_rows", [N, D], FP32, kind="Internal").ap()

    ctx = ExitStack()
    with ctx:
        def sb(name, shape, dt=FP32):
            return ctx.enter_context(nc.sbuf_tensor(name, shape, dt))

        def sem(name):
            return ctx.enter_context(nc.semaphore(name))

        X = sb("X", [P, B, IC, D])
        Hh = sb("Hh", [P, B, IC, D])
        U = sb("U", [P, IC, B, D])
        Z = sb("Z", [P, IC, B, D])
        BIG = sb("BIG", [P, TRING * 4 * JQ * P])
        T = BIG[:, :].rearrange("p (s g j r) -> p s g j r", s=TRING, g=4, j=JQ)
        W1s = BIG[:, 0:E * H].rearrange("p (e h) -> p e h", e=E)
        W2s = BIG[:, E * H:2 * E * H].rearrange("p (e k d) -> p e k d", e=E, k=KC)
        SBk = sb("SBk", [P, QD, JQ, IC * B])
        V = sb("V", [P, QD, P])
        Wst = sb("Wst", [P, (D + 1) * NS])
        XF = U[:, :, :, :].rearrange("p a b d -> p (a b) d")
        KN = SBk[:, 0:NS].rearrange("p g j m -> p g (j m)")
        NR = sb("NR", [P, IC, D])
        NTt = sb("NTt", [P, IC, P])
        YT2 = V[:, 0:IC, :]
        YS = sb("YS", [P, 2, 4, P])
        St = sb("St", [P, IC, QD, B])
        Stmp = sb("Stmp", [P, QD, B])
        MOD = sb("MOD", [P, B, 4, D])
        GT = YS[:, 0]
        GT2 = YS[:, 1]
        GL = sb("GL", [P, B, D])
        GLB = sb("GLB", [P, B, D])
        lngb = sb("lngb", [P, 2, D])
        scT = sb("scT", [P, B])
        cT = sb("cT", [P, B])
        wm = St[:].rearrange("p i g b -> p (i g b)")[:, 0:6 * D].rearrange("p (m d) -> p m d", m=6)
        cbsT = sb("cbsT", [P, 2, B])
        AL = sb("AL", [P, NS])
        BP = sb("BP", [P, NS])
        CP = sb("CP", [P, NS])
        LD = sb("LD", [P, 1])
        EA = sb("EA", [P, NS])
        DT = sb("DT", [P, 1])
        LA32 = sb("LA32", [P, QD])
        CB32 = sb("CB32", [P, QD])
        LAT = sb("LAT", [P, QD])
        CBT = sb("CBT", [P, QD])
        AQ = sb("AQ", [P, QD])
        KP = sb("KP", [P, 2 * P])
        iota_f = sb("iota_f", [P, P])
        iota_d = sb("iota_d", [P, P])
        iota_d1 = sb("iota_d1", [P, P])
        left = sb("left", [P, 1])
        part = sb("part", [P, 1])
        ident = sb("ident", [P, P])
        lower = sb("lower", [P, P], BF16)
        onesb = sb("onesb", [P, P], BF16)
        ones1 = sb("ones1", [1, P])
        ones3 = sb("ones3", [3, P], BF16)
        inw = NR[:, 1:3, :]
        outw = NR[:, 3, :]
        wpr = sb("wpr", [P, D])
        wgt = sb("wgt", [P, E])
        bpc = sb("bpc", [P, 1])
        lngc = sb("lngc", [P, 1])
        lnbc = sb("lnbc", [P, 1])
        inwT = sb("inwT", [P, 2 * D])
        inwG = sb("inwG", [P, 2 * D])
        outwT = sb("outwT", [P, D])
        wprT = NR[:, 0, :]
        WPG = sb("WPG", [P, PJ])
        WPB = sb("WPB", [P, B, PJ])
        row_in = sb("row_in", [1, 2 * D])
        row_out = sb("row_out", [1, D])
        row_pj = sb("row_pj", [1, PJ])
        row_pb = sb("row_pb", [1, B, PJ])
        gb1 = sb("gb1", [QD, 2, P])
        gb1T = sb("gb1T", [P, 2, E, KC])
        b1n = sb("b1n", [QD, P])
        b1r = sb("b1r", [QD, P])
        b1p = sb("b1p", [QD, 3, P], BF16)
        b2n = sb("b2n", [E, P])
        b2r = sb("b2r", [E, P])
        b2p = sb("b2p", [E, 3, P], BF16)
        BR = BIG[0:3, 2 * E * H:2 * E * H + (E * H + E * D) // 2].bitcast(BF16)
        BR1 = BR[:, 0:E * H].rearrange("p (e h) -> p e h", e=E)
        BR2 = BR[:, E * H:E * (H + D)].rearrange("p (e d) -> p e d", e=E)
        st = sb("st", [P, 2, IC, 6])
        mv = sb("mv", [P, 2, IC, 2])
        ve = sb("ve", [P, 2, IC])
        rs = sb("rs", [P, 2, IC])
        tick = sb("tick", [P, 1])
        half = sb("half", [P, IC])
        flat_w = Wst[:, 0:D * NS]
        LG = flat_w[:, 0:NT * E].rearrange("p (t e) -> p t e", e=E)
        top = sb("top", [P, NT])
        RA, Mf = (NTt[:, 2 * i:2 * i + 2, :].rearrange("p a (t e) -> p (a t) e", e=E) for i in range(2))
        tot, inc, exc, pos = (NR[:, 2 * i:2 * i + 2, :].rearrange("p a (e t) -> p (a e) t", t=NT) for i in range(4))
        sel = NTt[:, 4:6, :].rearrange("p a (e t) -> p (a e) t", t=NT)
        Mb = sb("Mb", [P, NT, E], BF16)
        erev = sb("erev", [P, E])
        k128 = sb("k128", [P, IC])
        seg = sb("seg", [P, E, NT])
        cmpk = flat_w[:, 1024:1024 + E * IC].rearrange("p (e i) -> p e i", e=E)
        nte = sb("nte", [P, E])
        tend = sb("tend", [P, E])
        tbeg = sb("tbeg", [P, E])
        one8 = sb("one8", [P, E])
        slot = sb("slot", [P, NT])
        keep = sb("keep", [P, NT])
        sloti = sb("sloti", [P, NT], I32)
        rowi = sb("rowi", [P, NT], I32)
        tili = sb("tili", [P, NT], I32)
        rowf = sb("rowf", [P, NT])
        tilf = sb("tilf", [P, NT])
        giota = sb("giota", [P, MAX_TILES])
        flat_s = SBk[:].rearrange("p g j m -> p (g j m)")
        OR = flat_s[:, 0:NT * P // 2].bitcast(BF16).rearrange("p (t r) -> p t r", t=NT)
        OT = flat_s[:, NT * P // 2:NT * P // 2 + NT * 3 * MAX_TILES // 2].bitcast(BF16).rearrange(
            "p (t c g) -> p t c g", t=NT, c=3)
        gcmp = V[:, 16:19].rearrange("p g r -> p (g r)")[:, 0:E * MAX_TILES].rearrange("p (e g) -> p e g", e=E)
        texp = sb("texp", [P, MAX_TILES + RING])
        texpi = sb("texpi", [P, MAX_TILES], I32)
        texpr = sb("texpr", [P, MAX_TILES // RING, 8], I32)
        idf = flat_w[:, 640:640 + 3 * MAX_TILES].rearrange("p (c g) -> p c g", c=3)
        idg = flat_w[:, 768:768 + MAX_TILES]
        ids = flat_w[:, 896:896 + MAX_TILES]
        idgi = sb("idgi", [P, MAX_TILES], I32)
        idsi = sb("idsi", [P, MAX_TILES], I32)
        flat_v = V[:].rearrange("p g r -> p (g r)")
        NH = flat_v[:, 0:RING * H].rearrange("p (u h) -> p u h", u=RING)
        AT = flat_v[:, RING * H:2 * RING * H].rearrange("p (u k q) -> p u k q", u=RING, k=KC)
        XG = flat_v[:, 2 * RING * H:2 * RING * H + RING * D].rearrange("p (u d) -> p u d", u=RING)
        XT = flat_v[:, 2 * RING * H + RING * D:2 * RING * (H + D)].rearrange("p (u d) -> p u d", u=RING)
        FO = flat_w[:, NT * E:NT * E + RING * D].rearrange("p (u d) -> p u d", u=RING)
        st1 = sb("st1", [P, RING, 2, 6])
        mv1 = sb("mv1", [P, RING, 2, 2])
        rs1 = sb("rs1", [P, RING, 2])
        ve1 = sb("ve1", [P, RING, 2])

        PS = ctx.enter_context(nc.psum_tensor("PS", [P, 8, 512], FP32))

        s_x = sem("x_loaded")
        s_ssm = sem("ssm_params_loaded")
        s_c = sem("c_loaded")
        s_wm = sem("wmod_loaded")
        s_w = sem("mixer_weights_loaded")
        s_e = sem("expert_vectors_loaded")
        s_bc = sem("final_norm_rows_loaded")
        s_iota = sem("iotas_ready")
        s_id = sem("identity_ready")
        s_one = sem("ones_ready")
        s_silu = sem("silu_c_ready")
        s_ea = sem("decay_exps_ready")
        s_la = sem("log_decay_ready")
        s_kl = sem("kernel_exponents_ready")
        s_ke = sem("kernel_exps_ready")
        s_kp = sem("kernel_ready")
        s_kd = sem("kernel_in_dram")
        s_ld = sem("log_decay_in_dram")
        s_lb = sem("log_decay_broadcast")
        s_wst = sem("state_input_weights_ready")
        s_vl = sem("state_output_exponents_ready")
        s_v = sem("state_output_weights_ready")
        s_aq = sem("chunk_decay_ready")
        s_sbz = sem("block_states_zeroed")
        s_t = [sem(f"toeplitz_loaded{k}") for k in range(8)]
        s_ptr = sem("setup_transposed")
        s_etr = sem("setup_transposes_copied")
        s_mod = sem("modulation_products")
        s_me = sem("modulation_copied")
        s_col = sem("modulation_columns")
        s_inw = sem("in_weights_ready")
        s_r1 = sem("in_bias_product")
        s_r1e = sem("in_bias_ready")
        s_wg = sem("router_weight_product")
        s_wge = sem("router_weight_copied")
        s_r2 = sem("projection_bias_products")
        s_r2e = sem("projection_weights_ready")
        s_gl = sem("final_gates_ready")
        s_b3 = sem("bias_parts_ready")
        s_br = sem("bias_parts_in_rows")
        s_var = sem("variances_ready")
        s_rsd = sem("rstds_ready")
        s_var1 = sem("hidden_variance_ready")
        s_rsd1 = sem("hidden_rstd_ready")
        s_n = sem("norm_rows_ready")
        s_tp = sem("rows_transposed")
        s_nt = sem("transposes_copied")
        s_uz = sem("in_products")
        s_uze = sem("in_products_used")
        s_sin = sem("chunk_inputs")
        s_st = sem("chunk_states_ready")
        s_sbd = sem("block_states_ready")
        s_in = sem("conv_inside_done")
        s_y = sem("conv_bank_done")
        s_ys = sem("conv_bank_copied")
        s_yt = sem("conv_bank_transposed")
        s_yz = sem("gated_bank_ready")
        s_tp2 = sem("gated_rows_transposed")
        s_nt2 = sem("gated_transposes_copied")
        s_op = sem("out_products")
        s_n2 = sem("norm2_rows_ready")
        s_tp3 = sem("norm2_rows_transposed")
        s_nt3 = sem("norm2_transposes_copied")
        s_pj = sem("projections")
        s_pje = sem("projections_copied")
        s_xf = sem("projected_rows_in_dram")
        s_w12 = sem("expert_weights_loaded")
        s_yzr = sem("expert_rows_zeroed")
        s_m = sem("assignment_ready")
        s_cnt = sem("counts_ready")
        s_oh = sem("slot_onehots_ready")
        s_ids = sem("slot_tokens")
        s_idx = sem("row_numbers_ready")
        s_te = sem("tile_experts_ready")
        s_g = [sem(f"rows_gathered{u}") for u in range(RING)]
        s_xp = sem("gathered_transposed")
        s_xt = sem("gathered_transpose_copied")
        s_h = sem("hidden_ready")
        s_nh = sem("hidden_normed")
        s_hp = sem("hidden_transposed")
        s_a = sem("gelu_ready")
        s_o = sem("expert_out")
        s_f = sem("expert_rows_ready")
        s_sc = [sem(f"rows_scattered{u}") for u in range(RING)]
        s_x1 = sem("x1_ready")
        s_x1b = sem("x1_shifted")
        s_yl = [sem(f"expert_rows_loaded{b}") for b in range(B)]
        s_fm = sem("final_product_ready")
        s_res = sem("result_ready")
        s_out = sem("result_stored")
        s_dve = sem("dve_steps")
        s_act = sem("act_steps")
        s_pool = sem("pool_steps")

        def bc(ap, shape):
            return ap.to_broadcast(shape)

        block = ctx.enter_context(nc.Block())

        @block.sync
        def _(sp):
            with nc.allow_non_contiguous_dma("small transposed vectors"):
                for dst, src in ((AL[:], A_log), (BP[:], B_param), (CP[:], C_param),
                                 (LD[:], log_dt.rearrange("(d a) -> d a", a=1))):
                    sp.dma_start(dst, src).then_inc(s_ssm, 16)
                sp.dma_start(cT[:], c.rearrange("b d -> d b")).then_inc(s_c, 16)
                sp.dma_start(wm, wmod.rearrange("k (m d) -> k m d", m=6)).then_inc(s_wm, 16)
                for b in range(B):
                    sp.dma_start(X[:, b], x[b].rearrange("(i p) d -> p i d", p=P)).then_inc(s_x, 16)
            sp.wait_ge(s_la, 1)
            sp.dma_start(la_rows, LA32[:, 0:NS]).then_inc(s_ld, 16)
            sp.wait_ge(s_ld, 16)
            sp.dma_start(Wst[:, 0:D * NS],
                         bass.AP(tensor=la_rows.tensor, offset=0, ap=[[0, P], [1, D * NS]])).then_inc(s_lb, 16)
            sp.wait_ge(s_kp, 1)
            sp.dma_start(k_pad, KP[:]).then_inc(s_kd, 16)
            sp.wait_ge(s_kd, 16)
            def toeplitz(k):
                for j in range(JQ):
                    src = bass.AP(tensor=k_pad.tensor, offset=(QD * j + 4 * k) * 2 * P,
                                  ap=[[1, P], [2 * P, 4], [1, P]])
                    sp.dma_start(T[:, k % TRING, :, j, :], src).then_inc(s_t[k], 16)

            for k in range(TRING):
                toeplitz(k)
            sp.wait_ge(s_sbz, 1)
            sp.dma_start(y_rows.rearrange("(p t) d -> p (t d)", p=P),
                         SBk[:].rearrange("p g j m -> p (g j m)")).then_inc(s_yzr, 16)
            for k in range(TRING, 8):
                sp.wait_ge(s_in, k - TRING + 1)
                toeplitz(k)
            sp.wait_ge(s_y, 8)
            sp.dma_start(W1s, W1.rearrange("e d h -> d e h")).then_inc(s_w12, 16)
            sp.dma_start(W2s, W2.rearrange("e (k q) d -> q e k d", q=P)).then_inc(s_w12, 16)
            sp.wait_ge(s_b3, 2)
            for q in range(3):
                sp.dma_start(BR1[q:q + 1].rearrange("p e h -> p (e h)"), b1p[:, q, :]).then_inc(s_br, 16)
                sp.dma_start(BR2[q:q + 1].rearrange("p e d -> p (e d)"), b2p[:, q, :]).then_inc(s_br, 16)
            for b in range(B):
                sp.wait_ge(s_pje, 2 * b + 2)
                sp.dma_start(xf_rows[b * L:(b + 1) * L].rearrange("(i p) d -> p i d", p=P),
                             XF[:, b * IC:(b + 1) * IC, :]).then_inc(s_xf, 16)
            for u in range(RING):
                sp.wait_ge(s_sc[u], 16 * (MAX_TILES // RING))
            for b in range(B):
                sp.dma_start(U[:, b * 2:(b + 1) * 2].rearrange("p a b d -> p (a b) d"),
                             y_rows[b * L:(b + 1) * L].rearrange("(i p) d -> p i d", p=P)).then_inc(s_yl[b], 16)
            for b in range(B):
                sp.wait_ge(s_res, b + 1)
                sp.dma_start(out[b].rearrange("(i p) d -> p i d", p=P), Hh[:, b]).then_inc(s_out, 16)
            sp.wait_ge(s_out, 16 * B)

        @block.gpsimd
        def _(pool):
            g = nc.gpsimd
            step = Steps(pool, s_pool)
            g.iota(iota_f[:], pattern=[[1, P]], base=0, channel_multiplier=0, allow_small_or_imprecise_dtypes=True)
            g.iota(iota_d[:], pattern=[[-1, P]], base=P - 1, channel_multiplier=0, allow_small_or_imprecise_dtypes=True)
            g.iota(iota_d1[:], pattern=[[-1, P]], base=P, channel_multiplier=0, allow_small_or_imprecise_dtypes=True)
            g.iota(left[:], pattern=[[0, 1]], base=P - 1, channel_multiplier=-1, allow_small_or_imprecise_dtypes=True)
            g.iota(part[:], pattern=[[0, 1]], base=0, channel_multiplier=1, allow_small_or_imprecise_dtypes=True)
            g.iota(erev[:], pattern=[[-1, E]], base=E, channel_multiplier=0, allow_small_or_imprecise_dtypes=True)
            g.iota(k128[:], pattern=[[P, IC]], base=0, channel_multiplier=0, allow_small_or_imprecise_dtypes=True)
            g.iota(giota[:], pattern=[[1, MAX_TILES]], base=0, channel_multiplier=0,
                   allow_small_or_imprecise_dtypes=True).then_inc(s_iota, 1)
            step.mark(g.memset(ident[:], 0.0))
            step.mark(g.memset(onesb[:], 1.0))
            g.memset(ones1[:], 1.0)
            g.memset(Wst[:, D * NS:], 0.0)
            g.memset(ones3[:], 1.0)
            g.memset(half[:], -0.5)
            g.memset(one8[:], 1.0)
            step.mark(g.memset(seg[:], 1.0))
            step.settle()
            g.memset(seg[:, :, 0:1], 0.0)
            g.affine_select(out=ident[:], in_=ident[:], pattern=[[-1, P]], compare_op=ALU.not_equal, fill=1.0,
                            base=0, channel_multiplier=1).then_inc(s_id, 1)
            g.affine_select(out=lower[:], in_=onesb[:], pattern=[[1, P]], compare_op=ALU.is_gt, fill=0.0,
                            base=0, channel_multiplier=-1).then_inc(s_one, 1)
            pool.wait_ge(s_kp, 1)
            g.memset(SBk[:].rearrange("p g j m -> p (g j m)"), 0.0).then_inc(s_sbz, 1)

            def rstd(n, w):
                pool.wait_ge(s_var, n + 1)
                g.tensor_tensor(rs[:, w, :], ve[:, w, :], half[:], ALU.pow).then_inc(s_rsd, 1)

            pool.wait_ge(s_la, 2)
            with nc.gpsimd.Fori(0, B) as b:
                rstd(2 * b, 0)
                rstd(2 * b + 1, 1)
                g.tensor_tensor(V[:, bass.ds(b * (QD // B), QD // B), :],
                                bc(iota_d1[:].unsqueeze(1), [P, QD // B, P]),
                                bc(LAT[:, bass.ds(b * (QD // B), QD // B)].unsqueeze(2), [P, QD // B, P]),
                                ALU.mult).then_inc(s_vl, 1)
            pool.wait_ge(s_gl, 1)
            for b in range(B):
                rstd(2 * B + b, 1)
                pool.wait_ge(s_x1, b + 1)
                g.tensor_tensor(Hh[:, b], X[:, b], bc(GLB[:, b:b + 1, :], [P, IC, D]), ALU.add).then_inc(s_x1b, 1)
            pool.wait_ge(s_idx, 1)
            pool.wait_ge(s_xf, 16 * B)
            pool.wait_ge(s_yzr, 16)

            def gather(t):
                u = t % RING
                if t >= RING:
                    pool.wait_ge(s_xp, t - RING + 1)
                pool.indirect_dma_start(out=XG[:, u, :], out_offset=None, in_=xf_rows,
                                        in_offset=bass.IndirectOffsetOnAxis(ap=idgi[:, t:t + 1], axis=0),
                                        bounds_check=N - 1, oob_is_err=False).then_inc(s_g[u], 16)

            def scatter(t):
                pool.wait_ge(s_f, t + 1)
                pool.indirect_dma_start(out=y_rows, out_offset=bass.IndirectOffsetOnAxis(ap=idsi[:, t:t + 1], axis=0),
                                        in_=FO[:, t % RING, :], in_offset=None,
                                        bounds_check=N - 1, oob_is_err=False).then_inc(s_sc[t % RING], 16)

            for t in range(AHEAD):
                gather(t)
            for t in range(MAX_TILES + RING + 1):
                if t < MAX_TILES + RING:
                    pool.wait_ge(s_var1, t + 1)
                    g.tensor_tensor(rs1[:, t % RING, :], ve1[:, t % RING, :], half[:, 0:2],
                                    ALU.pow).then_inc(s_rsd1, 1)
                if t + AHEAD < MAX_TILES:
                    gather(t + AHEAD)
                if t > RING:
                    scatter(t - RING - 1)

        @block.scalar
        def _(act):
            a = nc.scalar
            with nc.allow_non_contiguous_dma("weight vectors"):
                for dst, src in ((inw, in_w.rearrange("(a p) d -> p a d", p=P)), (outw, out_w),
                                 (wpr[:], W_proj), (wgt[:], W_gate),
                                 (bpc[:], b_proj.rearrange("(d a) -> d a", a=1)),
                                 (lngc[:], ln_g.rearrange("(d a) -> d a", a=1)),
                                 (lnbc[:], ln_b.rearrange("(d a) -> d a", a=1)),
                                 (row_in[:], in_b.rearrange("(a d) -> a d", a=1)),
                                 (row_out[:], out_b.rearrange("(a d) -> a d", a=1)),
                                 (row_pj[:, 0:D], b_proj.rearrange("(a d) -> a d", a=1))):
                    act.dma_start(dst, src).then_inc(s_w, 16)
                for dst, src in ((gb1[:, 0, :], ln1_g.rearrange("e (k p) -> (e k) p", p=P)),
                                 (gb1[:, 1, :], ln1_b.rearrange("e (k p) -> (e k) p", p=P)),
                                 (b1n[:], b1.rearrange("e (k p) -> (e k) p", p=P)), (b2n[:], b2)):
                    act.dma_start(dst, src).then_inc(s_e, 16)
                for m, src in enumerate((f_ln_g, f_ln_b)):
                    act.dma_start(lngb[:, m, :], bass.AP(tensor=src.tensor, offset=0, ap=[[0, P], [1, D]])
                                  ).then_inc(s_bc, 16)
            act.wait_ge(s_c, 16)
            a.activation(scT[:], cT[:], ACT.Silu).then_inc(s_silu, 1)
            act.wait_ge(s_ssm, 64)
            a.activation(EA[:], AL[:], ACT.Exp)
            a.activation(DT[:], LD[:], ACT.Exp).then_inc(s_ea, 1)
            act.wait_ge(s_ptr, 1)
            a.copy(inwT[:], PS[:, 0, 0:2 * D])
            a.copy(outwT[:], PS[:, 0, 2 * D:3 * D]).then_inc(s_uze, 1)
            a.copy(wprT, PS[:, 0, 3 * D:4 * D]).then_inc(s_etr, 1)
            act.wait_ge(s_kl, 1)
            a.activation(KN, KN, ACT.Exp).then_inc(s_ke, 1)
            act.wait_ge(s_ptr, 2)
            a.copy(gb1T[:].rearrange("p m e k -> p (m e k)"), PS[:, 1, 0:2 * QD]).then_inc(s_etr, 1)
            for b in range(B):
                act.wait_ge(s_mod, b + 1)
                for m, (blk_, one) in enumerate(((0, 0.0), (1, 1.0), (2, 0.0), (5, 0.0))):
                    src = PS[:, 2 + 2 * (b % 2) + blk_ // 4, blk_ % 4 * D:blk_ % 4 * D + D]
                    last = a.activation(MOD[:, b, m, :], src, ACT.Copy, bias=one)
                last.then_inc(s_me, 1)
            a.activation(AQ[:], LAT[:], ACT.Exp, scale=float(P)).then_inc(s_aq, 1)
            act.wait_ge(s_lb, 16)
            a.activation(Wst[:, 0:D * NS], Wst[:, 0:D * NS], ACT.Exp,
                         scale=left[:, 0:1]).then_inc(s_wst, 1)
            with nc.scalar.Fori(0, B) as b:
                for h in range(2):
                    act.wait_ge(s_tp, 2 * b + h + 2)
                    a.copy(NTt[:, 4 * h:4 * h + 4, :], PS[:, h, :]).then_inc(s_nt, 1)
                for h in range(2):
                    act.wait_ge(s_uz, 2 * b + h + 1)
                    src = PS[:, 2 + 2 * h:4 + 2 * h, :].rearrange("p k (a c) -> p (k a) c", a=2)
                    a.copy(U[:, 4 * h:4 * h + 4, bass.ds(b, 1), :].rearrange("p i a d -> p (i a) d"), src[:, :, 0:D])
                    a.activation(Z[:, 4 * h:4 * h + 4, bass.ds(b, 1), :].rearrange("p i a d -> p (i a) d"),
                                 src[:, :, D:2 * D], ACT.Silu).then_inc(s_uze, 1)
            act.wait_ge(s_vl, B)
            a.activation(V[:], V[:], ACT.Exp).then_inc(s_v, 1)
            act.wait_ge(s_st, 1)
            act.wait_ge(s_yzr, 16)
            for j in (2, 3):
                a.copy(SBk[QD * j:QD * j + QD, :, j, :].rearrange("p g (i b) -> p i g b", b=B),
                       St[QD * j:QD * j + QD]).then_inc(s_sbd, 1)
            for k in range(8):
                act.wait_ge(s_y, k + 1)
                if k >= 2:
                    act.wait_ge(s_yt, k - 1)
                dst = YS[:, k % 2, :, P - 1:P]
                dst = bass.AP(tensor=dst.tensor, offset=dst.offset, ap=[*dst.ap[:-1], [-1, P]])
                a.copy(dst, PS[:, k, :].rearrange("p (g q) -> p g q", g=4)).then_inc(s_ys, 1)

            def gated_out(b):
                for h in range(2):
                    act.wait_ge(s_tp2, 2 * b + h + 1)
                    a.copy(YT2[:, 4 * h:4 * h + 4, :], PS[:, h, :]).then_inc(s_nt2, 1)

            def project(b):
                for h in range(2):
                    act.wait_ge(s_tp3, 2 * b + h + 2)
                    a.copy(NTt[:, 4 * h:4 * h + 4, :], PS[:, 4 + h, :]).then_inc(s_nt3, 1)
                for h in range(2):
                    act.wait_ge(s_pj, 2 * b + h + 1)
                    src = PS[:, 6:8, :].rearrange("p k (a c) -> p (k a) c", a=2)
                    t0 = b * IC + 4 * h
                    a.copy(XF[:, bass.ds(t0, 4), :], src[:, :, 0:D])
                    a.copy(LG[:, bass.ds(t0, 4), :], src[:, :, D:PJ]).then_inc(s_pje, 1)

            gated_out(0)
            with nc.scalar.Fori(0, B - 1) as b:
                gated_out(b + 1)
                project(b)
            project(B - 1)

            def copy_xt(t, u, first):
                act.wait_ge(s_xp, t + 1)
                if not first:
                    act.wait_ge(s_h, t - RING + 1)
                a.copy(XT[:, u, :], PS[:, 4, 0:P]).then_inc(s_xt, 1)

            def gelu(t, u, first):
                e = act.value_load(texpi[0:1, bass.ds(t, 1)], min_val=0, max_val=E - 1)
                act.wait_ge(s_hp, t + 1)
                if not first:
                    act.wait_ge(s_o, t - RING + 1)
                for k in range(KC):
                    a.activation(AT[:, u, k, :], PS[:, 3, P * k:P * k + P], ACT.Gelu,
                                 bias=gb1T[:, 1, bass.ds(e, 1), k],
                                 scale=gb1T[:, 0, bass.ds(e, 1), k]).then_inc(s_a, 1)

            act.wait_ge(s_te, 1)
            for u in range(RING):
                copy_xt(u, u, True)
            for u in range(RING):
                copy_xt(RING + u, u, False)
                gelu(u, u, True)
            with nc.scalar.Fori(1, MAX_TILES // RING - 1) as i:
                for u in range(RING):
                    copy_xt(RING * i + u + RING, u, False)
                    gelu(RING * i + u, u, False)
            for t in range(MAX_TILES - RING, MAX_TILES):
                gelu(t, t % RING, False)

        @block.vector
        def _(dve):
            v = nc.vector
            step = Steps(dve, s_dve)
            v.memset(LA32[:], 0.0)
            v.memset(CB32[:], 0.0)
            step.mark(v.memset(KP[:, P:2 * P], 0.0))
            dve.wait_ge(s_ssm, 64)
            dve.wait_ge(s_ea, 1)
            step.mark(v.tensor_scalar(DT[:], DT[:], 1e-4, 1.0, ALU.max, ALU.min))
            step.settle()
            step.mark(v.tensor_scalar(EA[:], EA[:], DT[:, 0:1], -1.0, ALU.mult, ALU.mult))
            step.mark(v.tensor_scalar(CP[:], CP[:], DT[:, 0:1], None, ALU.mult))
            step.settle()
            v.tensor_scalar(LA32[:, 0:NS], EA[:], LOG_LO, 0.0, ALU.max, ALU.min).then_inc(s_la, 1)
            step.mark(v.tensor_tensor(CB32[:, 0:NS], CP[:], BP[:], ALU.mult))
            dve.wait_ge(s_la, 1)
            step.settle()
            step.mark(v.transpose(CBT[:], CB32[:]))
            v.transpose(LAT[:], LA32[:]).then_inc(s_la, 1)
            dve.wait_ge(s_iota, 1)
            v.tensor_tensor(KN, bc(iota_d[:].unsqueeze(1), [P, NS, P]), bc(LA32[:, 0:NS].unsqueeze(2), [P, NS, P]),
                            ALU.mult).then_inc(s_kl, 1)
            dve.wait_ge(s_ke, 1)
            step.mark(v.tensor_tensor(KN, KN, bc(CB32[:, 0:NS].unsqueeze(2), [P, NS, P]), ALU.mult))
            step.settle()
            v.tensor_reduce(KP[:, 0:P], KN.rearrange("p n l -> p l n"), AX.X, ALU.add).then_inc(s_kp, 1)
            dve.wait_ge(s_w, 160)
            dve.wait_ge(s_etr, 1)
            v.tensor_scalar(inwG[:], inwT[:], lngc[:, 0:1], None, ALU.mult).then_inc(s_inw, 1)
            dve.wait_ge(s_r1, 1)
            v.tensor_tensor(row_in[:], row_in[:], PS[0:1, 7, 0:2 * D], ALU.add).then_inc(s_r1e, 1)

            def norm_rows(src, w, dst_of, n):
                v.memset(tick[:], 0.0)
                for i in range(IC):
                    last = v.bn_stats(st[:, w, i, :], src(i))
                step.mark(last)
                step.settle()
                v.memset(tick[:], 0.0)
                for i in range(IC):
                    last = v.bn_aggr(mv[:, w, i, :], st[:, w, i, :])
                step.mark(last)
                step.settle()
                v.tensor_scalar(ve[:, w, :], mv[:, w, :, 1], LN_EPS, None, ALU.add).then_inc(s_var, 1)
                if w == 1:
                    dst_of(None)
                dve.wait_ge(s_rsd, n + 1)
                for i in range(IC):
                    last = v.tensor_scalar(dst_of(i), src(i), mv[:, w, i, 0:1], rs[:, w, i:i + 1],
                                           ALU.subtract, ALU.mult)
                return last

            dve.wait_ge(s_x, 16 * B)
            dve.wait_ge(s_wg, 1)
            dve.wait_ge(s_me, B)
            with nc.vector.Fori(0, B) as b:
                step.enter(b, 7)
                xb = X[:, bass.ds(b, 1)].rearrange("p a i d -> p (a i) d")
                hb = Hh[:, bass.ds(b, 1)].rearrange("p a i d -> p (a i) d")
                step.mark(norm_rows(lambda i: xb[:, i, :], 0, lambda i: hb[:, i, :], 2 * b))
                step.settle()
                ca1 = MOD[:, bass.ds(b, 1), 1, :]
                sa = MOD[:, bass.ds(b, 1), 0, :]
                step.mark(v.tensor_tensor(hb, hb, bc(ca1, [P, IC, D]), ALU.mult))
                step.settle()
                step.mark(v.tensor_tensor(hb, hb, bc(sa, [P, IC, D]), ALU.add))
                step.settle()

                def n_slot(i):
                    if i is None:
                        dve.wait_ge(s_tp, 2 * b + 1)
                        return None
                    return NR[:, i, :]
                norm_rows(lambda i: hb[:, i, :], 1, n_slot, 2 * b + 1).then_inc(s_n, 1)
                step.leave(B)
            dve.wait_ge(s_col, 1)
            step.mark(v.tensor_copy(cbsT[:, 0, :], PS[:, 6, 64:68]))
            step.mark(v.tensor_scalar(cbsT[:, 1, :], PS[:, 6, 68:72], 1.0, None, ALU.add))
            step.mark(v.tensor_copy(WPG[:, 0:D], wpr[:]))
            step.mark(v.tensor_copy(WPG[:, D:PJ], PS[:, 6, 72:80]))
            step.mark(v.tensor_copy(row_pj[:, D:PJ], PS[0:1, 6, 80:88]))
            step.settle()
            for b in range(B):
                last = v.tensor_scalar(WPB[:, b, :], WPG[:], cbsT[:, 1, b:b + 1], None, ALU.mult)
            last.then_inc(s_wge, 1)
            for m in (2, 3):
                step.mark(v.scalar_tensor_tensor(GT, MOD[:, :, m, :], -1.0, MOD[:, :, m, :], ALU.mult, ALU.max))
                step.mark(v.tensor_scalar(GT2, MOD[:, :, m, :], 0.0, 2.0, ALU.is_ge, ALU.mult))
                step.settle()
                step.mark(v.tensor_scalar(GT2, GT2, -1.0, None, ALU.add))
                step.mark(v.tensor_scalar(GT, GT, 0.25, None, ALU.max))
                step.settle()
                step.mark(v.tensor_tensor(MOD[:, :, m, :], GT, GT2, ALU.mult))
                step.settle()
            dve.wait_ge(s_bc, 32)
            v.tensor_tensor(GL[:], MOD[:, :, 3, :], bc(lngb[:, 0:1, :], [P, B, D]), ALU.mult)
            v.tensor_tensor(GLB[:], MOD[:, :, 3, :], bc(lngb[:, 1:2, :], [P, B, D]), ALU.mult).then_inc(s_gl, 1)
            dve.wait_ge(s_r2, 1)
            for b in range(B):
                last = v.tensor_tensor(row_pb[:, b, :], row_pj[:],
                                       PS[0:1, 2 + b // 2, b % 2 * 256:b % 2 * 256 + PJ], ALU.add)
            last.then_inc(s_r2e, 1)
            dve.wait_ge(s_e, 64)
            for nat, rest, parts in ((b1n, b1r, b1p), (b2n, b2r, b2p)):
                step.mark(v.tensor_copy(parts[:, 0, :], nat[:]))
                step.settle()
                step.mark(v.tensor_tensor(rest[:], nat[:], parts[:, 0, :], ALU.subtract))
                step.settle()
                step.mark(v.tensor_copy(parts[:, 1, :], rest[:]))
                step.settle()
                step.mark(v.tensor_tensor(rest[:], rest[:], parts[:, 1, :], ALU.subtract))
                step.settle()
                v.tensor_copy(parts[:, 2, :], rest[:]).then_inc(s_b3, 1)
            step.mark(v.memset(St[:, 0], 0.0))
            dve.wait_ge(s_aq, 1)
            dve.wait_ge(s_sin, 2)
            sin = PS[:, 6:8, :].rearrange("p k (g i b) -> p i (k g) b", i=IC, b=B)
            step.settle()
            step.mark(v.tensor_copy(St[:, 1], sin[:, 0]))
            step.settle()
            for i in range(1, IC - 1):
                step.mark(v.tensor_tensor(Stmp[:], St[:, i], bc(AQ[:].unsqueeze(2), [P, QD, B]), ALU.mult))
                step.settle()
                last = v.tensor_tensor(St[:, i + 1], Stmp[:], sin[:, i], ALU.add)
                if i < IC - 2:
                    step.mark(last)
                    step.settle()
            step.mark(last)
            step.settle()
            v.tensor_tensor(St[:].rearrange("p i g b -> p g i b"), St[:].rearrange("p i g b -> p g i b"),
                            bc(CBT[:].unsqueeze(2).unsqueeze(3), [P, QD, IC, B]), ALU.mult).then_inc(s_st, 1)
            dve.wait_ge(s_st, 1)
            dve.wait_ge(s_yzr, 16)
            for j in (0, 1):
                v.tensor_copy(SBk[QD * j:QD * j + QD, :, j, :].rearrange("p g (i b) -> p i g b", b=B),
                              St[QD * j:QD * j + QD]).then_inc(s_sbd, 1)
            for k in range(8):
                dve.wait_ge(s_yt, k + 1)
                zk = Z[:].rearrange("p i b (j g) -> p g j (i b)", g=QD)[:, 4 * k:4 * k + 4]
                src = PS[:, k, :].rearrange("p (g j m) -> p g j m", g=4, j=JQ)
                for g4 in range(4):
                    last = v.tensor_tensor(zk[:, g4], src[:, g4], zk[:, g4], ALU.mult)
                last.then_inc(s_yz, 1)

            def mixer_out(b):
                xb = X[:, bass.ds(b, 1)].rearrange("p a i d -> p (a i) d")
                hb = Hh[:, bass.ds(b, 1)].rearrange("p a i d -> p (a i) d")
                for h in range(2):
                    dve.wait_ge(s_op, 2 * b + h + 1)
                    step.mark(v.tensor_tensor(hb[:, 4 * h:4 * h + 4, :], PS[:, 2 + h, :].rearrange(
                        "p (i d) -> p i d", d=D), hb[:, 4 * h:4 * h + 4, :], ALU.add))
                step.settle()
                step.mark(v.tensor_scalar(hb, hb, 10.0, -10.0, ALU.min, ALU.max))
                step.settle()
                step.mark(v.tensor_tensor(hb, hb, bc(MOD[:, bass.ds(b, 1), 2, :], [P, IC, D]), ALU.mult))
                step.settle()
                ins = v.tensor_tensor(xb, xb, hb, ALU.add)
                ins.then_inc(s_x1, 1)
                dve.wait_ge(s_x1, b + 1)

                def n_slot(i):
                    if i is None:
                        dve.wait_ge(s_tp3, 2 * b + 1)
                        return None
                    return NR[:, i, :]
                norm_rows(lambda i: xb[:, i, :], 1, n_slot, 2 * B + b).then_inc(s_n2, 1)

            with nc.vector.Fori(0, B) as b:
                step.enter(b, 6)
                mixer_out(b)
                step.leave(B)

            dve.wait_ge(s_pje, 2 * B)
            step.mark(v.memset(texp[:], 0.0))
            step.mark(v.tensor_reduce(top[:], LG, AX.X, ALU.max))
            step.settle()
            step.mark(v.tensor_tensor(RA, LG, bc(top[:].unsqueeze(2), [P, NT, E]), ALU.is_equal))
            step.settle()
            step.mark(v.tensor_tensor(RA, RA, bc(erev[:].unsqueeze(1), [P, NT, E]), ALU.mult))
            step.settle()
            step.mark(v.tensor_reduce(top[:], RA, AX.X, ALU.max))
            step.settle()
            step.mark(v.tensor_tensor(Mf, bc(erev[:].unsqueeze(1), [P, NT, E]), bc(top[:].unsqueeze(2), [P, NT, E]),
                                      ALU.is_equal))
            step.settle()
            v.tensor_copy(Mb[:], Mf).then_inc(s_m, 1)
            dve.wait_ge(s_cnt, 1)
            rank = PS[:, 0, 0:NT * E].rearrange("p (t e) -> p e t", e=E)
            step.mark(v.tensor_copy(tot, PS[:, 1, 0:NT * E].rearrange("p (t e) -> p e t", e=E)))
            step.settle()
            flat = lambda ap: ap.rearrange("p e t -> p (e t)")
            step.mark(v.tensor_tensor_scan(flat(inc), flat(seg[:]), flat(tot), 0.0, ALU.mult, ALU.add))
            step.settle()
            step.mark(v.tensor_tensor(exc, inc, tot, ALU.subtract))
            step.mark(v.tensor_scalar(nte[:], inc[:, :, NT - 1], float(CAPACITY), None, ALU.min))
            step.settle()
            step.mark(v.tensor_tensor(cmpk, bc(nte[:].unsqueeze(2), [P, E, IC]), bc(k128[:].unsqueeze(1), [P, E, IC]),
                                      ALU.is_gt))
            step.mark(v.tensor_tensor(pos, exc, rank, ALU.add))
            step.settle()
            step.mark(v.tensor_reduce(nte[:], cmpk, AX.X, ALU.add))
            step.settle()
            step.mark(v.tensor_tensor_scan(tend[:], one8[:], nte[:], 0.0, ALU.mult, ALU.add))
            step.settle()
            step.mark(v.tensor_tensor(tbeg[:], tend[:], nte[:], ALU.subtract))
            step.mark(v.tensor_tensor(gcmp, bc(giota[:].unsqueeze(1), [P, E, MAX_TILES]),
                                      bc(tend[:].unsqueeze(2), [P, E, MAX_TILES]), ALU.is_ge))
            step.mark(v.tensor_scalar(sel, pos, float(CAPACITY), None, ALU.is_lt))
            step.settle()
            step.mark(v.tensor_scalar(tbeg[:], tbeg[:], float(P), None, ALU.mult))
            step.mark(v.tensor_reduce(texp[:, 1:1 + MAX_TILES], gcmp.rearrange("p e g -> p g e"), AX.X, ALU.add))
            me = Mf.rearrange("p t e -> p e t")
            step.mark(v.tensor_tensor(sel, sel, me, ALU.mult))
            step.settle()
            step.mark(v.tensor_tensor(pos, pos, bc(tbeg[:].unsqueeze(2), [P, E, NT]), ALU.add))
            step.mark(v.tensor_reduce(keep[:], sel.rearrange("p e t -> p t e"), AX.X, ALU.add))
            step.mark(v.tensor_scalar(texp[:], texp[:], float(E - 1), None, ALU.min))
            step.settle()
            rounds3 = texp[:].rearrange("p (i c) -> p i c", c=RING)
            v.tensor_copy(texpr[:, :, 0:RING], rounds3[:, 0:MAX_TILES // RING])
            v.tensor_copy(texpr[:, :, RING:2 * RING], rounds3[:, 1:])
            v.tensor_copy(texpi[:], texp[:, 1:1 + MAX_TILES]).then_inc(s_te, 1)
            step.mark(v.tensor_tensor(pos, pos, me, ALU.mult))
            step.settle()
            step.mark(v.tensor_reduce(slot[:], pos.rearrange("p e t -> p t e"), AX.X, ALU.add))
            step.mark(v.tensor_scalar(keep[:], keep[:], -float(2 * N), float(2 * N), ALU.mult, ALU.add))
            step.settle()
            step.mark(v.tensor_tensor(slot[:], slot[:], keep[:], ALU.add))
            step.settle()
            step.mark(v.tensor_copy(sloti[:], slot[:]))
            step.settle()
            step.mark(v.tensor_scalar(rowi[:], sloti[:], P - 1, None, ALU.bitwise_and))
            step.mark(v.tensor_scalar(tili[:], sloti[:], 7, None, ALU.arith_shift_right))
            step.settle()
            step.mark(v.tensor_copy(rowf[:], rowi[:]))
            step.mark(v.tensor_copy(tilf[:], tili[:]))
            step.settle()
            for t in range(NT):
                v.tensor_scalar(OR[:, t, :], iota_f[:], rowf[:, t:t + 1], None, ALU.is_equal)
            for t in range(NT):
                v.tensor_scalar(OT[:, t, 0, :], giota[:], tilf[:, t:t + 1], None, ALU.is_equal)
                v.tensor_scalar(OT[:, t, 1, :], giota[:], tilf[:, t:t + 1], float(t), ALU.is_equal, ALU.mult)
                last = v.tensor_scalar(OT[:, t, 2, :], giota[:], tilf[:, t:t + 1], part[:, 0:1],
                                       ALU.is_equal, ALU.mult)
            last.then_inc(s_oh, 1)
            dve.wait_ge(s_ids, 1)
            step.mark(v.tensor_copy(idf.rearrange("p c g -> p (c g)"), PS[:, 2, 0:3 * MAX_TILES]))
            step.settle()
            step.mark(v.tensor_scalar(idg, idf[:, 1, :], float(P), None, ALU.mult))
            step.mark(v.tensor_scalar(ids, idf[:, 0, :], -float(2 * N), float(2 * N), ALU.mult, ALU.add))
            step.settle()
            step.mark(v.tensor_tensor(idg, idg, idf[:, 2, :], ALU.add))
            step.settle()
            step.mark(v.tensor_tensor(ids, ids, idg, ALU.add))
            step.mark(v.tensor_copy(idgi[:], idg))
            step.settle()
            v.tensor_copy(idsi[:], ids).then_inc(s_idx, 1)

            def expert_step(t, u, rounds=None):
                static = isinstance(t, int)
                hidden, rows = not static or t < MAX_TILES, not static or RING <= t < MAX_TILES + RING
                stats = hidden or rows
                pairs = slice(0, 2) if hidden and rows else slice(0, 1) if hidden else slice(1, 2)
                if hidden:
                    dve.wait_ge(s_h, t + 1)
                    last = v.bn_stats(st1[:, u, 0, :], PS[:, u, :])
                if rows:
                    dve.wait_ge(s_o, t - RING + 1)
                    last = v.bn_stats(st1[:, u, 1, :], PS[:, 5 + u, 0:D])
                if stats:
                    step.mark(last)
                if not static or 1 <= t <= MAX_TILES:
                    dve.wait_ge(s_rsd1, t)
                    if not static or t > RING:
                        dve.wait_ge(s_hp, t - RING)
                    w = (u - 1) % RING
                    v.tensor_scalar(NH[:, w, :], PS[:, w, :], mv1[:, w, 0, 0:1], rs1[:, w, 0:1],
                                    ALU.subtract, ALU.mult).then_inc(s_nh, 1)
                if stats:
                    step.settle()
                    v.memset(tick[:], 0.0)
                    for q in (0, 1)[pairs]:
                        last = v.bn_aggr(mv1[:, u, q, :], st1[:, u, q, :])
                    step.mark(last)
                if not static or t > RING:
                    w = (u - 1) % RING
                    dve.wait_ge(s_rsd1, t)
                    if rounds is not None:
                        dve.wait_ge(s_sc[w], 16 * rounds)
                    v.tensor_scalar(FO[:, w, :], PS[:, 5 + w, 0:D], mv1[:, w, 1, 0:1], rs1[:, w, 1:2],
                                    ALU.subtract, ALU.mult).then_inc(s_f, 1)
                if stats:
                    step.settle()
                    v.tensor_scalar(ve1[:, u, pairs], mv1[:, u, pairs, 1], LN_EPS, None, ALU.add).then_inc(s_var1, 1)

            step.mark(v.memset(ve1[:], 1.0))
            step.settle()

            def rounds_at(t):
                done = (t - RING - 1) // RING
                return done if done > 0 else None

            for t in range(3 * RING):
                expert_step(t, t % RING, rounds_at(t))
            with nc.vector.Fori(3, MAX_TILES // RING) as i:
                step.enter(i - 3, 2 * RING)
                for u in range(RING):
                    expert_step(RING * i + u, u, i - 1 if u else i - 2)
                step.leave(MAX_TILES // RING - 3)
            for t in range(MAX_TILES, MAX_TILES + RING + 1):
                expert_step(t, t % RING, rounds_at(t))

            dve.wait_ge(s_x1b, B)
            for b in range(B):
                yb = U[:, b * 2:(b + 1) * 2].rearrange("p a b d -> p (a b) d")
                dve.wait_ge(s_yl[b], 16)
                step.mark(v.tensor_tensor(yb, yb, bc(GL[:, b:b + 1, :], [P, IC, D]), ALU.mult))
                step.settle()
                v.tensor_tensor(Hh[:, b], Hh[:, b], yb, ALU.add).then_inc(s_res, 1)

        @block.tensor
        def _(pe):
            m = nc.tensor
            pe.wait_ge(s_id, 1)
            pe.wait_ge(s_w, 160)
            m.transpose(PS[:, 0, 0:D], inw[:, 0, :], ident[:])
            m.transpose(PS[:, 0, D:2 * D], inw[:, 1, :], ident[:])
            m.transpose(PS[:, 0, 2 * D:3 * D], outw, ident[:]).then_inc(s_tp, 1)
            m.transpose(PS[:, 0, 3 * D:4 * D], wpr[:], ident[:]).then_inc(s_ptr, 1)
            pe.wait_ge(s_e, 64)
            m.transpose(PS[:, 1, 0:QD], gb1[:, 0, :], ident[0:QD, 0:QD])
            m.transpose(PS[:, 1, QD:2 * QD], gb1[:, 1, :], ident[0:QD, 0:QD]).then_inc(s_ptr, 1)
            pe.wait_ge(s_silu, 1)
            pe.wait_ge(s_wm, 16)
            wmf = wm.rearrange("p m d -> p (m d)")
            for b in range(B):
                if b >= 2:
                    pe.wait_ge(s_me, b - 1)
                k = 2 + 2 * (b % 2)
                m.matmul(PS[:, k, :], bc(scT[:, b:b + 1], [P, P]), wmf[:, 0:512], start=True, stop=True)
                m.matmul(PS[:, k + 1, 0:256], bc(scT[:, b:b + 1], [P, P]), wmf[:, 512:768],
                         start=True, stop=True).then_inc(s_mod, 1)
            m.matmul(PS[:, 6, 64:68], wm[:, 3, :], scT[:], start=True, stop=True).then_inc(s_tp3, 1)
            m.matmul(PS[:, 6, 68:72], wm[:, 4, :], scT[:], start=True, stop=True).then_inc(s_col, 1)
            pe.wait_ge(s_etr, 1)
            m.matmul(PS[0:1, 7, 0:2 * D], lnbc[:], inwT[:], start=True, stop=True).then_inc(s_r1, 1)
            m.matmul(PS[:, 6, 72:80], wprT, wgt[:], start=True, stop=True)
            m.matmul(PS[0:1, 6, 80:88], bpc[:], wgt[:], start=True, stop=True).then_inc(s_wg, 1)
            pe.wait_ge(s_inw, 1)
            pe.wait_ge(s_r1e, 1)
            pe.wait_ge(s_one, 1)
            pe.wait_ge(s_me, B)
            with nc.tensor.Fori(0, B) as b:
                pe.wait_ge(s_n, b + 1)
                for h in range(2):
                    for i in range(4):
                        last = m.transpose(PS[:, h, P * i:P * i + P], NR[:, 4 * h + i, :], ident[:])
                    last.then_inc(s_tp, 1)
                for h in range(2):
                    pe.wait_ge(s_nt, 2 * b + h + 1)
                    pe.wait_ge(s_uze, 2 * b + 1)
                    for i in range(4):
                        dst = PS[:, 2 + 2 * h + i // 2, i % 2 * 256:i % 2 * 256 + 256]
                        m.matmul(dst, NTt[:, 4 * h + i, :], inwG[:], start=True, stop=False)
                        last = m.matmul(dst, ones1[:], row_in[:], start=False, stop=True)
                    last.then_inc(s_uz, 1)
            pe.wait_ge(s_uze, 2 * B + 1)
            pe.wait_ge(s_wst, 1)
            pe.wait_ge(s_wge, 1)
            Um = U[:].rearrange("p i b d -> p (i b) d")
            for g in range(QD):
                for j in range(JQ):
                    d = QD * j + g
                    last = m.matmul(PS[QD * j:QD * j + QD, 6 + g // 16, g % 16 * QD:g % 16 * QD + QD],
                                    Wst[:, d * NS:d * NS + QD], Um[:, :, d], start=True, stop=True,
                                    skip_group_check=True)
                if g % 16 == 15:
                    last.then_inc(s_sin, 1)
            for b in range(B):
                last = m.matmul(PS[0:1, 2 + b // 2, b % 2 * 256:b % 2 * 256 + PJ], cbsT[:, 0, b:b + 1], WPG[:],
                                start=True, stop=True)
            last.then_inc(s_r2, 1)
            pe.wait_ge(s_r2e, 1)

            def inside(k):
                pe.wait_ge(s_t[k], 16 * JQ)
                for g in range(4 * k, 4 * k + 4):
                    for j in range(JQ):
                        last = m.matmul(PS[QD * j:QD * j + QD, k, g % 4 * P:g % 4 * P + P], Um[:, :, QD * j + g],
                                 T[:, k % TRING, g % 4, j, :], start=(g % 4 == 0), stop=False, skip_group_check=True)

                last.then_inc(s_in, 1)

            def between(k):
                for g in range(4 * k, 4 * k + 4):
                    last = m.matmul(PS[:, k, g % 4 * P:g % 4 * P + P], SBk[:, g].rearrange("p j m -> p (j m)"),
                                    V[:, g, :], start=False, stop=True, skip_group_check=True)
                last.then_inc(s_y, 1)

            def back(k):
                pe.wait_ge(s_ys, k + 1)
                for g in range(4):
                    last = m.transpose(PS[:, k, P * g:P * g + P], YS[:, k % 2, g, :], ident[:])
                last.then_inc(s_yt, 1)

            for k in range(6):
                inside(k)
            pe.wait_ge(s_sbd, JQ)
            pe.wait_ge(s_v, 1)
            for k in range(8):
                if k >= 6:
                    inside(k)
                between(k)
                if k:
                    back(k - 1)
            back(7)

            def gated_out(b):
                if b == 0:
                    pe.wait_ge(s_yz, 8)
                for h in range(2):
                    for i in range(4):
                        last = m.transpose(PS[:, h, P * i:P * i + P], Z[:, 4 * h + i, b, :], ident[:])
                    last.then_inc(s_tp2, 1)
                for h in range(2):
                    pe.wait_ge(s_nt2, 2 * b + h + 1)
                    if b:
                        pe.wait_ge(s_x1, b)
                    for i in range(4):
                        dst = PS[:, 2 + h, P * i:P * i + P]
                        m.matmul(dst, YT2[:, 4 * h + i, :], outwT[:], start=True, stop=False)
                        last = m.matmul(dst, ones1[:], row_out[:], start=False, stop=True)
                    last.then_inc(s_op, 1)

            def project(b):
                pe.wait_ge(s_n2, b + 1)
                for h in range(2):
                    for i in range(4):
                        last = m.transpose(PS[:, 4 + h, P * i:P * i + P], NR[:, 4 * h + i, :], ident[:])
                    last.then_inc(s_tp3, 1)
                wb, rb = WPB[:, b, :], row_pb[:, b, :]
                for h in range(2):
                    pe.wait_ge(s_nt3, 2 * b + h + 1)
                    if 2 * b + h:
                        pe.wait_ge(s_pje, 2 * b + h)
                    for i in range(4):
                        dst = PS[:, 6 + i // 2, i % 2 * 256:i % 2 * 256 + PJ]
                        m.matmul(dst, NTt[:, 4 * h + i, :], wb, start=True, stop=False)
                        last = m.matmul(dst, ones1[:], rb, start=False, stop=True)
                    last.then_inc(s_pj, 1)

            for b in range(B + 1):
                if b < B:
                    gated_out(b)
                if b >= 1:
                    project(b - 1)

            pe.wait_ge(s_m, 1)
            mb = Mb[:].rearrange("p t e -> p (t e)")
            m.matmul(PS[:, 0, 0:NT * E], lower[:], mb, start=True, stop=True)
            m.matmul(PS[:, 1, 0:NT * E], onesb[:], mb, start=True, stop=True).then_inc(s_cnt, 1)
            pe.wait_ge(s_oh, 1)
            for t in range(NT):
                last = m.matmul(PS[:, 2, 0:3 * MAX_TILES], OR[:, t, :], OT[:, t].rearrange("p c g -> p (c g)"),
                                start=(t == 0), stop=(t == NT - 1))
            last.then_inc(s_ids, 1)

            def rows_in(t, u, rounds):
                pe.wait_ge(s_g[u], 16 * rounds)
                m.transpose(PS[:, 4, 0:P], XG[:, u, :], ident[:]).then_inc(s_xp, 1)

            def experts(i, name):
                regs = [pe.alloc_register(f"experts_{name}{q}") for q in range(2 * RING)]
                pe.load(regs, texpr[0:1, bass.ds(i, 1), 0:2 * RING].rearrange("p a c -> p (a c)"))
                return [pe.snap(r, donate=True, min_val=0, max_val=E - 1) for r in regs]

            def up(t, u, e):
                pe.wait_ge(s_xt, t + 1)
                m.matmul(PS[:, u, :], XT[:, u, :], W1s[:, bass.ds(e, 1), :].rearrange("p a h -> p (a h)"),
                         start=True, stop=False)
                m.matmul(PS[:, u, :], ones3[:], BR1[:, bass.ds(e, 1), :].rearrange("p a h -> p (a h)"),
                         start=False, stop=True).then_inc(s_h, 1)

            def turn(t, u):
                pe.wait_ge(s_nh, t + 1)
                for k in range(KC):
                    last = m.transpose(PS[:, 3, P * k:P * k + P], NH[:, u, P * k:P * k + P], ident[:])
                last.then_inc(s_hp, 1)

            def down(t, u, e, first):
                dst = PS[:, 5 + u, 0:D]
                if not first:
                    pe.wait_ge(s_f, t - RING + 1)
                for k in range(KC):
                    pe.wait_ge(s_a, KC * t + k + 1)
                    m.matmul(dst, AT[:, u, k, :], W2s[:, bass.ds(e, 1), k, :].rearrange("p a d -> p (a d)"),
                             start=(k == 0), stop=False)
                m.matmul(dst, ones3[:], BR2[:, bass.ds(e, 1), :].rearrange("p a d -> p (a d)"),
                         start=False, stop=True).then_inc(s_o, 1)

            def tile_step(t, u, i, e):
                static = isinstance(i, int)
                if not static or t + 2 < MAX_TILES:
                    up(t + 2, (u + 2) % RING, e[u + RING])
                if not static or t + RING < MAX_TILES:
                    rows_in(t + RING, u, i + 2)
                if not static or t >= 1:
                    down(t - 1, (u - 1) % RING, e[u], static and t - 1 < RING)
                turn(t, u)

            pe.wait_ge(s_te, 1)
            pe.wait_ge(s_w12, 32)
            pe.wait_ge(s_br, 96)
            pe.wait_ge(s_idx, 1)
            e = experts(0, "start")
            rows_in(0, 0, 1)
            for t in range(2):
                pe.wait_ge(s_xt, t + 1)
                rows_in(t + 1, t + 1, 1)
                up(t, t, e[t + 1])
            for i in range(2):
                if i:
                    e = experts(i, "second")
                for u in range(RING):
                    tile_step(RING * i + u, u, i, e)
            with nc.tensor.Fori(2, MAX_TILES // RING - 1) as i:
                e = experts(i, "loop")
                for u in range(RING):
                    tile_step(RING * i + u, u, i, e)
            i = MAX_TILES // RING - 1
            e = experts(i, "end")
            for u in range(RING):
                tile_step(RING * i + u, u, i, e)
            e_last = pe.value_load(texpi[0:1, MAX_TILES - 1:MAX_TILES], min_val=0, max_val=E - 1)
            down(MAX_TILES - 1, RING - 1, e_last, False)


_INS = ['L0_attn_x', 'L0_attn_A_log', 'L0_attn_B_param', 'L0_attn_C_param', 'L0_attn_log_dt', 'L0_attn_in_w',
        'L0_attn_in_b', 'L0_attn_out_w', 'L0_attn_out_b', 'L0_attn_ln_g', 'L0_attn_ln_b', 'L0_ffn_W_proj',
        'L0_ffn_b_proj', 'L0_ffn_W_gate', 'L0_ffn_W1', 'L0_ffn_b1', 'L0_ffn_ln1_g', 'L0_ffn_ln1_b', 'L0_ffn_W2',
        'L0_ffn_b2', 'L0_ffn_ln_g', 'L0_ffn_ln_b', 'L0_c', 'L0_wmod']
_OUTS = [((4, 1024, 128), 'float32')]


def kernel(**inputs):
    import numpy as _np
    import concourse.bacc as _bacc
    from concourse import mybir as _mybir
    from concourse.bass_utils import run_bass_kernel_spmd as _run

    nc = _bacc.Bacc("TRN2", target_bir_lowering=False, num_devices=1)
    arrays, args = {}, []
    for name in _INS:
        a = _np.ascontiguousarray(inputs[name])
        arrays[f"in_{name}_dram"] = a
        args.append(nc.dram_tensor(f"in_{name}_dram", a.shape, _mybir.dt.from_np(a.dtype), kind="ExternalInput").ap())
    for i, (shape, dtype) in enumerate(_OUTS):
        dt = _mybir.dt.from_np(_np.dtype(dtype))
        args.append(nc.dram_tensor(f"out_{i}_dram", shape, dt, kind="ExternalOutput").ap())
    adaln_program(nc, *args)
    r = _run(nc, [arrays], core_ids=[0])
    got = tuple(r.results[0][f"out_{i}_dram"] for i in range(len(_OUTS)))
    return got[0]
```

```python
import concourse.bass as bass
from concourse import mybir
from contextlib import ExitStack

FP32 = mybir.dt.float32
BF16 = mybir.dt.bfloat16
I32 = mybir.dt.int32
ALU = mybir.AluOpType
ACT = mybir.ActivationFunctionType
AX = mybir.AxisListType

P = 128
B, L, D = 4, 1024, 128
NS = 16
IC = L // P
NT = B * IC
HT = IC // 2
N = B * L
E, H = 8, 512
KC = H // P
CAPACITY = int(2.0 * N / E)
MAX_TILES = N // P + E - 1
QD = 32
JQ = P // QD
LN_EPS = 1e-5
LOG_LO = -18.420680743952367
PJ = D + E
POOL_UNITS = (1, 4)
RING = 3
AHEAD = 5
TRING = 6


class Steps:

    def __init__(self, eng, sem):
        self.eng, self.sem, self.base, self.n = eng, sem, 0, 0

    def mark(self, ins):
        ins.then_inc(self.sem, 1)
        self.n += 1
        return self.now()

    def now(self):
        return self.base + self.n

    def settle(self, upto=None):
        self.eng.wait_ge(self.sem, self.now() if upto is None else upto)

    def enter(self, i, per):
        self.start, self.per = self.base + self.n, per
        self.base, self.n = self.start + i * per, 0

    def leave(self, rounds):
        assert self.n == self.per, (self.n, self.per)
        self.base, self.n = self.start + rounds * self.per, 0


def adaln_program(nc, x, A_log, B_param, C_param, log_dt, in_w, in_b, out_w, out_b, ln_g, ln_b,
                  W_proj, b_proj, W_gate, W1, b1, ln1_g, ln1_b, W2, b2, f_ln_g, f_ln_b, c, wmod, out):
    k_pad = nc.dram_tensor("k_pad", [D, 2 * P], FP32, kind="Internal").ap()
    la_rows = nc.dram_tensor("la_rows", [D, NS], FP32, kind="Internal").ap()
    xf_rows = nc.dram_tensor("xf_rows", [N, D], FP32, kind="Internal").ap()
    y_rows = nc.dram_tensor("y_rows", [N, D], FP32, kind="Internal").ap()

    ctx = ExitStack()
    with ctx:
        def sb(name, shape, dt=FP32):
            return ctx.enter_context(nc.sbuf_tensor(name, shape, dt))

        def sem(name):
            return ctx.enter_context(nc.semaphore(name))

        X = sb("X", [P, B, IC, D])
        Hh = sb("Hh", [P, B, IC, D])
        U = sb("U", [P, IC, B, D])
        Z = sb("Z", [P, IC, B, D])
        BIG = sb("BIG", [P, TRING * 4 * JQ * P])
        T = BIG[:, :].rearrange("p (s g j r) -> p s g j r", s=TRING, g=4, j=JQ)
        W1s = BIG[:, 0:E * H].rearrange("p (e h) -> p e h", e=E)
        W2s = BIG[:, E * H:2 * E * H].rearrange("p (e k d) -> p e k d", e=E, k=KC)
        SBk = sb("SBk", [P, QD, JQ, IC * B])
        V = sb("V", [P, QD, P])
        Wst = sb("Wst", [P, (D + 1) * NS])
        XF = U[:, :, :, :].rearrange("p a b d -> p (a b) d")
        KN = SBk[:, 0:NS].rearrange("p g j m -> p g (j m)")
        NR = sb("NR", [P, IC, D])
        NTt = sb("NTt", [P, IC, P])
        YT2 = V[:, 0:IC, :]
        YS = sb("YS", [P, 2, 4, P])
        St = sb("St", [P, IC, QD, B])
        Stmp = sb("Stmp", [P, QD, B])
        MOD = sb("MOD", [P, B, 4, D])
        GT = YS[:, 0]
        GT2 = YS[:, 1]
        GL = sb("GL", [P, B, D])
        GLB = sb("GLB", [P, B, D])
        lngb = sb("lngb", [P, 2, D])
        scT = sb("scT", [P, B])
        cT = sb("cT", [P, B])
        wm = St[:].rearrange("p i g b -> p (i g b)")[:, 0:6 * D].rearrange("p (m d) -> p m d", m=6)
        cbsT = sb("cbsT", [P, 2, B])
        AL = sb("AL", [P, NS])
        BP = sb("BP", [P, NS])
        CP = sb("CP", [P, NS])
        LD = sb("LD", [P, 1])
        EA = sb("EA", [P, NS])
        DT = sb("DT", [P, 1])
        LA32 = sb("LA32", [P, QD])
        CB32 = sb("CB32", [P, QD])
        LAT = sb("LAT", [P, QD])
        CBT = sb("CBT", [P, QD])
        AQ = sb("AQ", [P, QD])
        KP = sb("KP", [P, 2 * P])
        iota_d = sb("iota_d", [P, P])
        iota_d1 = sb("iota_d1", [P, P])
        left = sb("left", [P, 1])
        part = sb("part", [P, 1])
        ident = sb("ident", [P, P])
        lower = sb("lower", [P, P], BF16)
        onesb = sb("onesb", [P, P], BF16)
        ones3 = sb("ones3", [3, P], BF16)
        inw = NR[:, 1:3, :]
        outw = NR[:, 3, :]
        wpr = sb("wpr", [P, D])
        wgt = sb("wgt", [P, E])
        bpc = sb("bpc", [P, 1])
        lngc = sb("lngc", [P, 1])
        lnbc = sb("lnbc", [P, 1])
        inwT = sb("inwT", [P, 2 * D])
        inwG = sb("inwG", [P, 2 * D])
        outwT = sb("outwT", [P, D])
        wprT = NR[:, 0, :]
        WPG = sb("WPG", [P, PJ])
        WPB = sb("WPB", [P, B, PJ])
        row_in = sb("row_in", [3, 2 * D])
        row_out = sb("row_out", [3, D])
        row_pj = sb("row_pj", [3, PJ])
        row_pb = sb("row_pb", [3, B * PJ])
        part_in = sb("part_in", [3, 2 * D], BF16)
        part_out = sb("part_out", [3, D], BF16)
        part_pb = sb("part_pb", [3, B * PJ], BF16)
        below = sb("below", [3, 2])
        gb1 = sb("gb1", [QD, 2, P])
        gb1T = sb("gb1T", [P, 2, E, KC])
        b1n = sb("b1n", [QD, P])
        b1r = sb("b1r", [QD, P])
        b1p = sb("b1p", [QD, 3, P], BF16)
        b2n = sb("b2n", [E, P])
        b2r = sb("b2r", [E, P])
        b2p = sb("b2p", [E, 3, P], BF16)
        BR = BIG[0:3, 2 * E * H:2 * E * H + (E * H + E * D) // 2].bitcast(BF16)
        BR1 = BR[:, 0:E * H].rearrange("p (e h) -> p e h", e=E)
        BR2 = BR[:, E * H:E * (H + D)].rearrange("p (e d) -> p e d", e=E)
        st = sb("st", [P, 2, 2, HT, 6])
        mv = sb("mv", [P, 2, 2, HT, 2])
        ve = sb("ve", [P, 2, 2, HT])
        rs = sb("rs", [P, 2, 2, HT])
        nb = sb("nb", [P, 2, HT])
        tick = sb("tick", [P, 8])
        half = sb("half", [P, IC])
        flat_w = Wst[:, 0:D * NS]
        LG = flat_w[:, 0:NT * E].rearrange("p (t e) -> p t e", e=E)
        top = sb("top", [P, NT])
        RA, Mf = (NTt[:, 2 * i:2 * i + 2, :].rearrange("p a (t e) -> p (a t) e", e=E) for i in range(2))
        tot, inc, exc, pos = (NR[:, 2 * i:2 * i + 2, :].rearrange("p a (e t) -> p (a e) t", t=NT) for i in range(4))
        sel = NTt[:, 4:6, :].rearrange("p a (e t) -> p (a e) t", t=NT)
        Mb = sb("Mb", [P, NT, E], BF16)
        erev = sb("erev", [P, E])
        k128 = sb("k128", [P, IC])
        seg = sb("seg", [P, E, NT])
        cmpk = flat_w[:, 1024:1024 + E * IC].rearrange("p (e i) -> p e i", e=E)
        nte = sb("nte", [P, E])
        tend = sb("tend", [P, E])
        tbeg = sb("tbeg", [P, E])
        one8 = sb("one8", [P, E])
        slot = sb("slot", [P, NT])
        keep = sb("keep", [P, NT])
        sloti = sb("sloti", [P, NT], I32)
        rowi = sb("rowi", [P, NT], I32)
        tili = sb("tili", [P, NT], I32)
        rowb = sb("rowb", [P, NT], BF16)
        tilb = sb("tilb", [P, NT], BF16)
        iota_b = sb("iota_b", [P, P], BF16)
        giota_b = sb("giota_b", [P, MAX_TILES], BF16)
        tiota_b = sb("tiota_b", [P, NT], BF16)
        giota = sb("giota", [P, MAX_TILES])
        flat_s = SBk[:].rearrange("p g j m -> p (g j m)")
        OR = flat_s[:, 0:NT * P // 2].bitcast(BF16).rearrange("p (t r) -> p t r", t=NT)
        OT = flat_s[:, NT * P // 2:NT * P // 2 + NT * 3 * MAX_TILES // 2].bitcast(BF16).rearrange(
            "p (t c g) -> p t c g", t=NT, c=3)
        gcmp = V[:, 16:19].rearrange("p g r -> p (g r)")[:, 0:E * MAX_TILES].rearrange("p (e g) -> p e g", e=E)
        texp = sb("texp", [P, MAX_TILES + RING])
        texpi = sb("texpi", [P, MAX_TILES], I32)
        texpr = sb("texpr", [P, MAX_TILES // RING, 8], I32)
        idf = flat_w[:, 640:640 + 3 * MAX_TILES].rearrange("p (c g) -> p c g", c=3)
        idg = flat_w[:, 768:768 + MAX_TILES]
        ids = flat_w[:, 896:896 + MAX_TILES]
        idgi = sb("idgi", [P, MAX_TILES], I32)
        idsi = sb("idsi", [P, MAX_TILES], I32)
        flat_v = V[:].rearrange("p g r -> p (g r)")
        NH = flat_v[:, 0:RING * H].rearrange("p (u h) -> p u h", u=RING)
        AT = flat_v[:, RING * H:2 * RING * H].rearrange("p (u k q) -> p u k q", u=RING, k=KC)
        XG = flat_v[:, 2 * RING * H:2 * RING * H + RING * D].rearrange("p (u d) -> p u d", u=RING)
        XT = flat_v[:, 2 * RING * H + RING * D:2 * RING * (H + D)].rearrange("p (u d) -> p u d", u=RING)
        FO = flat_w[:, NT * E:NT * E + RING * D].rearrange("p (u d) -> p u d", u=RING)
        st1 = sb("st1", [P, RING, 2, 6])
        mv1 = sb("mv1", [P, RING, 2, 2])
        rs1 = sb("rs1", [P, RING, 2])
        ve1 = sb("ve1", [P, RING, 2])

        PS = ctx.enter_context(nc.psum_tensor("PS", [P, 8, 512], FP32))

        s_x = sem("x_loaded")
        s_ssm = sem("ssm_params_loaded")
        s_c = sem("c_loaded")
        s_wm = sem("wmod_loaded")
        s_w0 = sem("in_weights_loaded")
        s_w = sem("mixer_weights_loaded")
        s_e = sem("expert_vectors_loaded")
        s_bc = sem("final_norm_rows_loaded")
        s_iota = sem("iotas_ready")
        s_id = sem("identity_ready")
        s_one = sem("ones_ready")
        s_silu = sem("silu_c_ready")
        s_ea = sem("decay_exps_ready")
        s_la = sem("log_decay_ready")
        s_kl = sem("kernel_exponents_ready")
        s_ke = sem("kernel_exps_ready")
        s_kp = sem("kernel_ready")
        s_kd = sem("kernel_in_dram")
        s_ld = sem("log_decay_in_dram")
        s_lb = sem("log_decay_broadcast")
        s_wst = sem("state_input_weights_ready")
        s_vl = sem("state_output_exponents_ready")
        s_v = sem("state_output_weights_ready")
        s_aq = sem("chunk_decay_ready")
        s_sbz = sem("block_states_zeroed")
        s_t = [sem(f"toeplitz_loaded{k}") for k in range(8)]
        s_ptr = sem("setup_transposed")
        s_etr = sem("setup_transposes_copied")
        s_mod = sem("modulation_products")
        s_me = sem("modulation_copied")
        s_inw = sem("in_weights_ready")
        s_r1 = sem("in_bias_product")
        s_r1e = sem("in_bias_ready")
        s_wge = sem("router_weight_copied")
        s_r2 = sem("projection_bias_products")
        s_r2e = sem("projection_weights_ready")
        s_gl = sem("final_gates_ready")
        s_b3 = sem("bias_parts_ready")
        s_br = sem("bias_parts_in_rows")
        s_x0 = sem("first_batch_row_loaded")
        s_vx = sem("input_variances_ready")
        s_rx = sem("input_rstds_ready")
        s_vh = sem("modulated_variances_ready")
        s_rh = sem("modulated_rstds_ready")
        s_nb = sem("norm_shifts_ready")
        s_var1 = sem("hidden_variance_ready")
        s_rsd1 = sem("hidden_rstd_ready")
        s_n = sem("norm_rows_ready")
        s_tp = sem("rows_transposed")
        s_nt = sem("transposes_copied")
        s_uz = sem("in_products")
        s_uze = sem("in_products_used")
        s_sin = sem("chunk_inputs")
        s_st = sem("chunk_states_ready")
        s_sbd = [sem(f"block_states_ready{c2}") for c2 in range(2)]
        s_in = sem("conv_inside_done")
        s_y = sem("conv_bank_done")
        s_ys = sem("conv_bank_copied")
        s_yt = sem("conv_bank_transposed")
        s_yz = sem("gated_bank_ready")
        s_tp2 = sem("gated_rows_transposed")
        s_nt2 = sem("gated_transposes_copied")
        s_op = sem("out_products")
        s_tp3 = sem("norm2_rows_transposed")
        s_nt3 = sem("norm2_transposes_copied")
        s_pj = sem("projections")
        s_pje = sem("projections_copied")
        s_xf = sem("projected_rows_in_dram")
        s_w12 = sem("expert_weights_loaded")
        s_yzr = sem("expert_rows_zeroed")
        s_m = sem("assignment_ready")
        s_cnt = sem("counts_ready")
        s_ot = sem("tile_onehots_ready")
        s_otp = sem("tile_onehots_by_row")
        s_oh = sem("slot_onehots_ready")
        s_ids = sem("slot_tokens")
        s_idx = sem("row_numbers_ready")
        s_te = sem("tile_experts_ready")
        s_g = [sem(f"rows_gathered{u}") for u in range(RING)]
        s_xp = sem("gathered_transposed")
        s_xt = sem("gathered_transpose_copied")
        s_h = sem("hidden_ready")
        s_nh = sem("hidden_normed")
        s_hp = sem("hidden_transposed")
        s_a = sem("gelu_ready")
        s_o = sem("expert_out")
        s_f = sem("expert_rows_ready")
        s_sc = [sem(f"rows_scattered{u}") for u in range(RING)]
        s_x1 = sem("x1_ready")
        s_x1b = sem("x1_shifted")
        s_yl = [sem(f"expert_rows_loaded{q}") for q in range(2 * B)]
        s_fm = sem("pool_final_product")
        s_res = [sem(f"result_ready{q}") for q in range(2 * B)]
        s_out = sem("result_stored")
        s_dve = sem("dve_steps")
        s_pool = sem("pool_steps")

        def pb_product(b):
            return PS[0:3, 0, 0:PJ] if b == B - 1 else PS[0:3, 1, 64 + b * PJ:64 + b * PJ + PJ]

        def final_rows(q):
            return U[:, q]

        def bc(ap, shape):
            return ap.to_broadcast(shape)

        block = ctx.enter_context(nc.Block())

        @block.sync
        def _(sp):
            with nc.allow_non_contiguous_dma("small vectors"):
                for dst, src in ((AL[:], A_log), (LD[:], log_dt.rearrange("(d a) -> d a", a=1)),
                                 (BP[:], B_param), (CP[:], C_param)):
                    sp.dma_start(dst, src).then_inc(s_ssm, 16)
                for b in range(B):
                    sp.dma_start(X[:, b], x[b].rearrange("(i p) d -> p i d", p=P)).then_inc(s_x if b else s_x0, 16)
                for dst, src in ((outw, out_w), (wpr[:], W_proj), (wgt[:], W_gate),
                                 (bpc[:], b_proj.rearrange("(d a) -> d a", a=1)),
                                 (lngc[:], ln_g.rearrange("(d a) -> d a", a=1)),
                                 (lnbc[:], ln_b.rearrange("(d a) -> d a", a=1)),
                                 (row_in[:], bass.AP(tensor=in_b.tensor, offset=0, ap=[[0, 3], [1, 2 * D]])),
                                 (row_out[:], bass.AP(tensor=out_b.tensor, offset=0, ap=[[0, 3], [1, D]])),
                                 (row_pj[:, 0:D], bass.AP(tensor=b_proj.tensor, offset=0, ap=[[0, 3], [1, D]]))):
                    sp.dma_start(dst, src).then_inc(s_w, 16)
            sp.wait_ge(s_la, 1)
            sp.dma_start(la_rows, LA32[:, 0:NS]).then_inc(s_ld, 16)
            sp.wait_ge(s_ld, 16)
            sp.dma_start(Wst[:, 0:D * NS],
                         bass.AP(tensor=la_rows.tensor, offset=0, ap=[[0, P], [1, D * NS]])).then_inc(s_lb, 16)
            sp.wait_ge(s_kp, 1)
            sp.dma_start(k_pad, KP[:]).then_inc(s_kd, 16)
            for dst, src in ((gb1[:, 0, :], ln1_g.rearrange("e (k p) -> (e k) p", p=P)),
                             (gb1[:, 1, :], ln1_b.rearrange("e (k p) -> (e k) p", p=P)),
                             (b1n[:], b1.rearrange("e (k p) -> (e k) p", p=P)), (b2n[:], b2)):
                sp.dma_start(dst, src).then_inc(s_e, 16)
            for m, src in enumerate((f_ln_g, f_ln_b)):
                sp.dma_start(lngb[:, m, :], bass.AP(tensor=src.tensor, offset=0, ap=[[0, P], [1, D]])
                             ).then_inc(s_bc, 16)
            def toeplitz(k):
                for j in range(JQ):
                    src = bass.AP(tensor=k_pad.tensor, offset=(QD * j + 4 * k) * 2 * P,
                                  ap=[[1, P], [2 * P, 4], [1, P]])
                    sp.dma_start(T[:, k % TRING, :, j, :], src).then_inc(s_t[k], 16)

            sp.wait_ge(s_kd, 16)
            for k in range(TRING):
                toeplitz(k)
            sp.wait_ge(s_sbz, 2 * B)
            sp.dma_start(y_rows.rearrange("(p t) d -> p (t d)", p=P),
                         SBk[:].rearrange("p g j m -> p (g j m)")).then_inc(s_yzr, 16)
            for k in range(TRING, 8):
                sp.wait_ge(s_in, k - TRING + 1)
                toeplitz(k)
            sp.wait_ge(s_y, 8)
            sp.dma_start(W1s, W1.rearrange("e d h -> d e h")).then_inc(s_w12, 16)
            sp.dma_start(W2s, W2.rearrange("e (k q) d -> q e k d", q=P)).then_inc(s_w12, 16)
            sp.wait_ge(s_b3, 2)
            for q in range(3):
                sp.dma_start(BR1[q:q + 1].rearrange("p e h -> p (e h)"), b1p[:, q, :]).then_inc(s_br, 16)
                sp.dma_start(BR2[q:q + 1].rearrange("p e d -> p (e d)"), b2p[:, q, :]).then_inc(s_br, 16)
            for b in range(B):
                sp.wait_ge(s_pje, 2 * b + 2)
                sp.dma_start(xf_rows[b * L:(b + 1) * L].rearrange("(i p) d -> p i d", p=P),
                             XF[:, b * IC:(b + 1) * IC, :]).then_inc(s_xf, 16)
            for u in range(RING):
                sp.wait_ge(s_sc[u], 16 * (MAX_TILES // RING))
            for q in range(2 * B):
                sp.dma_start(final_rows(q), y_rows[q * HT * P:(q + 1) * HT * P].rearrange("(i p) d -> p i d", p=P)
                             ).then_inc(s_yl[q], 16)
            for q in range(2 * B):
                sp.wait_ge(s_res[q], 1)
                b, i = q // 2, HT * (q % 2)
                sp.dma_start(out[b, i * P:(i + HT) * P].rearrange("(i p) d -> p i d", p=P),
                             Hh[:, b, i:i + HT]).then_inc(s_out, 16)
            sp.wait_ge(s_out, 16 * 2 * B)

        @block.gpsimd
        def _(pool):
            g = nc.gpsimd
            step = Steps(pool, s_pool)
            def count_up(dst, n, base, per, channel):
                return g.iota(dst, pattern=[[per, n]], base=base, channel_multiplier=channel,
                              allow_small_or_imprecise_dtypes=True)

            step.mark(g.memset(ident[:], 0.0))
            step.mark(g.memset(onesb[:], 1.0))
            count_up(iota_d[:], P, P - 1, -1, 0)
            count_up(iota_d1[:], P, P, -1, 0)
            count_up(part[:], 1, 0, 0, 1)
            count_up(left[:], 1, P - 1, 0, -1).then_inc(s_iota, 1)
            step.settle()
            g.affine_select(out=ident[:], in_=ident[:], pattern=[[-1, P]], compare_op=ALU.not_equal, fill=1.0,
                            base=0, channel_multiplier=1).then_inc(s_id, 1)
            g.memset(half[:], -0.5)
            g.memset(Wst[:, D * NS:], 0.0)
            g.memset(ones3[:], 1.0).then_inc(s_one, 1)
            pool.wait_ge(s_iota, 1)
            pool.wait_ge(s_one, 1)
            pool.wait_ge(s_la, 2)

            def v_exponents(c):
                n = QD // 4
                g.tensor_tensor(V[:, c * n:c * n + n, :], bc(iota_d1[:].unsqueeze(1), [P, n, P]),
                                bc(LAT[:, c * n:c * n + n].unsqueeze(2), [P, n, P]), ALU.mult).then_inc(s_vl, 1)

            def rstd(w, h, ready, done, count):
                pool.wait_ge(ready, count)
                g.tensor_tensor(rs[:, w, h, :], ve[:, w, h, :], half[:, 0:HT], ALU.pow).then_inc(done, 1)

            def zero_states(q):
                n = QD // (2 * B)
                g.memset(SBk[:, n * q:n * q + n].rearrange("p g j m -> p (g j m)"), 0.0).then_inc(s_sbz, 1)

            v_exponents(0)
            v_exponents(1)
            rstd(0, 0, s_vx, s_rx, 1)
            v_exponents(2)
            rstd(0, 1, s_vx, s_rx, 2)
            v_exponents(3)
            pool.wait_ge(s_kp, 1)
            zero_states(0)

            def norm_step(q, h, clear):
                if clear:
                    pool.wait_ge(s_n, q - 2)
                rstd(1, 1 - h, s_vh, s_rh, q)
                rstd(0, 1 - h, s_vx, s_rx, q + 2)
                zero_states(q)

            for q in range(1, 2 * B - 1):
                norm_step(q, q % 2, q > 2)
            pool.wait_ge(s_n, 5)
            rstd(1, 0, s_vh, s_rh, 2 * B - 1)
            zero_states(2 * B - 1)
            pool.wait_ge(s_n, 6)
            rstd(1, 1, s_vh, s_rh, 2 * B)
            count_up(iota_b[:], P, 0, 1, 0)
            count_up(giota_b[:], MAX_TILES, 0, 1, 0)
            count_up(tiota_b[:], NT, 0, 1, 0)
            count_up(erev[:], E, E, -1, 0)
            count_up(k128[:], IC, 0, P, 0)
            count_up(giota[:], MAX_TILES, 0, 1, 0)
            g.memset(one8[:], 1.0)
            step.mark(g.memset(seg[:], 1.0))
            step.settle()
            g.memset(seg[:, :, 0:1], 0.0)
            g.affine_select(out=lower[:], in_=onesb[:], pattern=[[1, P]], compare_op=ALU.is_gt, fill=0.0,
                            base=0, channel_multiplier=-1).then_inc(s_one, 1)
            pool.wait_ge(s_gl, 1)
            for q in range(2 * B):
                pool.wait_ge(s_n, 2 * B + q - 1)
                rstd(1, q % 2, s_vh, s_rh, 2 * B + q + 1)
                b, t = q // 2, HT * (q % 2)
                g.tensor_tensor(Hh[:, b, t:t + HT], X[:, b, t:t + HT], bc(GLB[:, b:b + 1, :], [P, HT, D]),
                                ALU.add).then_inc(s_x1b, 1)
            pool.wait_ge(s_idx, 1)
            pool.wait_ge(s_xf, 16 * B)
            pool.wait_ge(s_yzr, 16)

            def gather(t):
                u = t % RING
                if t >= RING:
                    pool.wait_ge(s_xp, t - RING + 1)
                pool.indirect_dma_start(out=XG[:, u, :], out_offset=None, in_=xf_rows,
                                        in_offset=bass.IndirectOffsetOnAxis(ap=idgi[:, t:t + 1], axis=0),
                                        bounds_check=N - 1, oob_is_err=False).then_inc(s_g[u], 16)

            def scatter(t):
                pool.wait_ge(s_f, t + 1)
                pool.indirect_dma_start(out=y_rows, out_offset=bass.IndirectOffsetOnAxis(ap=idsi[:, t:t + 1], axis=0),
                                        in_=FO[:, t % RING, :], in_offset=None,
                                        bounds_check=N - 1, oob_is_err=False).then_inc(s_sc[t % RING], 16)

            for t in range(AHEAD):
                gather(t)
            for t in range(MAX_TILES + RING + 1):
                if t < MAX_TILES + RING:
                    pool.wait_ge(s_var1, t + 1)
                    g.tensor_tensor(rs1[:, t % RING, :], ve1[:, t % RING, :], half[:, 0:2],
                                    ALU.pow).then_inc(s_rsd1, 1)
                if t + AHEAD < MAX_TILES:
                    gather(t + AHEAD)
                if t > RING:
                    scatter(t - RING - 1)
            for n, q in enumerate(POOL_UNITS):
                pool.wait_ge(s_yl[q], 16)
                yb = final_rows(q)
                g.tensor_tensor(yb, yb, bc(GL[:, q // 2:q // 2 + 1, :], [P, HT, D]), ALU.mult).then_inc(s_fm, 1)
                pool.wait_ge(s_fm, n + 1)
                hb = Hh[:, q // 2, HT * (q % 2):HT * (q % 2) + HT]
                g.tensor_tensor(hb, hb, yb, ALU.add).then_inc(s_res[q], 1)

        @block.scalar
        def _(act):
            a = nc.scalar
            with nc.allow_non_contiguous_dma("c transposed"):
                act.dma_start(cT[:], c.rearrange("b d -> d b")).then_inc(s_c, 16)
            act.dma_start(wm, wmod.rearrange("k (m d) -> k m d", m=6)).then_inc(s_wm, 16)
            act.dma_start(inw, in_w.rearrange("(a p) d -> p a d", p=P)).then_inc(s_w0, 16)
            act.wait_ge(s_ssm, 64)
            a.activation(EA[:], AL[:], ACT.Exp)
            a.activation(DT[:], LD[:], ACT.Exp).then_inc(s_ea, 1)
            act.wait_ge(s_c, 16)
            a.activation(scT[:], cT[:], ACT.Silu).then_inc(s_silu, 1)
            act.wait_ge(s_kl, 1)
            a.activation(KN, KN, ACT.Exp).then_inc(s_ke, 1)
            act.wait_ge(s_ptr, 1)
            a.copy(inwT[:], PS[:, 0, 0:2 * D])
            a.copy(outwT[:], PS[:, 0, 2 * D:3 * D])
            a.copy(wprT, PS[:, 0, 3 * D:4 * D]).then_inc(s_etr, 1)
            for b in range(B):
                act.wait_ge(s_mod, b + 1)
                for m, one in ((0, 0.0), (1, 1.0), (2, 0.0)):
                    last = a.activation(MOD[:, b, m, :], PS[:, 2 + b, m * D:m * D + D], ACT.Copy, bias=one)
                last.then_inc(s_me, 1)
            act.wait_ge(s_mod, B + 1)
            a.copy(MOD[:, :, 3, :], PS[:, 6, :].rearrange("p (b d) -> p b d", b=B)).then_inc(s_me, 1)
            a.activation(AQ[:], LAT[:], ACT.Exp, scale=float(P)).then_inc(s_aq, 1)
            act.wait_ge(s_lb, 16)
            a.activation(Wst[:, 0:D * NS], Wst[:, 0:D * NS], ACT.Exp,
                         scale=left[:, 0:1]).then_inc(s_wst, 1)
            act.wait_ge(s_vl, 4)
            a.activation(V[:], V[:], ACT.Exp).then_inc(s_v, 1)

            def tiles(buf, b, h):
                return buf[:, bass.ds(b, 1), HT * h:HT * h + HT, :].rearrange("p a i d -> p (a i) d")

            def normed(src, b, h, before, turned, clear):
                q = 2 * b + h
                act.wait_ge(s_nb, before + q + 1)
                if clear:
                    act.wait_ge(turned, q - 1)
                for i in range(HT):
                    last = a.activation(NR[:, HT * h + i, :], tiles(src, b, h)[:, i, :], ACT.Identity,
                                        bias=nb[:, h, i:i + 1], scale=rs[:, 1, h, i:i + 1])
                last.then_inc(s_n, 1)

            def turned(b, h):
                act.wait_ge(s_tp, 2 * b + h + 1)
                a.copy(NTt[:, HT * h:HT * h + HT, :], PS[:, h, :]).then_inc(s_nt, 1)

            def split_uz(b, h):
                act.wait_ge(s_uz, 2 * b + h + 1)
                src = PS[:, 2 + 2 * h:4 + 2 * h, :].rearrange("p k (a c) -> p (k a) c", a=2)
                a.copy(U[:, HT * h:HT * h + HT, bass.ds(b, 1), :].rearrange("p i a d -> p (i a) d"), src[:, :, 0:D])
                a.activation(Z[:, HT * h:HT * h + HT, bass.ds(b, 1), :].rearrange("p i a d -> p (i a) d"),
                             src[:, :, D:2 * D], ACT.Silu).then_inc(s_uze, 1)

            act.wait_ge(s_r1, 1)
            normed(Hh, 0, 0, 0, s_tp, False)
            turned(0, 0)
            normed(Hh, 0, 1, 0, s_tp, False)
            split_uz(0, 0)
            turned(0, 1)
            with nc.scalar.Fori(1, B) as b:
                normed(Hh, b, 0, 0, s_tp, True)
                split_uz(b - 1, 1)
                turned(b, 0)
                normed(Hh, b, 1, 0, s_tp, True)
                split_uz(b, 0)
                turned(b, 1)
            split_uz(B - 1, 1)
            act.wait_ge(s_ptr, 2)
            a.copy(gb1T[:].rearrange("p m e k -> p (m e k)"), PS[:, 1, 0:2 * QD]).then_inc(s_etr, 1)
            act.wait_ge(s_yzr, 16)
            for c2 in range(2):
                act.wait_ge(s_st, c2 + 1)
                half_g = slice(16 * c2, 16 * c2 + 16)
                for j in (2, 3):
                    a.copy(SBk[QD * j:QD * j + QD, half_g, j, :].rearrange("p g (i b) -> p i g b", b=B),
                           St[QD * j:QD * j + QD, :, half_g]).then_inc(s_sbd[c2], 1)
            for k in range(8):
                act.wait_ge(s_y, k + 1)
                if k >= 2:
                    act.wait_ge(s_yt, k - 1)
                dst = YS[:, k % 2, :, P - 1:P]
                dst = bass.AP(tensor=dst.tensor, offset=dst.offset, ap=[*dst.ap[:-1], [-1, P]])
                a.copy(dst, PS[:, k, :].rearrange("p (g q) -> p g q", g=4)).then_inc(s_ys, 1)

            def gated(q):
                h = q % 2
                act.wait_ge(s_tp2, q + 1)
                if q >= 2:
                    act.wait_ge(s_op, q - 1)
                a.copy(YT2[:, HT * h:HT * h + HT, :], PS[:, h, :]).then_inc(s_nt2, 1)

            def projected(q):
                act.wait_ge(s_pj, q + 1)
                src = PS[:, 6:8, :].rearrange("p k (a c) -> p (k a) c", a=2)
                a.copy(XF[:, HT * q:HT * q + HT, :], src[:, :, 0:D])
                a.copy(LG[:, HT * q:HT * q + HT, :], src[:, :, D:PJ]).then_inc(s_pje, 1)

            def turned2(q):
                h = q % 2
                act.wait_ge(s_tp3, q + 1)
                a.copy(NTt[:, HT * h:HT * h + HT, :], PS[:, 4 + h, :]).then_inc(s_nt3, 1)

            gated(0)
            for q in range(2 * B + 3):
                if q + 1 < 2 * B:
                    gated(q + 1)
                if 0 <= q - 2 < 2 * B:
                    normed(X, (q - 2) // 2, q % 2, 2 * B, s_tp3, q >= 4)
                if q >= 3:
                    projected(q - 3)
                if 0 <= q - 2 < 2 * B:
                    turned2(q - 2)

            act.wait_ge(s_ot, 1)
            a.activation(OT[:, :, 2, :], OT[:, :, 0, :], ACT.Identity, scale=part[:, 0:1]).then_inc(s_otp, 1)

            def copy_xt(t, u, first):
                act.wait_ge(s_xp, t + 1)
                if not first:
                    act.wait_ge(s_h, t - RING + 1)
                a.copy(XT[:, u, :], PS[:, 4, 0:P]).then_inc(s_xt, 1)

            def gelu(t, u, first):
                e = act.value_load(texpi[0:1, bass.ds(t, 1)], min_val=0, max_val=E - 1)
                act.wait_ge(s_hp, t + 1)
                if not first:
                    act.wait_ge(s_o, t - RING + 1)
                for k in range(KC):
                    a.activation(AT[:, u, k, :], PS[:, 3, P * k:P * k + P], ACT.Gelu,
                                 bias=gb1T[:, 1, bass.ds(e, 1), k],
                                 scale=gb1T[:, 0, bass.ds(e, 1), k]).then_inc(s_a, 1)

            act.wait_ge(s_te, 1)
            for u in range(RING):
                copy_xt(u, u, True)
            for u in range(RING):
                copy_xt(RING + u, u, False)
                gelu(u, u, True)
            with nc.scalar.Fori(1, MAX_TILES // RING - 1) as i:
                for u in range(RING):
                    copy_xt(RING * i + u + RING, u, False)
                    gelu(RING * i + u, u, False)
            for t in range(MAX_TILES - RING, MAX_TILES):
                gelu(t, t % RING, False)

        @block.vector
        def _(dve):
            v = nc.vector
            step = Steps(dve, s_dve)
            v.memset(LA32[:], 0.0)
            v.memset(CB32[:], 0.0)
            step.mark(v.memset(KP[:, P:2 * P], 0.0))
            dve.wait_ge(s_ssm, 64)
            dve.wait_ge(s_ea, 1)
            step.mark(v.tensor_scalar(DT[:], DT[:], 1e-4, 1.0, ALU.max, ALU.min))
            step.settle()
            step.mark(v.tensor_scalar(EA[:], EA[:], DT[:, 0:1], -1.0, ALU.mult, ALU.mult))
            step.mark(v.tensor_scalar(CP[:], CP[:], DT[:, 0:1], None, ALU.mult))
            step.settle()
            v.tensor_scalar(LA32[:, 0:NS], EA[:], LOG_LO, 0.0, ALU.max, ALU.min).then_inc(s_la, 1)
            step.mark(v.tensor_tensor(CB32[:, 0:NS], CP[:], BP[:], ALU.mult))
            dve.wait_ge(s_la, 1)
            step.settle()
            step.mark(v.transpose(CBT[:], CB32[:]))
            v.transpose(LAT[:], LA32[:]).then_inc(s_la, 1)
            dve.wait_ge(s_iota, 1)
            v.tensor_tensor(KN, bc(iota_d[:].unsqueeze(1), [P, NS, P]), bc(LA32[:, 0:NS].unsqueeze(2), [P, NS, P]),
                            ALU.mult).then_inc(s_kl, 1)

            def tiles(buf, b, h):
                return buf[:, bass.ds(b, 1), HT * h:HT * h + HT, :].rearrange("p a i d -> p (a i) d")

            def row_stats(src, w, h):
                c = 4 * w + 2 * h
                v.memset(tick[:, c:c + 1], 0.0)
                for i in range(HT):
                    last = v.bn_stats(st[:, w, h, i, :], src[:, i, :])
                return last

            def row_means(w, h):
                c = 4 * w + 2 * h + 1
                v.memset(tick[:, c:c + 1], 0.0)
                for i in range(HT):
                    last = v.bn_aggr(mv[:, w, h, i, :], st[:, w, h, i, :])
                return last

            def row_vars(w, h):
                return v.tensor_scalar(ve[:, w, h, :], mv[:, w, h, :, 1], LN_EPS, None, ALU.add)

            def shifts(h):
                return v.scalar_tensor_tensor(nb[:, h, :], mv[:, 1, h, :, 0], -1.0, rs[:, 1, h, :],
                                              ALU.mult, ALU.mult)

            def modulate(b, h, first=False, last=False):
                q, o = 2 * b + h, 1 - h
                before = step.now()
                if not last:
                    sums_x = step.mark(row_stats(tiles(X, b + h, o), 0, o))
                if not first:
                    step.settle(before)
                    means_h = step.mark(row_means(1, o))
                dve.wait_ge(s_rx, q + 1)
                src, dst = tiles(X, b, h), tiles(Hh, b, h)
                for i in range(HT):
                    ins = v.tensor_scalar(dst[:, i, :], src[:, i, :], mv[:, 0, h, i, 0:1], rs[:, 0, h, i:i + 1],
                                          ALU.subtract, ALU.mult)
                normed = step.mark(ins)
                if not first:
                    step.settle(means_h)
                    row_vars(1, o).then_inc(s_vh, 1)
                if not last:
                    step.settle(sums_x)
                    means_x = step.mark(row_means(0, o))
                step.settle(normed)
                if first:
                    dve.wait_ge(s_me, 1)
                scaled = step.mark(v.tensor_tensor(dst, dst, bc(MOD[:, bass.ds(b, 1), 1, :], [P, HT, D]), ALU.mult))
                if not last:
                    step.settle(means_x)
                    row_vars(0, o).then_inc(s_vx, 1)
                step.settle(scaled)
                shifted = step.mark(v.tensor_tensor(dst, dst, bc(MOD[:, bass.ds(b, 1), 0, :], [P, HT, D]), ALU.add))
                if not first:
                    dve.wait_ge(s_rh, q)
                    shifts(o).then_inc(s_nb, 1)
                step.settle(shifted)
                step.mark(row_stats(dst, 1, h))

            def three_parts(row, part_row, tmp):
                for m in range(2):
                    step.mark(v.tensor_copy(tmp, row))
                    step.settle()
                    step.mark(v.scalar_tensor_tensor(row, tmp, below[:, m:m + 1], row, ALU.mult, ALU.add))
                    step.settle()
                return v.tensor_copy(part_row, row)

            dve.wait_ge(s_x0, 16)
            step.mark(row_stats(tiles(X, 0, 0), 0, 0))
            for m in range(2):
                v.tensor_scalar(below[:, m:m + 1], part[0:3], m + 0.5, -1.0, ALU.is_ge, ALU.mult)
            step.settle()
            step.mark(row_means(0, 0))
            step.settle()
            row_vars(0, 0).then_inc(s_vx, 1)
            dve.wait_ge(s_ke, 1)
            step.mark(v.tensor_tensor(KN, KN, bc(CB32[:, 0:NS].unsqueeze(2), [P, NS, P]), ALU.mult))
            step.settle()
            v.tensor_reduce(KP[:, 0:P], KN.rearrange("p n l -> p l n"), AX.X, ALU.add).then_inc(s_kp, 1)
            modulate(0, 0, first=True)
            dve.wait_ge(s_w, 144)
            dve.wait_ge(s_etr, 1)
            v.tensor_scalar(inwG[:], inwT[:], lngc[:, 0:1], None, ALU.mult).then_inc(s_inw, 1)
            dve.wait_ge(s_r1, 1)
            step.mark(v.tensor_tensor(row_in[:], row_in[:], PS[0:3, 7, 0:2 * D], ALU.add))
            step.settle()
            three_parts(row_in[:], part_in[:], part_in[:]).then_inc(s_r1e, 1)
            dve.wait_ge(s_x, 16 * (B - 1))
            dve.wait_ge(s_me, B)
            with nc.vector.Fori(1, B) as b:
                step.enter(b - 1, 14)
                modulate(b - 1, 1)
                modulate(b, 0)
                step.leave(B - 1)
            modulate(B - 1, 1, last=True)
            step.settle()
            step.mark(row_means(1, 1))
            step.settle()
            row_vars(1, 1).then_inc(s_vh, 1)
            dve.wait_ge(s_rh, 2 * B)
            shifts(1).then_inc(s_nb, 1)

            step.mark(v.tensor_copy(cbsT[:, 0, :], PS[:, 7, 256:260]))
            step.mark(v.tensor_scalar(cbsT[:, 1, :], PS[:, 7, 260:264], 1.0, None, ALU.add))
            step.mark(v.tensor_copy(WPG[:, 0:D], wpr[:]))
            step.mark(v.tensor_copy(WPG[:, D:PJ], PS[:, 7, 264:272]))
            step.mark(v.tensor_copy(row_pj[:, D:PJ], PS[0:3, 7, 272:280]))
            step.settle()
            for b in range(B):
                last = v.tensor_scalar(WPB[:, b, :], WPG[:], cbsT[:, 1, b:b + 1], None, ALU.mult)
            last.then_inc(s_wge, 1)
            dve.wait_ge(s_me, B + 1)
            for m in (2, 3):
                step.mark(v.scalar_tensor_tensor(GT, MOD[:, :, m, :], -1.0, MOD[:, :, m, :], ALU.mult, ALU.max))
                step.mark(v.tensor_scalar(GT2, MOD[:, :, m, :], 0.0, 2.0, ALU.is_ge, ALU.mult))
                step.settle()
                step.mark(v.tensor_scalar(GT2, GT2, -1.0, None, ALU.add))
                step.mark(v.tensor_scalar(GT, GT, 0.25, None, ALU.max))
                step.settle()
                step.mark(v.tensor_tensor(MOD[:, :, m, :], GT, GT2, ALU.mult))
                step.settle()
            dve.wait_ge(s_bc, 32)
            v.tensor_tensor(GL[:], MOD[:, :, 3, :], bc(lngb[:, 0:1, :], [P, B, D]), ALU.mult)
            v.tensor_tensor(GLB[:], MOD[:, :, 3, :], bc(lngb[:, 1:2, :], [P, B, D]), ALU.mult).then_inc(s_gl, 1)
            dve.wait_ge(s_r2, 1)
            for b in range(B):
                last = v.tensor_tensor(row_pb[:, b * PJ:b * PJ + PJ], row_pj[:],
                                       pb_product(b), ALU.add)
            step.mark(last)
            step.settle()
            step.mark(three_parts(row_out[:], part_out[:], part_out[:]))
            three_parts(row_pb[:], part_pb[:], part_pb[:]).then_inc(s_r2e, 1)
            step.mark(v.memset(St[:, 0], 0.0))
            dve.wait_ge(s_aq, 1)
            for c2 in range(2):
                dve.wait_ge(s_sin, c2 + 1)
                half_g = slice(16 * c2, 16 * c2 + 16)
                sin = PS[:, 6 + c2, :].rearrange("p (g i b) -> p i g b", i=IC, b=B)
                S, decay, tmp = St[:, :, half_g], bc(AQ[:, half_g].unsqueeze(2), [P, 16, B]), Stmp[:, half_g]
                step.mark(v.tensor_copy(S[:, 1], sin[:, 0]))
                step.settle()
                for i in range(1, IC - 1):
                    step.mark(v.tensor_tensor(tmp, S[:, i], decay, ALU.mult))
                    step.settle()
                    step.mark(v.tensor_tensor(S[:, i + 1], tmp, sin[:, i], ALU.add))
                    step.settle()
                S = S.rearrange("p i g b -> p g i b")
                v.tensor_tensor(S, S, bc(CBT[:, half_g].unsqueeze(2).unsqueeze(3), [P, 16, IC, B]),
                                ALU.mult).then_inc(s_st, 1)
                dve.wait_ge(s_st, c2 + 1)
                if c2 == 0:
                    dve.wait_ge(s_yzr, 16)
                for j in (0, 1):
                    v.tensor_copy(SBk[QD * j:QD * j + QD, half_g, j, :].rearrange("p g (i b) -> p i g b", b=B),
                                  St[QD * j:QD * j + QD, :, half_g]).then_inc(s_sbd[c2], 1)
            dve.wait_ge(s_e, 64)
            for nat, rest, parts in ((b1n, b1r, b1p), (b2n, b2r, b2p)):
                step.mark(v.tensor_copy(parts[:, 0, :], nat[:]))
                step.settle()
                step.mark(v.tensor_tensor(rest[:], nat[:], parts[:, 0, :], ALU.subtract))
                step.settle()
                step.mark(v.tensor_copy(parts[:, 1, :], rest[:]))
                step.settle()
                step.mark(v.tensor_tensor(rest[:], rest[:], parts[:, 1, :], ALU.subtract))
                step.settle()
                v.tensor_copy(parts[:, 2, :], rest[:]).then_inc(s_b3, 1)
            for k in range(8):
                dve.wait_ge(s_yt, k + 1)
                zk = Z[:].rearrange("p i b (j g) -> p g j (i b)", g=QD)[:, 4 * k:4 * k + 4]
                src = PS[:, k, :].rearrange("p (g j m) -> p g j m", g=4, j=JQ)
                for g4 in range(4):
                    last = v.tensor_tensor(zk[:, g4], src[:, g4], zk[:, g4], ALU.mult)
                last.then_inc(s_yz, 1)

            def mixer_out(b, h, first=False):
                q, o = 2 * b + h, 1 - h
                hb, xb = tiles(Hh, b, h), tiles(X, b, h)
                before = step.now()
                dve.wait_ge(s_op, q + 1)
                summed = step.mark(v.tensor_tensor(hb, PS[:, 2 + h, :].rearrange("p (i d) -> p i d", d=D), hb,
                                                   ALU.add))
                if not first:
                    step.settle(before)
                    means = step.mark(row_means(1, o))
                step.settle(summed)
                clipped = step.mark(v.tensor_scalar(hb, hb, 10.0, -10.0, ALU.min, ALU.max))
                if not first:
                    step.settle(means)
                    row_vars(1, o).then_inc(s_vh, 1)
                step.settle(clipped)
                gated = step.mark(v.tensor_tensor(hb, hb, bc(MOD[:, bass.ds(b, 1), 2, :], [P, HT, D]), ALU.mult))
                step.settle(gated)
                v.tensor_tensor(xb, xb, hb, ALU.add).then_inc(s_x1, 1)
                if not first:
                    dve.wait_ge(s_rh, 2 * B + q)
                    shifts(o).then_inc(s_nb, 1)
                dve.wait_ge(s_x1, q + 1)
                step.mark(row_stats(xb, 1, h))

            mixer_out(0, 0, first=True)
            with nc.vector.Fori(1, B) as b:
                step.enter(b - 1, 10)
                mixer_out(b - 1, 1)
                mixer_out(b, 0)
                step.leave(B - 1)
            mixer_out(B - 1, 1)
            step.settle()
            step.mark(row_means(1, 1))
            step.settle()
            row_vars(1, 1).then_inc(s_vh, 1)
            dve.wait_ge(s_rh, 4 * B)
            shifts(1).then_inc(s_nb, 1)

            dve.wait_ge(s_pje, 2 * B)
            step.mark(v.memset(texp[:], 0.0))
            step.mark(v.tensor_reduce(top[:], LG, AX.X, ALU.max))
            step.settle()
            step.mark(v.tensor_tensor(RA, LG, bc(top[:].unsqueeze(2), [P, NT, E]), ALU.is_equal))
            step.settle()
            step.mark(v.tensor_tensor(RA, RA, bc(erev[:].unsqueeze(1), [P, NT, E]), ALU.mult))
            step.settle()
            step.mark(v.tensor_reduce(top[:], RA, AX.X, ALU.max))
            step.settle()
            step.mark(v.tensor_tensor(Mf, bc(erev[:].unsqueeze(1), [P, NT, E]), bc(top[:].unsqueeze(2), [P, NT, E]),
                                      ALU.is_equal))
            step.settle()
            v.tensor_copy(Mb[:], Mf).then_inc(s_m, 1)
            dve.wait_ge(s_cnt, 1)
            rank = PS[:, 0, 0:NT * E].rearrange("p (t e) -> p e t", e=E)
            step.mark(v.tensor_copy(tot, PS[:, 1, 0:NT * E].rearrange("p (t e) -> p e t", e=E)))
            step.settle()
            flat = lambda ap: ap.rearrange("p e t -> p (e t)")
            step.mark(v.tensor_tensor_scan(flat(inc), flat(seg[:]), flat(tot), 0.0, ALU.mult, ALU.add))
            step.settle()
            step.mark(v.tensor_tensor(exc, inc, tot, ALU.subtract))
            step.mark(v.tensor_scalar(nte[:], inc[:, :, NT - 1], float(CAPACITY), None, ALU.min))
            step.settle()
            step.mark(v.tensor_tensor(cmpk, bc(nte[:].unsqueeze(2), [P, E, IC]), bc(k128[:].unsqueeze(1), [P, E, IC]),
                                      ALU.is_gt))
            step.mark(v.tensor_tensor(pos, exc, rank, ALU.add))
            step.settle()
            step.mark(v.tensor_reduce(nte[:], cmpk, AX.X, ALU.add))
            step.settle()
            step.mark(v.tensor_tensor_scan(tend[:], one8[:], nte[:], 0.0, ALU.mult, ALU.add))
            step.settle()
            step.mark(v.tensor_tensor(tbeg[:], tend[:], nte[:], ALU.subtract))
            step.mark(v.tensor_tensor(gcmp, bc(giota[:].unsqueeze(1), [P, E, MAX_TILES]),
                                      bc(tend[:].unsqueeze(2), [P, E, MAX_TILES]), ALU.is_ge))
            step.mark(v.tensor_scalar(sel, pos, float(CAPACITY), None, ALU.is_lt))
            step.settle()
            step.mark(v.tensor_scalar(tbeg[:], tbeg[:], float(P), None, ALU.mult))
            step.mark(v.tensor_reduce(texp[:, 1:1 + MAX_TILES], gcmp.rearrange("p e g -> p g e"), AX.X, ALU.add))
            me = Mf.rearrange("p t e -> p e t")
            step.mark(v.tensor_tensor(sel, sel, me, ALU.mult))
            step.settle()
            step.mark(v.tensor_tensor(pos, pos, bc(tbeg[:].unsqueeze(2), [P, E, NT]), ALU.add))
            step.mark(v.tensor_reduce(keep[:], sel.rearrange("p e t -> p t e"), AX.X, ALU.add))
            step.mark(v.tensor_scalar(texp[:], texp[:], float(E - 1), None, ALU.min))
            step.settle()
            rounds3 = texp[:].rearrange("p (i c) -> p i c", c=RING)
            v.tensor_copy(texpr[:, :, 0:RING], rounds3[:, 0:MAX_TILES // RING])
            v.tensor_copy(texpr[:, :, RING:2 * RING], rounds3[:, 1:])
            v.tensor_copy(texpi[:], texp[:, 1:1 + MAX_TILES]).then_inc(s_te, 1)
            step.mark(v.tensor_tensor(pos, pos, me, ALU.mult))
            step.settle()
            step.mark(v.tensor_reduce(slot[:], pos.rearrange("p e t -> p t e"), AX.X, ALU.add))
            step.mark(v.tensor_scalar(keep[:], keep[:], -float(2 * N), float(2 * N), ALU.mult, ALU.add))
            step.settle()
            step.mark(v.tensor_tensor(slot[:], slot[:], keep[:], ALU.add))
            step.settle()
            step.mark(v.tensor_copy(sloti[:], slot[:]))
            step.settle()
            step.mark(v.tensor_scalar(rowi[:], sloti[:], P - 1, None, ALU.bitwise_and))
            step.mark(v.tensor_scalar(tili[:], sloti[:], 7, None, ALU.arith_shift_right))
            step.settle()
            step.mark(v.tensor_copy(rowb[:], rowi[:]))
            step.mark(v.tensor_copy(tilb[:], tili[:]))
            step.settle()
            wide = [P, NT, MAX_TILES]
            v.tensor_tensor(OT[:, :, 0, :], bc(giota_b[:].unsqueeze(1), wide), bc(tilb[:].unsqueeze(2), wide),
                            ALU.is_equal).then_inc(s_ot, 1)
            n = NT // 4
            for c4 in range(4):
                v.tensor_tensor(OR[:, n * c4:n * c4 + n], bc(iota_b[:].unsqueeze(1), [P, n, P]),
                                bc(rowb[:, n * c4:n * c4 + n].unsqueeze(2), [P, n, P]), ALU.is_equal).then_inc(s_oh, 1)
                if c4 == 0:
                    dve.wait_ge(s_ot, 1)
                    v.tensor_tensor(OT[:, :, 1, :], OT[:, :, 0, :], bc(tiota_b[:].unsqueeze(2), wide),
                                    ALU.mult).then_inc(s_oh, 1)
            dve.wait_ge(s_ids, 1)
            step.mark(v.tensor_copy(idf.rearrange("p c g -> p (c g)"), PS[:, 2, 0:3 * MAX_TILES]))
            step.settle()
            step.mark(v.tensor_scalar(idg, idf[:, 1, :], float(P), None, ALU.mult))
            step.mark(v.tensor_scalar(ids, idf[:, 0, :], -float(2 * N), float(2 * N), ALU.mult, ALU.add))
            step.settle()
            step.mark(v.tensor_tensor(idg, idg, idf[:, 2, :], ALU.add))
            step.settle()
            step.mark(v.tensor_tensor(ids, ids, idg, ALU.add))
            step.mark(v.tensor_copy(idgi[:], idg))
            step.settle()
            v.tensor_copy(idsi[:], ids).then_inc(s_idx, 1)

            def expert_step(t, u, rounds=None):
                static = isinstance(t, int)
                hidden, rows = not static or t < MAX_TILES, not static or RING <= t < MAX_TILES + RING
                stats = hidden or rows
                pairs = slice(0, 2) if hidden and rows else slice(0, 1) if hidden else slice(1, 2)
                if hidden:
                    dve.wait_ge(s_h, t + 1)
                    last = v.bn_stats(st1[:, u, 0, :], PS[:, u, :])
                if rows:
                    dve.wait_ge(s_o, t - RING + 1)
                    last = v.bn_stats(st1[:, u, 1, :], PS[:, 5 + u, 0:D])
                if stats:
                    step.mark(last)
                if not static or 1 <= t <= MAX_TILES:
                    dve.wait_ge(s_rsd1, t)
                    if not static or t > RING:
                        dve.wait_ge(s_hp, t - RING)
                    w = (u - 1) % RING
                    v.tensor_scalar(NH[:, w, :], PS[:, w, :], mv1[:, w, 0, 0:1], rs1[:, w, 0:1],
                                    ALU.subtract, ALU.mult).then_inc(s_nh, 1)
                if stats:
                    step.settle()
                    v.memset(tick[:, 0:1], 0.0)
                    for q in (0, 1)[pairs]:
                        last = v.bn_aggr(mv1[:, u, q, :], st1[:, u, q, :])
                    step.mark(last)
                if not static or t > RING:
                    w = (u - 1) % RING
                    dve.wait_ge(s_rsd1, t)
                    if rounds is not None:
                        dve.wait_ge(s_sc[w], 16 * rounds)
                    v.tensor_scalar(FO[:, w, :], PS[:, 5 + w, 0:D], mv1[:, w, 1, 0:1], rs1[:, w, 1:2],
                                    ALU.subtract, ALU.mult).then_inc(s_f, 1)
                if stats:
                    step.settle()
                    v.tensor_scalar(ve1[:, u, pairs], mv1[:, u, pairs, 1], LN_EPS, None, ALU.add).then_inc(s_var1, 1)

            step.mark(v.memset(ve1[:], 1.0))
            step.settle()

            def rounds_at(t):
                done = (t - RING - 1) // RING
                return done if done > 0 else None

            for t in range(3 * RING):
                expert_step(t, t % RING, rounds_at(t))
            with nc.vector.Fori(3, MAX_TILES // RING) as i:
                step.enter(i - 3, 2 * RING)
                for u in range(RING):
                    expert_step(RING * i + u, u, i - 1 if u else i - 2)
                step.leave(MAX_TILES // RING - 3)
            for t in range(MAX_TILES, MAX_TILES + RING + 1):
                expert_step(t, t % RING, rounds_at(t))

            dve.wait_ge(s_x1b, 2 * B)
            last_units = [q for q in range(2 * B) if q not in POOL_UNITS]
            for q in last_units:
                dve.wait_ge(s_yl[q], 16)
                yb = final_rows(q)
                step.mark(v.tensor_tensor(yb, yb, bc(GL[:, q // 2:q // 2 + 1, :], [P, HT, D]), ALU.mult))
                step.settle()
                hb = Hh[:, q // 2, HT * (q % 2):HT * (q % 2) + HT]
                v.tensor_tensor(hb, hb, yb, ALU.add).then_inc(s_res[q], 1)

        @block.tensor
        def _(pe):
            m = nc.tensor
            pe.wait_ge(s_id, 1)
            pe.wait_ge(s_w0, 16)
            m.transpose(PS[:, 0, 0:D], inw[:, 0, :], ident[:])
            m.transpose(PS[:, 0, D:2 * D], inw[:, 1, :], ident[:])
            pe.wait_ge(s_silu, 1)
            pe.wait_ge(s_wm, 16)
            wmf = wm.rearrange("p m d -> p (m d)")
            for b in range(B):
                m.matmul(PS[:, 2 + b, 0:3 * D], bc(scT[:, b:b + 1], [P, P]), wmf[:, 0:3 * D],
                         start=True, stop=True).then_inc(s_mod, 1)
                if b == 0:
                    pe.wait_ge(s_w, 144)
                    m.transpose(PS[:, 0, 2 * D:3 * D], outw, ident[:])
                    m.transpose(PS[:, 0, 3 * D:4 * D], wpr[:], ident[:]).then_inc(s_ptr, 1)
            for b in range(B):
                last = m.matmul(PS[:, 6, b * D:b * D + D], bc(scT[:, b:b + 1], [P, P]), wm[:, 5, :],
                                start=True, stop=True)
            last.then_inc(s_mod, 1)
            pe.wait_ge(s_etr, 1)
            m.matmul(PS[0:3, 7, 0:2 * D], bc(lnbc[:], [P, 3]), inwT[:], start=True, stop=True)
            m.matmul(PS[:, 7, 256:260], wm[:, 3, :], scT[:], start=True, stop=True)
            m.matmul(PS[:, 7, 260:264], wm[:, 4, :], scT[:], start=True, stop=True)
            m.matmul(PS[:, 7, 264:272], wprT, wgt[:], start=True, stop=True)
            m.matmul(PS[0:3, 7, 272:280], bc(bpc[:], [P, 3]), wgt[:], start=True, stop=True).then_inc(s_r1, 1)

            def rows_turn(h, q):
                pe.wait_ge(s_n, q + 1)
                for i in range(HT):
                    last = m.transpose(PS[:, h, P * i:P * i + P], NR[:, HT * h + i, :], ident[:])
                last.then_inc(s_tp, 1)

            def in_products(h, q, clear):
                pe.wait_ge(s_nt, q + 1)
                if clear:
                    pe.wait_ge(s_uze, q - 1)
                for i in range(HT):
                    dst = PS[:, 2 + 2 * h + i // 2, i % 2 * 256:i % 2 * 256 + 256]
                    m.matmul(dst, NTt[:, HT * h + i, :], inwG[:], start=True, stop=False)
                    last = m.matmul(dst, ones3[:], part_in[:], start=False, stop=True)
                last.then_inc(s_uz, 1)

            pe.wait_ge(s_me, B)
            pe.wait_ge(s_inw, 1)
            pe.wait_ge(s_r1e, 1)
            pe.wait_ge(s_one, 1)
            for h in range(2):
                rows_turn(h, h)
                in_products(h, h, False)
            with nc.tensor.Fori(1, B) as b:
                for h in range(2):
                    rows_turn(h, 2 * b + h)
                    in_products(h, 2 * b + h, True)
            pe.wait_ge(s_e, 64)
            m.transpose(PS[:, 1, 0:QD], gb1[:, 0, :], ident[0:QD, 0:QD])
            m.transpose(PS[:, 1, QD:2 * QD], gb1[:, 1, :], ident[0:QD, 0:QD]).then_inc(s_ptr, 1)
            pe.wait_ge(s_wge, 1)
            pe.wait_ge(s_etr, 2)
            for b in range(B):
                last = m.matmul(pb_product(b), bc(cbsT[:, 0, b:b + 1], [P, 3]), WPG[:], start=True, stop=True)
            last.then_inc(s_r2, 1)
            pe.wait_ge(s_uze, 2 * B)
            pe.wait_ge(s_wst, 1)
            pe.wait_ge(s_me, B + 1)
            Um = U[:].rearrange("p i b d -> p (i b) d")
            for g in range(QD):
                for j in range(JQ):
                    d = QD * j + g
                    last = m.matmul(PS[QD * j:QD * j + QD, 6 + g // 16, g % 16 * QD:g % 16 * QD + QD],
                                    Wst[:, d * NS:d * NS + QD], Um[:, :, d], start=True, stop=True,
                                    skip_group_check=True)
                if g % 16 == 15:
                    last.then_inc(s_sin, 1)
            pe.wait_ge(s_r2e, 1)

            def inside(k):
                pe.wait_ge(s_t[k], 16 * JQ)
                for g in range(4 * k, 4 * k + 4):
                    for j in range(JQ):
                        last = m.matmul(PS[QD * j:QD * j + QD, k, g % 4 * P:g % 4 * P + P], Um[:, :, QD * j + g],
                                 T[:, k % TRING, g % 4, j, :], start=(g % 4 == 0), stop=False, skip_group_check=True)

                last.then_inc(s_in, 1)

            def between(k):
                if k % 4 == 0:
                    pe.wait_ge(s_sbd[k // 4], JQ)
                for g in range(4 * k, 4 * k + 4):
                    last = m.matmul(PS[:, k, g % 4 * P:g % 4 * P + P], SBk[:, g].rearrange("p j m -> p (j m)"),
                                    V[:, g, :], start=False, stop=True, skip_group_check=True)
                last.then_inc(s_y, 1)

            def back(k):
                pe.wait_ge(s_ys, k + 1)
                for g in range(4):
                    last = m.transpose(PS[:, k, P * g:P * g + P], YS[:, k % 2, g, :], ident[:])
                last.then_inc(s_yt, 1)

            for k in range(6):
                inside(k)
            pe.wait_ge(s_v, 1)
            for k in range(8):
                if k >= 6:
                    inside(k)
                between(k)
                if k:
                    back(k - 1)
            back(7)

            def gated_turn(q):
                for i in range(HT):
                    last = m.transpose(PS[:, q % 2, P * i:P * i + P], Z[:, HT * (q % 2) + i, q // 2, :], ident[:])
                last.then_inc(s_tp2, 1)

            def gated_out(q):
                h = q % 2
                pe.wait_ge(s_nt2, q + 1)
                if q >= 2:
                    pe.wait_ge(s_x1, q - 1)
                for i in range(HT):
                    dst = PS[:, 2 + h, P * i:P * i + P]
                    m.matmul(dst, YT2[:, HT * h + i, :], outwT[:], start=True, stop=False)
                    last = m.matmul(dst, ones3[:], part_out[:], start=False, stop=True)
                last.then_inc(s_op, 1)

            def rows_turn2(q):
                pe.wait_ge(s_n, 2 * B + q + 1)
                for i in range(HT):
                    last = m.transpose(PS[:, 4 + q % 2, P * i:P * i + P], NR[:, HT * (q % 2) + i, :], ident[:])
                last.then_inc(s_tp3, 1)

            def project(q):
                b = q // 2
                pe.wait_ge(s_nt3, q + 1)
                if q:
                    pe.wait_ge(s_pje, q)
                for i in range(HT):
                    dst = PS[:, 6 + i // 2, i % 2 * 256:i % 2 * 256 + PJ]
                    m.matmul(dst, NTt[:, HT * (q % 2) + i, :], WPB[:, b, :], start=True, stop=False)
                    last = m.matmul(dst, ones3[:], part_pb[:, b * PJ:b * PJ + PJ], start=False, stop=True)
                last.then_inc(s_pj, 1)

            pe.wait_ge(s_yz, 8)
            gated_turn(0)
            for q in range(2 * B + 3):
                if q + 1 < 2 * B:
                    gated_turn(q + 1)
                if q < 2 * B:
                    gated_out(q)
                if q >= 3:
                    project(q - 3)
                if 0 <= q - 2 < 2 * B:
                    rows_turn2(q - 2)

            pe.wait_ge(s_one, 2)
            pe.wait_ge(s_m, 1)
            mb = Mb[:].rearrange("p t e -> p (t e)")
            m.matmul(PS[:, 0, 0:NT * E], lower[:], mb, start=True, stop=True)
            m.matmul(PS[:, 1, 0:NT * E], onesb[:], mb, start=True, stop=True).then_inc(s_cnt, 1)
            pe.wait_ge(s_otp, 1)
            for t in range(NT):
                if t % (NT // 4) == 0:
                    pe.wait_ge(s_oh, 2 + t // (NT // 4))
                last = m.matmul(PS[:, 2, 0:3 * MAX_TILES], OR[:, t, :], OT[:, t].rearrange("p c g -> p (c g)"),
                                start=(t == 0), stop=(t == NT - 1))
            last.then_inc(s_ids, 1)

            def rows_in(t, u, rounds):
                pe.wait_ge(s_g[u], 16 * rounds)
                m.transpose(PS[:, 4, 0:P], XG[:, u, :], ident[:]).then_inc(s_xp, 1)

            def experts(i, name):
                regs = [pe.alloc_register(f"experts_{name}{q}") for q in range(2 * RING)]
                pe.load(regs, texpr[0:1, bass.ds(i, 1), 0:2 * RING].rearrange("p a c -> p (a c)"))
                return [pe.snap(r, donate=True, min_val=0, max_val=E - 1) for r in regs]

            def up(t, u, e):
                pe.wait_ge(s_xt, t + 1)
                m.matmul(PS[:, u, :], XT[:, u, :], W1s[:, bass.ds(e, 1), :].rearrange("p a h -> p (a h)"),
                         start=True, stop=False)
                m.matmul(PS[:, u, :], ones3[:], BR1[:, bass.ds(e, 1), :].rearrange("p a h -> p (a h)"),
                         start=False, stop=True).then_inc(s_h, 1)

            def turn(t, u):
                pe.wait_ge(s_nh, t + 1)
                for k in range(KC):
                    last = m.transpose(PS[:, 3, P * k:P * k + P], NH[:, u, P * k:P * k + P], ident[:])
                last.then_inc(s_hp, 1)

            def down(t, u, e, first):
                dst = PS[:, 5 + u, 0:D]
                if not first:
                    pe.wait_ge(s_f, t - RING + 1)
                for k in range(KC):
                    pe.wait_ge(s_a, KC * t + k + 1)
                    m.matmul(dst, AT[:, u, k, :], W2s[:, bass.ds(e, 1), k, :].rearrange("p a d -> p (a d)"),
                             start=(k == 0), stop=False)
                m.matmul(dst, ones3[:], BR2[:, bass.ds(e, 1), :].rearrange("p a d -> p (a d)"),
                         start=False, stop=True).then_inc(s_o, 1)

            def tile_step(t, u, i, e):
                static = isinstance(i, int)
                if not static or t + 2 < MAX_TILES:
                    up(t + 2, (u + 2) % RING, e[u + RING])
                if not static or t + RING < MAX_TILES:
                    rows_in(t + RING, u, i + 2)
                if not static or t >= 1:
                    down(t - 1, (u - 1) % RING, e[u], static and t - 1 < RING)
                turn(t, u)

            pe.wait_ge(s_te, 1)
            pe.wait_ge(s_w12, 32)
            pe.wait_ge(s_br, 96)
            pe.wait_ge(s_idx, 1)
            e = experts(0, "start")
            rows_in(0, 0, 1)
            for t in range(2):
                pe.wait_ge(s_xt, t + 1)
                rows_in(t + 1, t + 1, 1)
                up(t, t, e[t + 1])
            for i in range(2):
                if i:
                    e = experts(i, "second")
                for u in range(RING):
                    tile_step(RING * i + u, u, i, e)
            with nc.tensor.Fori(2, MAX_TILES // RING - 1) as i:
                e = experts(i, "loop")
                for u in range(RING):
                    tile_step(RING * i + u, u, i, e)
            i = MAX_TILES // RING - 1
            e = experts(i, "end")
            for u in range(RING):
                tile_step(RING * i + u, u, i, e)
            e_last = pe.value_load(texpi[0:1, MAX_TILES - 1:MAX_TILES], min_val=0, max_val=E - 1)
            down(MAX_TILES - 1, RING - 1, e_last, False)


_INS = ['L0_attn_x', 'L0_attn_A_log', 'L0_attn_B_param', 'L0_attn_C_param', 'L0_attn_log_dt', 'L0_attn_in_w',
        'L0_attn_in_b', 'L0_attn_out_w', 'L0_attn_out_b', 'L0_attn_ln_g', 'L0_attn_ln_b', 'L0_ffn_W_proj',
        'L0_ffn_b_proj', 'L0_ffn_W_gate', 'L0_ffn_W1', 'L0_ffn_b1', 'L0_ffn_ln1_g', 'L0_ffn_ln1_b', 'L0_ffn_W2',
        'L0_ffn_b2', 'L0_ffn_ln_g', 'L0_ffn_ln_b', 'L0_c', 'L0_wmod']
_OUTS = [((4, 1024, 128), 'float32')]


def kernel(**inputs):
    import numpy as _np
    import concourse.bacc as _bacc
    from concourse import mybir as _mybir
    from concourse.bass_utils import run_bass_kernel_spmd as _run

    nc = _bacc.Bacc("TRN2", target_bir_lowering=False, num_devices=1)
    arrays, args = {}, []
    for name in _INS:
        a = _np.ascontiguousarray(inputs[name])
        arrays[f"in_{name}_dram"] = a
        args.append(nc.dram_tensor(f"in_{name}_dram", a.shape, _mybir.dt.from_np(a.dtype), kind="ExternalInput").ap())
    for i, (shape, dtype) in enumerate(_OUTS):
        dt = _mybir.dt.from_np(_np.dtype(dtype))
        args.append(nc.dram_tensor(f"out_{i}_dram", shape, dt, kind="ExternalOutput").ap())
    adaln_program(nc, *args)
    r = _run(nc, [arrays], core_ids=[0])
    got = tuple(r.results[0][f"out_{i}_dram"] for i in range(len(_OUTS)))
    return got[0]
```

```python
import concourse.bass as bass
from concourse import mybir
from contextlib import ExitStack

FP32 = mybir.dt.float32
BF16 = mybir.dt.bfloat16
I32 = mybir.dt.int32
ALU = mybir.AluOpType
ACT = mybir.ActivationFunctionType
AX = mybir.AxisListType

P = 128
B, L, D = 4, 1024, 128
NS = 16
IC = L // P
NT = B * IC
HT = IC // 2
N = B * L
E, H = 8, 512
KC = H // P
CAPACITY = int(2.0 * N / E)
MAX_TILES = N // P + E - 1
QD = 32
JQ = P // QD
LN_EPS = 1e-5
LOG_LO = -18.420680743952367
PJ = D + E
HALVES = (slice(0, NT // 2), slice(NT // 2, NT))
OHC = 8
POOL_UNITS = (1, 4)
RANGES = ((0, 24), (24, 8))
LAG = 4
DVE_NORMS = 2
SPARE_BANK_UNITS = (5, 7)
RING = 3
AHEAD = 5
TRING = 6
INSIDE = (3, 4, 5, 2, 0, 1, 6, 7)
SLOT = {k: INSIDE[k - TRING] if k >= TRING else k for k in INSIDE}


class Steps:

    def __init__(self, eng, sem):
        self.eng, self.sem, self.base, self.n = eng, sem, 0, 0

    def mark(self, ins):
        ins.then_inc(self.sem, 1)
        self.n += 1
        return self.now()

    def now(self):
        return self.base + self.n

    def settle(self, upto=None):
        self.eng.wait_ge(self.sem, self.now() if upto is None else upto)

    def enter(self, i, per):
        self.start, self.per = self.base + self.n, per
        self.base, self.n = self.start + i * per, 0

    def leave(self, rounds):
        assert self.n == self.per, (self.n, self.per)
        self.base, self.n = self.start + rounds * self.per, 0


def adaln_program(nc, x, A_log, B_param, C_param, log_dt, in_w, in_b, out_w, out_b, ln_g, ln_b,
                  W_proj, b_proj, W_gate, W1, b1, ln1_g, ln1_b, W2, b2, f_ln_g, f_ln_b, c, wmod, out):
    k_pad = nc.dram_tensor("k_pad", [D, 2 * P], FP32, kind="Internal").ap()
    la_rows = nc.dram_tensor("la_rows", [D, NS], FP32, kind="Internal").ap()
    xf_rows = nc.dram_tensor("xf_rows", [N, D], FP32, kind="Internal").ap()
    y_rows = nc.dram_tensor("y_rows", [N, D], FP32, kind="Internal").ap()

    ctx = ExitStack()
    with ctx:
        def sb(name, shape, dt=FP32):
            return ctx.enter_context(nc.sbuf_tensor(name, shape, dt))

        def sem(name):
            return ctx.enter_context(nc.semaphore(name))

        X = sb("X", [P, B, IC, D])
        Hh = sb("Hh", [P, B, IC, D])
        U = sb("U", [P, IC, B, D])
        Z = sb("Z", [P, IC, B, D])
        BIG = sb("BIG", [P, TRING * 4 * JQ * P])
        T = BIG[:, :].rearrange("p (s g j r) -> p s g j r", s=TRING, g=4, j=JQ)
        W1s = BIG[:, 0:E * H].rearrange("p (e h) -> p e h", e=E)
        W2s = BIG[:, E * H:2 * E * H].rearrange("p (e k d) -> p e k d", e=E, k=KC)
        SBk = sb("SBk", [P, QD, JQ, IC * B])
        V = sb("V", [P, QD, P])
        Wst = sb("Wst", [P, (D + 1) * NS])
        XF = U[:, :, :, :].rearrange("p a b d -> p (a b) d")
        KN = BIG[:, 0:NS * P].rearrange("p (n l) -> p n l", n=NS)
        NR = sb("NR", [P, IC, D])
        NTt = sb("NTt", [P, IC, P])
        YT2 = V[:, 0:IC, :]
        YS = sb("YS", [P, 2, 4, P])
        St = sb("St", [P, IC, QD, B])
        Stmp = sb("Stmp", [P, QD, B])
        MOD = sb("MOD", [P, B, 4, D])
        GT = YS[:, 0]
        GT2 = YS[:, 1]
        GL = sb("GL", [P, B, D])
        GLB = sb("GLB", [P, B, D])
        lngb = sb("lngb", [P, 2, D])
        scT = sb("scT", [P, B])
        cT = sb("cT", [P, B])
        wm = St[:].rearrange("p i g b -> p (i g b)")[:, 0:6 * D].rearrange("p (m d) -> p m d", m=6)
        cbsT = sb("cbsT", [P, 2, B])
        AL = sb("AL", [P, NS])
        BP = sb("BP", [P, NS])
        CP = sb("CP", [P, NS])
        LD = sb("LD", [P, 1])
        EA = sb("EA", [P, NS])
        DT = sb("DT", [P, 1])
        LA32 = sb("LA32", [P, QD])
        CB32 = sb("CB32", [P, QD])
        LAT = sb("LAT", [P, QD])
        CBT = sb("CBT", [P, QD])
        AQ = sb("AQ", [P, QD])
        KP = sb("KP", [P, 2 * P])
        iota_d = sb("iota_d", [P, P])
        iota_d1 = sb("iota_d1", [P, P])
        left = sb("left", [P, 1])
        part = sb("part", [P, 1])
        ident = sb("ident", [P, P])
        lower = sb("lower", [P, P], BF16)
        onesb = sb("onesb", [P, P], BF16)
        ones3 = sb("ones3", [3, P], BF16)
        inw = NR[:, 1:3, :]
        outw = NR[:, 3, :]
        wpr = sb("wpr", [P, D])
        wgt = sb("wgt", [P, E])
        bpc = sb("bpc", [P, 1])
        lngc = sb("lngc", [P, 1])
        lnbc = sb("lnbc", [P, 1])
        inwT = sb("inwT", [P, 2 * D])
        inwG = sb("inwG", [P, 2 * D])
        outwT = sb("outwT", [P, D])
        wprT = NR[:, 0, :]
        WPG = sb("WPG", [P, PJ])
        WPB = sb("WPB", [P, B, PJ])
        row_in = sb("row_in", [3, 2 * D])
        row_out = sb("row_out", [3, D])
        row_pj = sb("row_pj", [3, PJ])
        row_pb = sb("row_pb", [3, B * PJ])
        part_in = sb("part_in", [3, 2 * D], BF16)
        part_out = sb("part_out", [3, D], BF16)
        part_pb = sb("part_pb", [3, B * PJ], BF16)
        below = sb("below", [3, 2])
        gb1 = sb("gb1", [QD, 2, P])
        gb1T = sb("gb1T", [P, 2, E, KC])
        b1n = sb("b1n", [QD, P])
        b1r = sb("b1r", [QD, P])
        b1p = sb("b1p", [QD, 3, P], BF16)
        b2n = sb("b2n", [E, P])
        b2r = sb("b2r", [E, P])
        b2p = sb("b2p", [E, 3, P], BF16)
        BR = BIG[0:3, 2 * E * H:2 * E * H + (E * H + E * D) // 2].bitcast(BF16)
        BR1 = BR[:, 0:E * H].rearrange("p (e h) -> p e h", e=E)
        BR2 = BR[:, E * H:E * (H + D)].rearrange("p (e d) -> p e d", e=E)
        st = sb("st", [P, 2, 2, HT, 6])
        mv = sb("mv", [P, 2, 2, HT, 2])
        ve = sb("ve", [P, 2, 2, HT])
        rs = sb("rs", [P, 2, 2, HT])
        nb = sb("nb", [P, 2, HT])
        tick = sb("tick", [P, 8])
        half = sb("half", [P, IC])
        flat_w = Wst[:, 0:D * NS]
        LG = flat_w[:, 0:NT * E].rearrange("p (t e) -> p t e", e=E)
        top = sb("top", [P, NT])
        flat_r = V[:, IC:IC + 12].rearrange("p g r -> p (g r)")
        RA = flat_r[:, 0:NT * E].rearrange("p (t e) -> p t e", e=E)

        def by_expert(slot, k):
            at = NT * E * (1 + slot) + RANGES[k][0] * E
            return flat_r[:, at:at + RANGES[k][1] * E].rearrange("p (e t) -> p e t", e=E)

        tot, inc, pos, sel = ([by_expert(slot, k) for k in range(2)] for slot in range(4))
        Mb = sb("Mb", [P, NT, E], BF16)
        erev = sb("erev", [P, E])
        k128 = sb("k128", [P, IC])
        seg = [sb(f"seg{k}", [P, E, n]) for k, (_, n) in enumerate(RANGES)]
        cmpk = flat_w[:, 1024:1024 + E * IC].rearrange("p (e i) -> p e i", e=E)
        nte = sb("nte", [P, E])
        tend = sb("tend", [P, E])
        tbeg = sb("tbeg", [P, E])
        one8 = sb("one8", [P, E])
        place, drop, tilf, begin = (V[:, IC + 15, NT * q:NT * q + NT] for q in range(4))
        placei = sb("placei", [P, NT], I32)
        rowi = sb("rowi", [P, NT], I32)
        tili = sb("tili", [P, NT], I32)
        rowb = sb("rowb", [P, NT], BF16)
        tilb = sb("tilb", [P, NT], BF16)
        iota_b = sb("iota_b", [P, P], BF16)
        giota_b = sb("giota_b", [P, MAX_TILES], BF16)
        tiota_b = sb("tiota_b", [P, NT], BF16)
        giota = sb("giota", [P, MAX_TILES])
        flat_s = SBk[:].rearrange("p g j m -> p (g j m)")
        OR = flat_s[:, 0:NT * P // 2].bitcast(BF16).rearrange("p (t r) -> p t r", t=NT)
        OT = flat_s[:, NT * P // 2:NT * P // 2 + NT * 3 * MAX_TILES // 2].bitcast(BF16).rearrange(
            "p (t c g) -> p t c g", t=NT, c=3)
        gcmp = V[:, IC + 12:IC + 15].rearrange("p g r -> p (g r)")[:, 0:E * MAX_TILES].rearrange("p (e g) -> p e g", e=E)
        texp = sb("texp", [P, MAX_TILES + 2 * RING])
        texpi = sb("texpi", [P, MAX_TILES], I32)
        texpr = sb("texpr", [P, MAX_TILES // RING, 12], I32)
        idf = flat_w[:, 640:640 + 3 * MAX_TILES].rearrange("p (c g) -> p c g", c=3)
        idg = flat_w[:, 768:768 + MAX_TILES]
        ids = flat_w[:, 896:896 + MAX_TILES]
        idgi = sb("idgi", [P, MAX_TILES], I32)
        idsi = sb("idsi", [P, MAX_TILES], I32)
        flat_v = V[:].rearrange("p g r -> p (g r)")
        NH = flat_v[:, 0:RING * H].rearrange("p (u h) -> p u h", u=RING)
        AT = flat_v[:, RING * H:2 * RING * H].rearrange("p (u k q) -> p u k q", u=RING, k=KC)
        XG = flat_v[:, 2 * RING * H:2 * RING * H + RING * D].rearrange("p (u d) -> p u d", u=RING)
        XT = flat_v[:, 2 * RING * H + RING * D:2 * RING * (H + D)].rearrange("p (u d) -> p u d", u=RING)
        FO = flat_w[:, NT * E:NT * E + RING * D].rearrange("p (u d) -> p u d", u=RING)
        st1 = sb("st1", [P, RING, 2, 6])
        mv1 = sb("mv1", [P, RING, 2, 2])
        rs1 = sb("rs1", [P, RING, 2])
        ve1 = sb("ve1", [P, RING, 2])

        PS = ctx.enter_context(nc.psum_tensor("PS", [P, 8, 512], FP32))

        s_x = sem("x_loaded")
        s_ssm = sem("decay_params_loaded")
        s_bcp = sem("coefficients_loaded")
        s_c = sem("c_loaded")
        s_wm = sem("wmod_loaded")
        s_w0 = sem("in_weights_loaded")
        s_w = sem("mixer_weights_loaded")
        s_e = sem("expert_vectors_loaded")
        s_bc = sem("final_norm_rows_loaded")
        s_iota = sem("iotas_ready")
        s_id = sem("identity_ready")
        s_one = sem("ones_ready")
        s_silu = sem("silu_c_ready")
        s_ea = sem("decay_exps_ready")
        s_la = sem("log_decay_ready")
        s_ke = sem("kernel_exps_ready")
        s_kp = sem("kernel_ready")
        s_kd = sem("kernel_in_dram")
        s_ld = sem("log_decay_in_dram")
        s_lb = sem("log_decay_broadcast")
        s_wst = sem("state_input_weights_ready")
        s_vl = sem("state_output_exponents_ready")
        s_v = sem("state_output_weights_ready")
        s_aq = sem("chunk_decay_ready")
        s_sbz = sem("block_states_zeroed")
        s_t = [sem(f"toeplitz_loaded{k}") for k in range(8)]
        s_ptr = sem("setup_transposed")
        s_etr = sem("setup_transposes_copied")
        s_mod = sem("modulation_products")
        s_me = sem("modulation_copied")
        s_inw = sem("in_weights_ready")
        s_r1 = sem("in_bias_product")
        s_r1e = sem("in_bias_ready")
        s_wge = sem("router_weight_copied")
        s_r2 = sem("projection_bias_products")
        s_r2e = sem("projection_weights_ready")
        s_gl = sem("final_gates_ready")
        s_b3 = sem("bias_parts_ready")
        s_br = sem("bias_parts_in_rows")
        s_x0 = sem("first_batch_row_loaded")
        s_vx = sem("input_variances_ready")
        s_rx = sem("input_rstds_ready")
        s_vh = sem("modulated_variances_ready")
        s_rh = sem("modulated_rstds_ready")
        s_nb = sem("norm_shifts_ready")
        s_var1 = sem("hidden_variance_ready")
        s_rsd1 = sem("hidden_rstd_ready")
        s_n = sem("norm_rows_ready")
        s_tp = sem("rows_transposed")
        s_nt = sem("transposes_copied")
        s_uz = sem("in_products")
        s_uze = sem("in_products_used")
        s_sin = sem("chunk_inputs")
        s_st = sem("chunk_states_ready")
        s_sbd = [sem(f"block_states_ready{c2}") for c2 in range(2)]
        s_in = sem("conv_inside_done")
        s_y = sem("conv_bank_done")
        s_ys = sem("conv_bank_copied")
        s_yt = sem("conv_bank_transposed")
        s_yz = sem("gated_bank_ready")
        s_tp2 = sem("gated_rows_transposed")
        s_nt2 = sem("gated_transposes_copied")
        s_op = sem("out_products")
        s_tp3 = sem("norm2_rows_transposed")
        s_nt3 = sem("norm2_transposes_copied")
        s_pj = sem("projections")
        s_pje = sem("projections_copied")
        s_xf = sem("projected_rows_in_dram")
        s_w12 = sem("expert_weights_loaded")
        s_yzr = sem("expert_rows_zeroed")
        s_m = sem("assignment_ready")
        s_cnt = sem("counts_ready")
        s_row = sem("rows_ready")
        s_ott = sem("tile_onehots_by_tile")
        s_ot = sem("tile_onehots_ready")
        s_otp = sem("tile_onehots_by_row")
        s_oh = sem("slot_onehots_ready")
        s_ids = sem("slot_tokens")
        s_idx = sem("row_numbers_ready")
        s_te = sem("tile_experts_ready")
        s_g = [sem(f"rows_gathered{u}") for u in range(RING)]
        s_xp = sem("gathered_transposed")
        s_xt = sem("gathered_transpose_copied")
        s_h = sem("hidden_ready")
        s_nh = sem("hidden_normed")
        s_hp = sem("hidden_transposed")
        s_a = sem("gelu_ready")
        s_o = sem("expert_out")
        s_f = sem("expert_rows_ready")
        s_sc = [sem(f"rows_scattered{u}") for u in range(RING)]
        s_x1 = sem("x1_ready")
        s_nl = sem("last_x1_rows_normed")
        s_cl = sem("mixer_rows_clipped")
        s_gt = sem("mixer_rows_gated")
        s_x1b = sem("x1_shifted")
        s_yl = [sem(f"expert_rows_loaded{q}") for q in range(2 * B)]
        s_fm = sem("pool_final_product")
        s_res = [sem(f"result_ready{q}") for q in range(2 * B)]
        s_out = sem("result_stored")
        s_dve = sem("dve_steps")
        s_pool = sem("pool_steps")

        def pb_product(b):
            return PS[0:3, 0, 0:PJ] if b == B - 1 else PS[0:3, 1, 64 + b * PJ:64 + b * PJ + PJ]

        def proj_banks(q):
            at = 2 if q in SPARE_BANK_UNITS else 6
            return PS[:, at:at + 2, :]

        def final_rows(q):
            return U[:, q]

        def bc(ap, shape):
            return ap.to_broadcast(shape)

        def row_onehots(c):
            return nc.vector.tensor_tensor(OR[:, OHC * c:OHC * c + OHC], bc(iota_b[:].unsqueeze(1), [P, OHC, P]),
                                     bc(rowb[:, OHC * c:OHC * c + OHC].unsqueeze(2), [P, OHC, P]), ALU.is_equal)

        block = ctx.enter_context(nc.Block())

        @block.sync
        def _(sp):
            with nc.allow_non_contiguous_dma("small vectors"):
                for dst, src in ((AL[:], A_log), (LD[:], log_dt.rearrange("(d a) -> d a", a=1))):
                    sp.dma_start(dst, src).then_inc(s_ssm, 16)
                sp.dma_start(X[:, 0], x[0].rearrange("(i p) d -> p i d", p=P)).then_inc(s_x0, 16)
                for dst, src in ((BP[:], B_param), (CP[:], C_param)):
                    sp.dma_start(dst, src).then_inc(s_bcp, 16)
                for b in range(1, B):
                    sp.dma_start(X[:, b], x[b].rearrange("(i p) d -> p i d", p=P)).then_inc(s_x, 16)
                for dst, src in ((outw, out_w), (wpr[:], W_proj), (wgt[:], W_gate),
                                 (bpc[:], b_proj.rearrange("(d a) -> d a", a=1)),
                                 (lngc[:], ln_g.rearrange("(d a) -> d a", a=1)),
                                 (lnbc[:], ln_b.rearrange("(d a) -> d a", a=1)),
                                 (row_in[:], bass.AP(tensor=in_b.tensor, offset=0, ap=[[0, 3], [1, 2 * D]])),
                                 (row_out[:], bass.AP(tensor=out_b.tensor, offset=0, ap=[[0, 3], [1, D]])),
                                 (row_pj[:, 0:D], bass.AP(tensor=b_proj.tensor, offset=0, ap=[[0, 3], [1, D]]))):
                    sp.dma_start(dst, src).then_inc(s_w, 16)
            sp.wait_ge(s_la, 1)
            sp.dma_start(la_rows, LA32[:, 0:NS]).then_inc(s_ld, 16)
            sp.wait_ge(s_ld, 16)
            sp.dma_start(Wst[:, 0:D * NS],
                         bass.AP(tensor=la_rows.tensor, offset=0, ap=[[0, P], [1, D * NS]])).then_inc(s_lb, 16)
            sp.wait_ge(s_kp, 1)
            sp.dma_start(k_pad, KP[:]).then_inc(s_kd, 16)
            for dst, src in ((gb1[:, 0, :], ln1_g.rearrange("e (k p) -> (e k) p", p=P)),
                             (gb1[:, 1, :], ln1_b.rearrange("e (k p) -> (e k) p", p=P)),
                             (b1n[:], b1.rearrange("e (k p) -> (e k) p", p=P)), (b2n[:], b2)):
                sp.dma_start(dst, src).then_inc(s_e, 16)
            for m, src in enumerate((f_ln_g, f_ln_b)):
                sp.dma_start(lngb[:, m, :], bass.AP(tensor=src.tensor, offset=0, ap=[[0, P], [1, D]])
                             ).then_inc(s_bc, 16)
            def toeplitz(k):
                for j in range(JQ):
                    src = bass.AP(tensor=k_pad.tensor, offset=(QD * j + 4 * k) * 2 * P,
                                  ap=[[1, P], [2 * P, 4], [1, P]])
                    sp.dma_start(T[:, SLOT[k], :, j, :], src).then_inc(s_t[k], 16)

            sp.wait_ge(s_kd, 16)
            for k in INSIDE[:TRING]:
                toeplitz(k)
            sp.wait_ge(s_sbz, B)
            sp.dma_start(y_rows.rearrange("(p t) d -> p (t d)", p=P),
                         SBk[:].rearrange("p g j m -> p (g j m)")).then_inc(s_yzr, 16)
            for k in range(TRING, 8):
                sp.wait_ge(s_in, k - TRING + 1)
                toeplitz(k)
            sp.wait_ge(s_y, 8)
            sp.dma_start(W1s, W1.rearrange("e d h -> d e h")).then_inc(s_w12, 16)
            sp.dma_start(W2s, W2.rearrange("e (k q) d -> q e k d", q=P)).then_inc(s_w12, 16)
            sp.wait_ge(s_b3, 2)
            for q in range(3):
                sp.dma_start(BR1[q:q + 1].rearrange("p e h -> p (e h)"), b1p[:, q, :]).then_inc(s_br, 16)
                sp.dma_start(BR2[q:q + 1].rearrange("p e d -> p (e d)"), b2p[:, q, :]).then_inc(s_br, 16)
            for b in range(B):
                sp.wait_ge(s_pje, 2 * b + 2)
                sp.dma_start(xf_rows[b * L:(b + 1) * L].rearrange("(i p) d -> p i d", p=P),
                             XF[:, b * IC:(b + 1) * IC, :]).then_inc(s_xf, 16)
            for u in range(RING):
                sp.wait_ge(s_sc[u], 16 * (MAX_TILES // RING))
            for q in range(2 * B):
                sp.dma_start(final_rows(q), y_rows[q * HT * P:(q + 1) * HT * P].rearrange("(i p) d -> p i d", p=P)
                             ).then_inc(s_yl[q], 16)
            for q in range(2 * B):
                sp.wait_ge(s_res[q], 1)
                b, i = q // 2, HT * (q % 2)
                sp.dma_start(out[b, i * P:(i + HT) * P].rearrange("(i p) d -> p i d", p=P),
                             Hh[:, b, i:i + HT]).then_inc(s_out, 16)
            sp.wait_ge(s_out, 16 * 2 * B)

        @block.gpsimd
        def _(pool):
            g = nc.gpsimd
            step = Steps(pool, s_pool)
            def count_up(dst, n, base, per, channel):
                return g.iota(dst, pattern=[[per, n]], base=base, channel_multiplier=channel,
                              allow_small_or_imprecise_dtypes=True)

            step.mark(g.memset(ident[:], 0.0))
            step.mark(g.memset(onesb[:], 1.0))
            count_up(iota_d[:], P, P - 1, -1, 0)
            count_up(iota_d1[:], P, P, -1, 0)
            count_up(part[:], 1, 0, 0, 1)
            count_up(left[:], 1, P - 1, 0, -1).then_inc(s_iota, 1)
            step.settle()
            g.affine_select(out=ident[:], in_=ident[:], pattern=[[-1, P]], compare_op=ALU.not_equal, fill=1.0,
                            base=0, channel_multiplier=1).then_inc(s_id, 1)
            g.memset(half[:], -0.5)
            g.memset(Wst[:, D * NS:], 0.0)
            g.memset(ones3[:], 1.0).then_inc(s_one, 1)
            pool.wait_ge(s_iota, 1)
            pool.wait_ge(s_one, 1)
            pool.wait_ge(s_la, 2)

            def v_exponents(c):
                n = QD // 4
                g.tensor_tensor(V[:, c * n:c * n + n, :], bc(iota_d1[:].unsqueeze(1), [P, n, P]),
                                bc(LAT[:, c * n:c * n + n].unsqueeze(2), [P, n, P]), ALU.mult).then_inc(s_vl, 1)

            def rstd(w, h, ready, done, count):
                pool.wait_ge(ready, count)
                g.tensor_tensor(rs[:, w, h, :], ve[:, w, h, :], half[:, 0:HT], ALU.pow).then_inc(done, 1)

            def zero_states(q):
                n = QD // B
                g.memset(SBk[:, n * q:n * q + n].rearrange("p g j m -> p (g j m)"), 0.0).then_inc(s_sbz, 1)

            v_exponents(0)
            rstd(0, 0, s_vx, s_rx, 1)
            v_exponents(1)
            v_exponents(2)
            rstd(0, 1, s_vx, s_rx, 2)
            v_exponents(3)

            def norm_step(q, h, clear):
                if clear:
                    pool.wait_ge(s_n, q - 2)
                rstd(1, 1 - h, s_vh, s_rh, q)
                rstd(0, 1 - h, s_vx, s_rx, q + 2)
                if q <= 2:
                    half_n = slice(8 * (q - 1), 8 * q)
                    step.mark(g.tensor_tensor(KN[:, half_n], KN[:, half_n],
                                              bc(CB32[:, half_n].unsqueeze(2), [P, 8, P]), ALU.mult))
                elif q <= 4:
                    for n in (8,) if q == 3 else (4, 2):
                        step.settle()
                        step.mark(g.tensor_tensor(KN[:, 0:n], KN[:, 0:n], KN[:, n:2 * n], ALU.add))
                    if q == 4:
                        step.settle()
                        g.tensor_tensor(KP[:, 0:P], KN[:, 0], KN[:, 1], ALU.add).then_inc(s_kp, 1)
                else:
                    zero_states(q - 5)

            pool.wait_ge(s_ke, 1)
            for q in range(1, 2 * B - 1):
                norm_step(q, q % 2, q > 2)
            pool.wait_ge(s_n, 5)
            rstd(1, 0, s_vh, s_rh, 2 * B - 1)
            zero_states(2)
            pool.wait_ge(s_n, 6)
            rstd(1, 1, s_vh, s_rh, 2 * B)
            zero_states(3)
            count_up(iota_b[:], P, 0, 1, 0)
            count_up(giota_b[:], MAX_TILES, 0, 1, 0)
            count_up(tiota_b[:], NT, 0, 1, 0)
            count_up(erev[:], E, E, -1, 0)
            count_up(k128[:], IC, 0, P, 0)
            count_up(giota[:], MAX_TILES, 0, 1, 0)
            g.memset(one8[:], 1.0)
            for k in range(2):
                step.mark(g.memset(seg[k][:], 1.0))
            step.settle()
            for k in range(2):
                g.memset(seg[k][:, :, 0:1], 0.0)
            g.affine_select(out=lower[:], in_=onesb[:], pattern=[[1, P]], compare_op=ALU.is_gt, fill=0.0,
                            base=0, channel_multiplier=-1).then_inc(s_one, 1)
            pool.wait_ge(s_gl, 1)
            for q in range(2 * B + 1):
                if q < 2 * B:
                    pool.wait_ge(s_cl, q + 1)
                    hb = Hh[:, q // 2, HT * (q % 2):HT * (q % 2) + HT]
                    g.tensor_tensor(hb, hb, bc(MOD[:, q // 2, 2:3, :], [P, HT, D]), ALU.mult).then_inc(s_gt, 1)
                if q:
                    pool.wait_ge(s_n, 2 * B + q - 2)
                    rstd(1, (q - 1) % 2, s_vh, s_rh, 2 * B + q)
            pool.wait_ge(s_gl, 1)
            pool.wait_ge(s_x1, 2 * B)
            for b in range(B):
                g.tensor_tensor(Hh[:, b], X[:, b], bc(GLB[:, b:b + 1, :], [P, IC, D]), ALU.add).then_inc(s_x1b, 1)
            for n, half_t in enumerate(HALVES):
                pool.wait_ge(s_ot, n + 1)
                g.tensor_tensor(OT[:, half_t, 1, :], OT[:, half_t, 0, :],
                                bc(tiota_b[:, half_t].unsqueeze(2), [P, NT // 2, MAX_TILES]),
                                ALU.mult).then_inc(s_ott, 1)
            pool.wait_ge(s_idx, 1)
            pool.wait_ge(s_xf, 16 * B)
            pool.wait_ge(s_yzr, 16)

            def gather(t):
                u = t % RING
                if t >= RING:
                    pool.wait_ge(s_xp, t - RING + 1)
                pool.indirect_dma_start(out=XG[:, u, :], out_offset=None, in_=xf_rows,
                                        in_offset=bass.IndirectOffsetOnAxis(ap=idgi[:, t:t + 1], axis=0),
                                        bounds_check=N - 1, oob_is_err=False).then_inc(s_g[u], 16)

            def scatter(t):
                pool.wait_ge(s_f, t + 1)
                pool.indirect_dma_start(out=y_rows, out_offset=bass.IndirectOffsetOnAxis(ap=idsi[:, t:t + 1], axis=0),
                                        in_=FO[:, t % RING, :], in_offset=None,
                                        bounds_check=N - 1, oob_is_err=False).then_inc(s_sc[t % RING], 16)

            for t in range(AHEAD):
                gather(t)
            for t in range(MAX_TILES + RING + 1):
                if t < MAX_TILES + RING:
                    pool.wait_ge(s_var1, t + 1)
                    g.tensor_tensor(rs1[:, t % RING, :], ve1[:, t % RING, :], half[:, 0:2],
                                    ALU.pow).then_inc(s_rsd1, 1)
                if t + AHEAD < MAX_TILES:
                    gather(t + AHEAD)
                if t > RING:
                    scatter(t - RING - 1)
            for n, q in enumerate(POOL_UNITS):
                pool.wait_ge(s_yl[q], 16)
                yb = final_rows(q)
                g.tensor_tensor(yb, yb, bc(GL[:, q // 2:q // 2 + 1, :], [P, HT, D]), ALU.mult).then_inc(s_fm, 1)
                pool.wait_ge(s_fm, n + 1)
                hb = Hh[:, q // 2, HT * (q % 2):HT * (q % 2) + HT]
                g.tensor_tensor(hb, hb, yb, ALU.add).then_inc(s_res[q], 1)

        @block.scalar
        def _(act):
            a = nc.scalar
            with nc.allow_non_contiguous_dma("c transposed"):
                act.dma_start(cT[:], c.rearrange("b d -> d b")).then_inc(s_c, 16)
            act.dma_start(wm, wmod.rearrange("k (m d) -> k m d", m=6)).then_inc(s_wm, 16)
            act.dma_start(inw, in_w.rearrange("(a p) d -> p a d", p=P)).then_inc(s_w0, 16)
            act.wait_ge(s_ssm, 32)
            a.activation(EA[:], AL[:], ACT.Exp)
            a.activation(DT[:], LD[:], ACT.Exp).then_inc(s_ea, 1)
            act.wait_ge(s_c, 16)
            a.activation(scT[:], cT[:], ACT.Silu).then_inc(s_silu, 1)
            for b in range(B):
                act.wait_ge(s_mod, b + 1)
                for m, one in ((0, 0.0), (1, 1.0), (2, 0.0)):
                    last = a.activation(MOD[:, b, m, :], PS[:, 2 + b, m * D:m * D + D], ACT.Copy, bias=one)
                last.then_inc(s_me, 1)
            act.wait_ge(s_ptr, 1)
            a.copy(inwT[:], PS[:, 0, 0:2 * D])
            a.copy(outwT[:], PS[:, 0, 2 * D:3 * D])
            a.copy(wprT, PS[:, 0, 3 * D:4 * D]).then_inc(s_etr, 1)
            act.wait_ge(s_la, 2)
            act.wait_ge(s_iota, 1)
            for n in range(NS):
                last = a.activation(KN[:, n], iota_d[:], ACT.Exp, scale=LA32[:, n:n + 1])
            last.then_inc(s_ke, 1)
            act.wait_ge(s_mod, B + 1)
            a.copy(MOD[:, :, 3, :], PS[:, 6, :].rearrange("p (b d) -> p b d", b=B)).then_inc(s_me, 1)
            a.activation(AQ[:], LAT[:], ACT.Exp, scale=float(P)).then_inc(s_aq, 1)
            act.wait_ge(s_lb, 16)
            a.activation(Wst[:, 0:D * NS], Wst[:, 0:D * NS], ACT.Exp,
                         scale=left[:, 0:1]).then_inc(s_wst, 1)

            def tiles(buf, b, h):
                return buf[:, bass.ds(b, 1), HT * h:HT * h + HT, :].rearrange("p a i d -> p (a i) d")

            def normed(src, b, h, before, turned, clear):
                q = 2 * b + h
                act.wait_ge(s_nb, before + q + 1)
                if clear:
                    act.wait_ge(turned, q - 1)
                for i in range(HT):
                    last = a.activation(NR[:, HT * h + i, :], tiles(src, b, h)[:, i, :], ACT.Identity,
                                        bias=nb[:, h, i:i + 1], scale=rs[:, 1, h, i:i + 1])
                last.then_inc(s_n, 1)

            def turned(b, h):
                act.wait_ge(s_tp, 2 * b + h + 1)
                a.copy(NTt[:, HT * h:HT * h + HT, :], PS[:, h, :]).then_inc(s_nt, 1)

            def split_uz(b, h):
                act.wait_ge(s_uz, 2 * b + h + 1)
                src = PS[:, 2 + 2 * h:4 + 2 * h, :].rearrange("p k (a c) -> p (k a) c", a=2)
                a.copy(U[:, HT * h:HT * h + HT, bass.ds(b, 1), :].rearrange("p i a d -> p (i a) d"), src[:, :, 0:D])
                a.activation(Z[:, HT * h:HT * h + HT, bass.ds(b, 1), :].rearrange("p i a d -> p (i a) d"),
                             src[:, :, D:2 * D], ACT.Silu).then_inc(s_uze, 1)

            act.wait_ge(s_r1, 1)
            normed(Hh, 0, 0, 0, s_tp, False)
            turned(0, 0)
            normed(Hh, 0, 1, 0, s_tp, False)
            split_uz(0, 0)
            turned(0, 1)
            with nc.scalar.Fori(1, B) as b:
                normed(Hh, b, 0, 0, s_tp, True)
                split_uz(b - 1, 1)
                turned(b, 0)
                normed(Hh, b, 1, 0, s_tp, True)
                split_uz(b, 0)
                turned(b, 1)
            split_uz(B - 1, 1)
            act.wait_ge(s_ptr, 2)
            a.copy(gb1T[:].rearrange("p m e k -> p (m e k)"), PS[:, 2, 0:2 * QD]).then_inc(s_etr, 1)
            act.wait_ge(s_vl, 4)
            a.activation(V[:], V[:], ACT.Exp).then_inc(s_v, 1)
            act.wait_ge(s_yzr, 16)
            def block_states(c2):
                act.wait_ge(s_st, c2 + 1)
                half_g = slice(16 * c2, 16 * c2 + 16)
                for j in (2, 3):
                    a.copy(SBk[QD * j:QD * j + QD, half_g, j, :].rearrange("p g (i b) -> p i g b", b=B),
                           St[QD * j:QD * j + QD, :, half_g]).then_inc(s_sbd[c2], 1)

            block_states(0)
            for k in range(8):
                act.wait_ge(s_y, k + 1)
                if k >= 2:
                    act.wait_ge(s_yt, k - 1)
                dst = YS[:, k % 2, :, P - 1:P]
                dst = bass.AP(tensor=dst.tensor, offset=dst.offset, ap=[*dst.ap[:-1], [-1, P]])
                a.copy(dst, PS[:, k, :].rearrange("p (g q) -> p g q", g=4)).then_inc(s_ys, 1)
                if k == 1:
                    block_states(1)

            def gated(q):
                h = q % 2
                act.wait_ge(s_tp2, q + 1)
                if q >= 2:
                    act.wait_ge(s_op, q - 1)
                a.copy(YT2[:, HT * h:HT * h + HT, :], PS[:, h, :]).then_inc(s_nt2, 1)

            def projected(q):
                act.wait_ge(s_pj, q + 1)
                src = proj_banks(q).rearrange("p k (a c) -> p (k a) c", a=2)
                a.copy(XF[:, HT * q:HT * q + HT, :], src[:, :, 0:D])
                a.copy(LG[:, HT * q:HT * q + HT, :], src[:, :, D:PJ]).then_inc(s_pje, 1)

            def turned2(q):
                h = q % 2
                act.wait_ge(s_tp3, q + 1)
                a.copy(NTt[:, HT * h:HT * h + HT, :], PS[:, 4 + h, :]).then_inc(s_nt3, 1)

            gated(0)
            for q in range(2 * B + LAG + 1):
                n = q - LAG
                if q + 1 < 2 * B:
                    gated(q + 1)
                if 0 <= n < 2 * B - DVE_NORMS:
                    normed(X, n // 2, n % 2, 2 * B, s_tp3, n >= 2)
                early = 2 * B - DVE_NORMS <= n < 2 * B
                if early:
                    turned2(n)
                if n >= 1:
                    projected(n - 1)
                if 0 <= n < 2 * B and not early:
                    turned2(n)

            for n, half_t in enumerate(HALVES):
                act.wait_ge(s_ot, n + 1)
                a.activation(OT[:, half_t, 2, :], OT[:, half_t, 0, :], ACT.Identity,
                             scale=part[:, 0:1]).then_inc(s_otp, 1)

            def copy_xt(t, u, first):
                act.wait_ge(s_xp, t + 1)
                if not first:
                    act.wait_ge(s_h, t - RING + 1)
                a.copy(XT[:, u, :], PS[:, 4, 0:P]).then_inc(s_xt, 1)

            def gelu(t, u, first):
                e = act.value_load(texpi[0:1, bass.ds(t, 1)], min_val=0, max_val=E - 1)
                act.wait_ge(s_hp, t + 1)
                if not first:
                    act.wait_ge(s_o, t - RING + 1)
                for k in range(KC):
                    a.activation(AT[:, u, k, :], PS[:, 3, P * k:P * k + P], ACT.Gelu,
                                 bias=gb1T[:, 1, bass.ds(e, 1), k],
                                 scale=gb1T[:, 0, bass.ds(e, 1), k]).then_inc(s_a, 1)

            act.wait_ge(s_te, 1)
            for u in range(RING):
                copy_xt(u, u, True)
            for u in range(RING):
                copy_xt(RING + u, u, False)
                gelu(u, u, True)
            with nc.scalar.Fori(1, MAX_TILES // RING - 1) as i:
                for u in range(RING):
                    copy_xt(RING * i + u + RING, u, False)
                    gelu(RING * i + u, u, False)
            for t in range(MAX_TILES - RING, MAX_TILES):
                gelu(t, t % RING, False)

        @block.vector
        def _(dve):
            v = nc.vector
            step = Steps(dve, s_dve)
            v.memset(LA32[:], 0.0)
            v.memset(CB32[:], 0.0)
            step.mark(v.memset(KP[:, P:2 * P], 0.0))
            dve.wait_ge(s_ssm, 32)
            dve.wait_ge(s_ea, 1)
            step.mark(v.tensor_scalar(DT[:], DT[:], 1e-4, 1.0, ALU.max, ALU.min))
            step.settle()
            step.mark(v.tensor_scalar(EA[:], EA[:], DT[:, 0:1], -1.0, ALU.mult, ALU.mult))
            step.settle()
            v.tensor_scalar(LA32[:, 0:NS], EA[:], LOG_LO, 0.0, ALU.max, ALU.min).then_inc(s_la, 1)
            dve.wait_ge(s_bcp, 32)
            step.mark(v.tensor_scalar(CP[:], CP[:], DT[:, 0:1], None, ALU.mult))
            step.settle()
            step.mark(v.tensor_tensor(CB32[:, 0:NS], CP[:], BP[:], ALU.mult))
            dve.wait_ge(s_la, 1)
            step.settle()
            step.mark(v.transpose(CBT[:], CB32[:]))
            v.transpose(LAT[:], LA32[:]).then_inc(s_la, 1)
            dve.wait_ge(s_iota, 1)

            def tiles(buf, b, h):
                return buf[:, bass.ds(b, 1), HT * h:HT * h + HT, :].rearrange("p a i d -> p (a i) d")

            def row_stats(src, w, h):
                c = 4 * w + 2 * h
                v.memset(tick[:, c:c + 1], 0.0)
                for i in range(HT):
                    last = v.bn_stats(st[:, w, h, i, :], src[:, i, :])
                return last

            def row_means(w, h):
                c = 4 * w + 2 * h + 1
                v.memset(tick[:, c:c + 1], 0.0)
                for i in range(HT):
                    last = v.bn_aggr(mv[:, w, h, i, :], st[:, w, h, i, :])
                return last

            def row_vars(w, h):
                return v.tensor_scalar(ve[:, w, h, :], mv[:, w, h, :, 1], LN_EPS, None, ALU.add)

            def shifts(h):
                return v.scalar_tensor_tensor(nb[:, h, :], mv[:, 1, h, :, 0], -1.0, rs[:, 1, h, :],
                                              ALU.mult, ALU.mult)

            def modulate(b, h, first=False, last=False):
                q, o = 2 * b + h, 1 - h
                before = step.now()
                if not last:
                    sums_x = step.mark(row_stats(tiles(X, b + h, o), 0, o))
                if not first:
                    step.settle(before)
                    means_h = step.mark(row_means(1, o))
                if first:
                    dve.wait_ge(s_me, 1)
                src, dst = tiles(X, b, h), tiles(Hh, b, h)
                ca1, sa = (MOD[:, bass.ds(b, 1), m, :].rearrange("p a d -> p (a d)") for m in (1, 0))
                for i in range(HT):
                    ins = v.scalar_tensor_tensor(dst[:, i, :], src[:, i, :], mv[:, 0, h, i, 0:1], ca1,
                                                 ALU.subtract, ALU.mult)
                scaled = step.mark(ins)
                if not first:
                    step.settle(means_h)
                    row_vars(1, o).then_inc(s_vh, 1)
                if not last:
                    step.settle(sums_x)
                    means_x = step.mark(row_means(0, o))
                dve.wait_ge(s_rx, q + 1)
                step.settle(scaled)
                for i in range(HT):
                    ins = v.scalar_tensor_tensor(dst[:, i, :], dst[:, i, :], rs[:, 0, h, i:i + 1], sa,
                                                 ALU.mult, ALU.add)
                shifted = step.mark(ins)
                if not last:
                    step.settle(means_x)
                    row_vars(0, o).then_inc(s_vx, 1)
                if not first:
                    dve.wait_ge(s_rh, q)
                    shifts(o).then_inc(s_nb, 1)
                step.settle(shifted)
                step.mark(row_stats(dst, 1, h))

            def three_parts(row, part_row, tmp):
                for m in range(2):
                    step.mark(v.tensor_copy(tmp, row))
                    step.settle()
                    step.mark(v.scalar_tensor_tensor(row, tmp, below[:, m:m + 1], row, ALU.mult, ALU.add))
                    step.settle()
                return v.tensor_copy(part_row, row)

            dve.wait_ge(s_x0, 16)
            step.mark(row_stats(tiles(X, 0, 0), 0, 0))
            for m in range(2):
                v.tensor_scalar(below[:, m:m + 1], part[0:3], m + 0.5, -1.0, ALU.is_ge, ALU.mult)
            step.settle()
            step.mark(row_means(0, 0))
            step.settle()
            row_vars(0, 0).then_inc(s_vx, 1)
            modulate(0, 0, first=True)
            dve.wait_ge(s_w, 144)
            dve.wait_ge(s_etr, 1)
            v.tensor_scalar(inwG[:], inwT[:], lngc[:, 0:1], None, ALU.mult).then_inc(s_inw, 1)
            dve.wait_ge(s_r1, 1)
            step.mark(v.tensor_tensor(row_in[:], row_in[:], PS[0:3, 7, 0:2 * D], ALU.add))
            step.settle()
            three_parts(row_in[:], part_in[:], part_in[:]).then_inc(s_r1e, 1)
            dve.wait_ge(s_x, 16 * (B - 1))
            dve.wait_ge(s_me, B)
            with nc.vector.Fori(1, B) as b:
                step.enter(b - 1, 12)
                modulate(b - 1, 1)
                modulate(b, 0)
                step.leave(B - 1)
            modulate(B - 1, 1, last=True)
            step.settle()
            step.mark(row_means(1, 1))
            step.settle()
            row_vars(1, 1).then_inc(s_vh, 1)
            dve.wait_ge(s_rh, 2 * B)
            shifts(1).then_inc(s_nb, 1)

            step.mark(v.tensor_copy(cbsT[:, 0, :], PS[:, 7, 256:260]))
            step.mark(v.tensor_scalar(cbsT[:, 1, :], PS[:, 7, 260:264], 1.0, None, ALU.add))
            step.mark(v.tensor_copy(WPG[:, 0:D], wpr[:]))
            step.mark(v.tensor_copy(WPG[:, D:PJ], PS[:, 7, 264:272]))
            step.mark(v.tensor_copy(row_pj[:, D:PJ], PS[0:3, 7, 272:280]))
            step.settle()
            for b in range(B):
                last = v.tensor_scalar(WPB[:, b, :], WPG[:], cbsT[:, 1, b:b + 1], None, ALU.mult)
            last.then_inc(s_wge, 1)
            dve.wait_ge(s_me, B + 1)
            for m in (2, 3):
                step.mark(v.scalar_tensor_tensor(GT, MOD[:, :, m, :], -1.0, MOD[:, :, m, :], ALU.mult, ALU.max))
                step.mark(v.tensor_scalar(GT2, MOD[:, :, m, :], 0.0, 2.0, ALU.is_ge, ALU.mult))
                step.settle()
                step.mark(v.tensor_scalar(GT2, GT2, -1.0, None, ALU.add))
                step.mark(v.tensor_scalar(GT, GT, 0.25, None, ALU.max))
                step.settle()
                step.mark(v.tensor_tensor(MOD[:, :, m, :], GT, GT2, ALU.mult))
                step.settle()
            dve.wait_ge(s_bc, 32)
            v.tensor_tensor(GL[:], MOD[:, :, 3, :], bc(lngb[:, 0:1, :], [P, B, D]), ALU.mult)
            v.tensor_tensor(GLB[:], MOD[:, :, 3, :], bc(lngb[:, 1:2, :], [P, B, D]), ALU.mult).then_inc(s_gl, 1)
            dve.wait_ge(s_e, 64)
            for nat, rest, parts in ((b1n, b1r, b1p), (b2n, b2r, b2p)):
                step.mark(v.tensor_copy(parts[:, 0, :], nat[:]))
                step.settle()
                step.mark(v.tensor_tensor(rest[:], nat[:], parts[:, 0, :], ALU.subtract))
                step.settle()
                step.mark(v.tensor_copy(parts[:, 1, :], rest[:]))
                step.settle()
                step.mark(v.tensor_tensor(rest[:], rest[:], parts[:, 1, :], ALU.subtract))
                step.settle()
                v.tensor_copy(parts[:, 2, :], rest[:]).then_inc(s_b3, 1)
            dve.wait_ge(s_r2, 1)
            for b in range(B):
                last = v.tensor_tensor(row_pb[:, b * PJ:b * PJ + PJ], row_pj[:],
                                       pb_product(b), ALU.add)
            step.mark(last)
            step.settle()
            step.mark(three_parts(row_out[:], part_out[:], part_out[:]))
            three_parts(row_pb[:], part_pb[:], part_pb[:]).then_inc(s_r2e, 1)
            step.mark(v.memset(St[:, 0], 0.0))
            dve.wait_ge(s_aq, 1)
            for c2 in range(2):
                dve.wait_ge(s_sin, c2 + 1)
                half_g = slice(16 * c2, 16 * c2 + 16)
                sin = PS[:, 6 + c2, :].rearrange("p (g i b) -> p i g b", i=IC, b=B)
                S, decay, tmp = St[:, :, half_g], bc(AQ[:, half_g].unsqueeze(2), [P, 16, B]), Stmp[:, half_g]
                step.mark(v.tensor_copy(S[:, 1], sin[:, 0]))
                step.settle()
                for i in range(1, IC - 1):
                    step.mark(v.tensor_tensor(tmp, S[:, i], decay, ALU.mult))
                    step.settle()
                    step.mark(v.tensor_tensor(S[:, i + 1], tmp, sin[:, i], ALU.add))
                    step.settle()
                S = S.rearrange("p i g b -> p g i b")
                v.tensor_tensor(S, S, bc(CBT[:, half_g].unsqueeze(2).unsqueeze(3), [P, 16, IC, B]),
                                ALU.mult).then_inc(s_st, 1)
                dve.wait_ge(s_st, c2 + 1)
                if c2 == 0:
                    dve.wait_ge(s_yzr, 16)
                for j in (0, 1):
                    v.tensor_copy(SBk[QD * j:QD * j + QD, half_g, j, :].rearrange("p g (i b) -> p i g b", b=B),
                                  St[QD * j:QD * j + QD, :, half_g]).then_inc(s_sbd[c2], 1)
            for k in range(8):
                dve.wait_ge(s_yt, k + 1)
                zk = Z[:].rearrange("p i b (j g) -> p g j (i b)", g=QD)[:, 4 * k:4 * k + 4]
                src = PS[:, k, :].rearrange("p (g j m) -> p g j m", g=4, j=JQ)
                for g4 in range(4):
                    last = v.tensor_tensor(zk[:, g4], src[:, g4], zk[:, g4], ALU.mult)
                last.then_inc(s_yz, 1)

            def mixer_sum(b, h):
                dve.wait_ge(s_op, 2 * b + h + 1)
                hb = tiles(Hh, b, h)
                return step.mark(v.tensor_tensor(hb, PS[:, 2 + h, :].rearrange("p (i d) -> p i d", d=D), hb,
                                                 ALU.add))

            def mixer_clip(b, h, summed):
                step.settle(summed)
                hb = tiles(Hh, b, h)
                v.tensor_scalar(hb, hb, 10.0, -10.0, ALU.min, ALU.max).then_inc(s_cl, 1)

            def mixer_x1(b, h):
                dve.wait_ge(s_gt, 2 * b + h + 1)
                xb = tiles(X, b, h)
                v.tensor_tensor(xb, xb, tiles(Hh, b, h), ALU.add).then_inc(s_x1, 1)

            def normed_here(q):
                h = q % 2
                dve.wait_ge(s_rh, 2 * B + q + 1)
                dve.wait_ge(s_tp3, q - 1)
                for i in range(HT):
                    last = v.tensor_scalar(NR[:, HT * h + i, :], tiles(X, q // 2, h)[:, i, :],
                                           mv[:, 1, h, i, 0:1], rs[:, 1, h, i:i + 1], ALU.subtract, ALU.mult)
                last.then_inc(s_nl, 1)

            def x1_stats(b, h, earlier):
                q = 2 * b + h
                dve.wait_ge(s_x1, q + 1)
                sums = step.mark(row_stats(tiles(X, b, h), 1, h))
                if isinstance(b, int) and q - 1 >= 2 * B - DVE_NORMS:
                    normed_here(q - 1)
                elif earlier:
                    dve.wait_ge(s_rh, 2 * B + q)
                    shifts(1 - h).then_inc(s_nb, 1)
                step.settle(sums)
                step.settle(step.mark(row_means(1, h)))
                row_vars(1, h).then_inc(s_vh, 1)

            def mixer_step(b, h, b_before, earlier):
                summed = mixer_sum(b, h)
                mixer_x1(b_before, 1 - h)
                mixer_clip(b, h, summed)
                x1_stats(b_before, 1 - h, earlier)

            mixer_clip(0, 0, mixer_sum(0, 0))
            mixer_step(0, 1, 0, False)
            with nc.vector.Fori(1, B) as b:
                step.enter(b - 1, 6)
                mixer_step(b, 0, b - 1, True)
                mixer_step(b, 1, b, True)
                step.leave(B - 1)
            mixer_x1(B - 1, 1)
            x1_stats(B - 1, 1, True)
            normed_here(2 * B - 1)

            def assign(k):
                a, n = RANGES[k]
                rng, wide = slice(a, a + n), [P, n, E]
                dve.wait_ge(s_pje, (a + n) // HT)
                step.mark(v.tensor_reduce(top[:, rng], LG[:, rng], AX.X, ALU.max))
                step.settle()
                step.mark(v.tensor_tensor(RA[:, rng], LG[:, rng], bc(top[:, rng].unsqueeze(2), wide), ALU.is_equal))
                step.settle()
                step.mark(v.tensor_tensor(RA[:, rng], RA[:, rng], bc(erev[:].unsqueeze(1), wide), ALU.mult))
                step.settle()
                step.mark(v.tensor_reduce(top[:, rng], RA[:, rng], AX.X, ALU.max))
                step.settle()
                v.tensor_tensor(Mb[:, rng], bc(erev[:].unsqueeze(1), wide), bc(top[:, rng].unsqueeze(2), wide),
                                ALU.is_equal).then_inc(s_m, 1)

            def flat(ap):
                return ap.rearrange("p e t -> p (e t)")

            def running_counts(k):
                a, n = RANGES[k]
                dve.wait_ge(s_cnt, k + 1)
                totals = PS[:, 2 * k + 1, 0:n * E].rearrange("p (t e) -> p e t", e=E)
                step.mark(v.tensor_copy(tot[k], totals))
                step.settle()
                if k:
                    step.mark(v.tensor_tensor(tot[1][:, :, 0:1], tot[1][:, :, 0:1],
                                              inc[0][:, :, RANGES[0][1] - 1:RANGES[0][1]], ALU.add))
                    step.settle()
                step.mark(v.tensor_tensor_scan(flat(inc[k]), flat(seg[k][:]), flat(tot[k]), 0.0, ALU.mult, ALU.add))
                step.settle()

            def places(k):
                a, n = RANGES[k]
                rng = slice(a, a + n)
                totals, rank = (PS[:, 2 * k + q, 0:n * E].rearrange("p (t e) -> p e t", e=E) for q in (1, 0))
                step.mark(v.tensor_tensor(pos[k], inc[k], totals, ALU.subtract))
                step.settle()
                step.mark(v.tensor_tensor(pos[k], pos[k], rank, ALU.add))
                step.settle()
                step.mark(v.tensor_tensor(sel[k], pos[k], Mb[:, rng].rearrange("p t e -> p e t"), ALU.mult))
                step.settle()
                step.mark(v.tensor_reduce(place[:, rng], sel[k].rearrange("p e t -> p t e"), AX.X, ALU.add))
                step.settle()
                step.mark(v.tensor_copy(placei[:, rng], place[:, rng]))
                step.mark(v.tensor_scalar(drop[:, rng], place[:, rng], float(CAPACITY), float(2 * NT),
                                          ALU.is_ge, ALU.mult))
                step.settle()
                step.mark(v.tensor_scalar(rowi[:, rng], placei[:, rng], P - 1, None, ALU.bitwise_and))
                step.mark(v.tensor_scalar(tili[:, rng], placei[:, rng], 7, None, ALU.arith_shift_right))
                step.settle()
                v.tensor_copy(rowb[:, rng], rowi[:, rng]).then_inc(s_row, 1)
                step.mark(v.tensor_copy(tilf[:, rng], tili[:, rng]))

            step.mark(v.memset(texp[:], 0.0))
            assign(0)
            running_counts(0)
            places(0)
            dve.wait_ge(s_row, 1)
            row_onehots(0).then_inc(s_oh, 1)
            assign(1)
            row_onehots(1).then_inc(s_oh, 1)
            running_counts(1)
            step.mark(v.tensor_scalar(nte[:], inc[1][:, :, RANGES[1][1] - 1], float(CAPACITY), None, ALU.min))
            step.settle()
            step.mark(v.tensor_tensor(cmpk, bc(nte[:].unsqueeze(2), [P, E, IC]), bc(k128[:].unsqueeze(1), [P, E, IC]),
                                      ALU.is_gt))
            step.settle()
            step.mark(v.tensor_reduce(nte[:], cmpk, AX.X, ALU.add))
            step.settle()
            step.mark(v.tensor_tensor_scan(tend[:], one8[:], nte[:], 0.0, ALU.mult, ALU.add))
            step.settle()
            step.mark(v.tensor_tensor(tbeg[:], tend[:], nte[:], ALU.subtract))
            step.settle()
            step.mark(v.tensor_tensor(RA, Mb[:], bc(tbeg[:].unsqueeze(1), [P, NT, E]), ALU.mult))
            places(1)
            step.mark(v.tensor_reduce(begin, RA, AX.X, ALU.add))
            step.settle()
            step.mark(v.tensor_tensor(tilf, tilf, drop, ALU.add))
            step.settle()
            step.mark(v.tensor_tensor(tilb[:], tilf, begin, ALU.add))
            step.settle()
            wide = [P, NT // 2, MAX_TILES]
            for half_t in HALVES:
                v.tensor_tensor(OT[:, half_t, 0, :], bc(giota_b[:].unsqueeze(1), wide),
                                bc(tilb[:, half_t].unsqueeze(2), wide), ALU.is_equal).then_inc(s_ot, 1)
            dve.wait_ge(s_row, 2)
            for c4 in range(2, NT // OHC):
                row_onehots(c4).then_inc(s_oh, 1)
            step.mark(v.tensor_tensor(gcmp, bc(giota[:].unsqueeze(1), [P, E, MAX_TILES]),
                                      bc(tend[:].unsqueeze(2), [P, E, MAX_TILES]), ALU.is_ge))
            step.settle()
            step.mark(v.tensor_reduce(texp[:, 1:1 + MAX_TILES], gcmp.rearrange("p e g -> p g e"), AX.X, ALU.add))
            step.settle()
            step.mark(v.tensor_scalar(texp[:], texp[:], float(E - 1), None, ALU.min))
            step.settle()
            rounds3 = texp[:].rearrange("p (i c) -> p i c", c=RING)
            for c3 in range(3):
                v.tensor_copy(texpr[:, :, RING * c3:RING * c3 + RING], rounds3[:, c3:c3 + MAX_TILES // RING])
            v.tensor_copy(texpi[:], texp[:, 1:1 + MAX_TILES]).then_inc(s_te, 1)
            dve.wait_ge(s_ids, 1)
            step.mark(v.tensor_copy(idf.rearrange("p c g -> p (c g)"), PS[:, 5, 0:3 * MAX_TILES]))
            step.settle()
            step.mark(v.tensor_scalar(idg, idf[:, 1, :], float(P), None, ALU.mult))
            step.mark(v.tensor_scalar(ids, idf[:, 0, :], -float(2 * N), float(2 * N), ALU.mult, ALU.add))
            step.settle()
            step.mark(v.tensor_tensor(idg, idg, idf[:, 2, :], ALU.add))
            step.settle()
            step.mark(v.tensor_tensor(ids, ids, idg, ALU.add))
            step.mark(v.tensor_copy(idgi[:], idg))
            step.settle()
            v.tensor_copy(idsi[:], ids).then_inc(s_idx, 1)

            def expert_step(t, u, rounds=None):
                static = isinstance(t, int)
                hidden, rows = not static or t < MAX_TILES, not static or RING <= t < MAX_TILES + RING
                stats = hidden or rows
                pairs = slice(0, 2) if hidden and rows else slice(0, 1) if hidden else slice(1, 2)
                if hidden:
                    dve.wait_ge(s_h, t + 1)
                    last = v.bn_stats(st1[:, u, 0, :], PS[:, u, :])
                if rows:
                    dve.wait_ge(s_o, t - RING + 1)
                    last = v.bn_stats(st1[:, u, 1, :], PS[:, 5 + u, 0:D])
                if stats:
                    step.mark(last)
                if not static or 1 <= t <= MAX_TILES:
                    dve.wait_ge(s_rsd1, t)
                    if not static or t > RING:
                        dve.wait_ge(s_hp, t - RING)
                    w = (u - 1) % RING
                    v.tensor_scalar(NH[:, w, :], PS[:, w, :], mv1[:, w, 0, 0:1], rs1[:, w, 0:1],
                                    ALU.subtract, ALU.mult).then_inc(s_nh, 1)
                if stats:
                    step.settle()
                    v.memset(tick[:, 0:1], 0.0)
                    for q in (0, 1)[pairs]:
                        last = v.bn_aggr(mv1[:, u, q, :], st1[:, u, q, :])
                    step.mark(last)
                if not static or t > RING:
                    w = (u - 1) % RING
                    dve.wait_ge(s_rsd1, t)
                    if rounds is not None:
                        dve.wait_ge(s_sc[w], 16 * rounds)
                    v.tensor_scalar(FO[:, w, :], PS[:, 5 + w, 0:D], mv1[:, w, 1, 0:1], rs1[:, w, 1:2],
                                    ALU.subtract, ALU.mult).then_inc(s_f, 1)
                if stats:
                    step.settle()
                    v.tensor_scalar(ve1[:, u, pairs], mv1[:, u, pairs, 1], LN_EPS, None, ALU.add).then_inc(s_var1, 1)

            step.mark(v.memset(ve1[:], 1.0))
            step.settle()

            def rounds_at(t):
                done = (t - RING - 1) // RING
                return done if done > 0 else None

            for t in range(3 * RING):
                expert_step(t, t % RING, rounds_at(t))
            with nc.vector.Fori(3, MAX_TILES // RING) as i:
                step.enter(i - 3, 2 * RING)
                for u in range(RING):
                    expert_step(RING * i + u, u, i - 1 if u else i - 2)
                step.leave(MAX_TILES // RING - 3)
            for t in range(MAX_TILES, MAX_TILES + RING + 1):
                expert_step(t, t % RING, rounds_at(t))

            dve.wait_ge(s_x1b, B)
            last_units = [q for q in range(2 * B) if q not in POOL_UNITS]
            mine = {}
            for n in range(len(last_units) + 1):
                if n < len(last_units):
                    q = last_units[n]
                    dve.wait_ge(s_yl[q], 16)
                    yb = final_rows(q)
                    mine[q] = step.mark(v.tensor_tensor(yb, yb, bc(GL[:, q // 2:q // 2 + 1, :], [P, HT, D]),
                                                        ALU.mult))
                if n:
                    q = last_units[n - 1]
                    step.settle(mine[q])
                    hb = Hh[:, q // 2, HT * (q % 2):HT * (q % 2) + HT]
                    v.tensor_tensor(hb, hb, final_rows(q), ALU.add).then_inc(s_res[q], 1)

        @block.tensor
        def _(pe):
            m = nc.tensor
            pe.wait_ge(s_id, 1)
            pe.wait_ge(s_w0, 16)
            m.transpose(PS[:, 0, 0:D], inw[:, 0, :], ident[:])
            m.transpose(PS[:, 0, D:2 * D], inw[:, 1, :], ident[:])
            pe.wait_ge(s_silu, 1)
            pe.wait_ge(s_wm, 16)
            wmf = wm.rearrange("p m d -> p (m d)")
            for b in range(B):
                m.matmul(PS[:, 2 + b, 0:3 * D], bc(scT[:, b:b + 1], [P, P]), wmf[:, 0:3 * D],
                         start=True, stop=True).then_inc(s_mod, 1)
            for b in range(B):
                last = m.matmul(PS[:, 6, b * D:b * D + D], bc(scT[:, b:b + 1], [P, P]), wm[:, 5, :],
                                start=True, stop=True)
            last.then_inc(s_mod, 1)
            pe.wait_ge(s_w, 144)
            m.transpose(PS[:, 0, 2 * D:3 * D], outw, ident[:])
            m.transpose(PS[:, 0, 3 * D:4 * D], wpr[:], ident[:]).then_inc(s_ptr, 1)
            pe.wait_ge(s_etr, 1)
            m.matmul(PS[0:3, 7, 0:2 * D], bc(lnbc[:], [P, 3]), inwT[:], start=True, stop=True)
            m.matmul(PS[:, 7, 256:260], wm[:, 3, :], scT[:], start=True, stop=True)
            m.matmul(PS[:, 7, 260:264], wm[:, 4, :], scT[:], start=True, stop=True)
            m.matmul(PS[:, 7, 264:272], wprT, wgt[:], start=True, stop=True)
            m.matmul(PS[0:3, 7, 272:280], bc(bpc[:], [P, 3]), wgt[:], start=True, stop=True).then_inc(s_r1, 1)

            def rows_turn(h, q):
                pe.wait_ge(s_n, q + 1)
                for i in range(HT):
                    last = m.transpose(PS[:, h, P * i:P * i + P], NR[:, HT * h + i, :], ident[:])
                last.then_inc(s_tp, 1)

            def in_products(h, q, clear):
                pe.wait_ge(s_nt, q + 1)
                if clear:
                    pe.wait_ge(s_uze, q - 1)
                for i in range(HT):
                    dst = PS[:, 2 + 2 * h + i // 2, i % 2 * 256:i % 2 * 256 + 256]
                    m.matmul(dst, NTt[:, HT * h + i, :], inwG[:], start=True, stop=False)
                    last = m.matmul(dst, ones3[:], part_in[:], start=False, stop=True)
                last.then_inc(s_uz, 1)

            pe.wait_ge(s_me, B)
            pe.wait_ge(s_inw, 1)
            pe.wait_ge(s_r1e, 1)
            pe.wait_ge(s_one, 1)
            for h in range(2):
                rows_turn(h, h)
                in_products(h, h, False)
            with nc.tensor.Fori(1, B) as b:
                for h in range(2):
                    rows_turn(h, 2 * b + h)
                    in_products(h, 2 * b + h, True)
            pe.wait_ge(s_wge, 1)
            pe.wait_ge(s_e, 64)
            for b in range(B):
                last = m.matmul(pb_product(b), bc(cbsT[:, 0, b:b + 1], [P, 3]), WPG[:], start=True, stop=True)
            last.then_inc(s_r2, 1)
            pe.wait_ge(s_uze, 2 * B - 1)
            m.transpose(PS[:, 2, 0:QD], gb1[:, 0, :], ident[0:QD, 0:QD])
            m.transpose(PS[:, 2, QD:2 * QD], gb1[:, 1, :], ident[0:QD, 0:QD]).then_inc(s_ptr, 1)
            def inside(k):
                pe.wait_ge(s_t[k], 16 * JQ)
                for g in range(4 * k, 4 * k + 4):
                    for j in range(JQ):
                        last = m.matmul(PS[QD * j:QD * j + QD, k, g % 4 * P:g % 4 * P + P], Um[:, :, QD * j + g],
                                 T[:, SLOT[k], g % 4, j, :], start=(g % 4 == 0), stop=False, skip_group_check=True)

                last.then_inc(s_in, 1)

            pe.wait_ge(s_uze, 2 * B)
            pe.wait_ge(s_wst, 1)
            pe.wait_ge(s_me, B + 1)
            Um = U[:].rearrange("p i b d -> p (i b) d")
            for g in range(QD):
                for j in range(JQ):
                    d = QD * j + g
                    last = m.matmul(PS[QD * j:QD * j + QD, 6 + g // 16, g % 16 * QD:g % 16 * QD + QD],
                                    Wst[:, d * NS:d * NS + QD], Um[:, :, d], start=True, stop=True,
                                    skip_group_check=True)
                if g % 16 == 15:
                    last.then_inc(s_sin, 1)
                    inside(INSIDE[g // 16])
            def between(k):
                if k % 4 == 0:
                    pe.wait_ge(s_sbd[k // 4], JQ)
                for g in range(4 * k, 4 * k + 4):
                    last = m.matmul(PS[:, k, g % 4 * P:g % 4 * P + P], SBk[:, g].rearrange("p j m -> p (j m)"),
                                    V[:, g, :], start=False, stop=True, skip_group_check=True)
                last.then_inc(s_y, 1)

            def back(k):
                pe.wait_ge(s_ys, k + 1)
                for g in range(4):
                    last = m.transpose(PS[:, k, P * g:P * g + P], YS[:, k % 2, g, :], ident[:])
                last.then_inc(s_yt, 1)

            for k in INSIDE[2:TRING]:
                if k == 2:
                    pe.wait_ge(s_etr, 2)
                if k == 0:
                    pe.wait_ge(s_r2e, 1)
                inside(k)
            pe.wait_ge(s_v, 1)
            for k in range(8):
                if k >= 6:
                    inside(k)
                between(k)
                if k:
                    back(k - 1)
            back(7)

            def gated_turn(q):
                for i in range(HT):
                    last = m.transpose(PS[:, q % 2, P * i:P * i + P], Z[:, HT * (q % 2) + i, q // 2, :], ident[:])
                last.then_inc(s_tp2, 1)

            def gated_out(q):
                h = q % 2
                pe.wait_ge(s_nt2, q + 1)
                if q >= 2:
                    pe.wait_ge(s_cl, q - 1)
                for i in range(HT):
                    dst = PS[:, 2 + h, P * i:P * i + P]
                    m.matmul(dst, YT2[:, HT * h + i, :], outwT[:], start=True, stop=False)
                    last = m.matmul(dst, ones3[:], part_out[:], start=False, stop=True)
                last.then_inc(s_op, 1)

            def rows_turn2(q):
                if q < 2 * B - DVE_NORMS:
                    pe.wait_ge(s_n, 2 * B + q + 1)
                else:
                    pe.wait_ge(s_nl, q - (2 * B - DVE_NORMS) + 1)
                for i in range(HT):
                    last = m.transpose(PS[:, 4 + q % 2, P * i:P * i + P], NR[:, HT * (q % 2) + i, :], ident[:])
                last.then_inc(s_tp3, 1)

            def project(q):
                b = q // 2
                pe.wait_ge(s_nt3, q + 1)
                if q in SPARE_BANK_UNITS:
                    pe.wait_ge(s_cl, 2 * B)
                same = [p for p in range(q) if (p in SPARE_BANK_UNITS) == (q in SPARE_BANK_UNITS)]
                if same:
                    pe.wait_ge(s_pje, same[-1] + 1)
                for i in range(HT):
                    dst = proj_banks(q)[:, i // 2, i % 2 * 256:i % 2 * 256 + PJ]
                    m.matmul(dst, NTt[:, HT * (q % 2) + i, :], WPB[:, b, :], start=True, stop=False)
                    last = m.matmul(dst, ones3[:], part_pb[:, b * PJ:b * PJ + PJ], start=False, stop=True)
                last.then_inc(s_pj, 1)

            def counts(k):
                a, n = RANGES[k]
                if k == 0:
                    pe.wait_ge(s_one, 2)
                pe.wait_ge(s_m, k + 1)
                mb = Mb[:, a:a + n].rearrange("p t e -> p (t e)")
                m.matmul(PS[:, 2 * k, 0:n * E], lower[:], mb, start=True, stop=True)
                m.matmul(PS[:, 2 * k + 1, 0:n * E], onesb[:], mb, start=True, stop=True).then_inc(s_cnt, 1)

            pe.wait_ge(s_yz, 8)
            gated_turn(0)
            for q in range(2 * B + LAG + 1):
                n = q - LAG
                if q + 1 < 2 * B:
                    gated_turn(q + 1)
                if q < 2 * B:
                    gated_out(q)
                early = 2 * B - DVE_NORMS <= n < 2 * B
                if early:
                    rows_turn2(n)
                if n >= 1:
                    project(n - 1)
                if 0 <= n < 2 * B and not early:
                    rows_turn2(n)
                if n == 2 * B - 1:
                    counts(0)
            counts(1)

            for t in range(NT):
                if t % (NT // 2) == 0:
                    pe.wait_ge(s_otp, t // (NT // 2) + 1)
                    pe.wait_ge(s_ott, t // (NT // 2) + 1)
                if t % OHC == 0:
                    pe.wait_ge(s_oh, t // OHC + 1)
                last = m.matmul(PS[:, 5, 0:3 * MAX_TILES], OR[:, t, :], OT[:, t].rearrange("p c g -> p (c g)"),
                                start=(t == 0), stop=(t == NT - 1))
            last.then_inc(s_ids, 1)

            def rows_in(t, u, rounds):
                pe.wait_ge(s_g[u], 16 * rounds)
                m.transpose(PS[:, 4, 0:P], XG[:, u, :], ident[:]).then_inc(s_xp, 1)

            def experts(i, name):
                regs = [pe.alloc_register(f"experts_{name}{q}") for q in range(3 * RING)]
                pe.load(regs, texpr[0:1, bass.ds(i, 1), 0:3 * RING].rearrange("p a c -> p (a c)"))
                return [pe.snap(r, donate=True, min_val=0, max_val=E - 1) for r in regs]

            def up(t, u, e):
                pe.wait_ge(s_xt, t + 1)
                m.matmul(PS[:, u, :], XT[:, u, :], W1s[:, bass.ds(e, 1), :].rearrange("p a h -> p (a h)"),
                         start=True, stop=False)
                m.matmul(PS[:, u, :], ones3[:], BR1[:, bass.ds(e, 1), :].rearrange("p a h -> p (a h)"),
                         start=False, stop=True).then_inc(s_h, 1)

            def turn(t, u):
                pe.wait_ge(s_nh, t + 1)
                for k in range(KC):
                    last = m.transpose(PS[:, 3, P * k:P * k + P], NH[:, u, P * k:P * k + P], ident[:])
                last.then_inc(s_hp, 1)

            def down(t, u, e, first):
                dst = PS[:, 5 + u, 0:D]
                if not first:
                    pe.wait_ge(s_f, t - RING + 1)
                for k in range(KC):
                    pe.wait_ge(s_a, KC * t + k + 1)
                    m.matmul(dst, AT[:, u, k, :], W2s[:, bass.ds(e, 1), k, :].rearrange("p a d -> p (a d)"),
                             start=(k == 0), stop=False)
                m.matmul(dst, ones3[:], BR2[:, bass.ds(e, 1), :].rearrange("p a d -> p (a d)"),
                         start=False, stop=True).then_inc(s_o, 1)

            def tile_step(t, u, i, e):
                static = isinstance(i, int)
                if not static or t + 2 < MAX_TILES:
                    up(t + 2, (u + 2) % RING, e[u + RING])
                if not static or t + RING < MAX_TILES:
                    rows_in(t + RING, u, i + 2)
                if not static or t >= 1:
                    down(t - 1, (u - 1) % RING, e[u], static and t - 1 < RING)
                turn(t, u)

            pe.wait_ge(s_te, 1)
            pe.wait_ge(s_w12, 32)
            pe.wait_ge(s_br, 96)
            pe.wait_ge(s_idx, 1)
            e = experts(0, "start")
            rows_in(0, 0, 1)
            for t in range(2):
                pe.wait_ge(s_xt, t + 1)
                rows_in(t + 1, t + 1, 1)
                up(t, t, e[t + 1])
            for i in range(2):
                for u in range(RING):
                    tile_step(RING * i + u, u, i, e[RING * i:])
            with nc.tensor.Fori(1, (MAX_TILES // RING - 1) // 2) as c:
                e = experts(2 * c, "loop")
                for i in range(2):
                    for u in range(RING):
                        tile_step(2 * RING * c + RING * i + u, u, 2 * c + i, e[RING * i:])
            i = MAX_TILES // RING - 1
            e = experts(i, "end")
            for u in range(RING):
                tile_step(RING * i + u, u, i, e)
            e_last = pe.value_load(texpi[0:1, MAX_TILES - 1:MAX_TILES], min_val=0, max_val=E - 1)
            down(MAX_TILES - 1, RING - 1, e_last, False)


_INS = ['L0_attn_x', 'L0_attn_A_log', 'L0_attn_B_param', 'L0_attn_C_param', 'L0_attn_log_dt', 'L0_attn_in_w',
        'L0_attn_in_b', 'L0_attn_out_w', 'L0_attn_out_b', 'L0_attn_ln_g', 'L0_attn_ln_b', 'L0_ffn_W_proj',
        'L0_ffn_b_proj', 'L0_ffn_W_gate', 'L0_ffn_W1', 'L0_ffn_b1', 'L0_ffn_ln1_g', 'L0_ffn_ln1_b', 'L0_ffn_W2',
        'L0_ffn_b2', 'L0_ffn_ln_g', 'L0_ffn_ln_b', 'L0_c', 'L0_wmod']
_OUTS = [((4, 1024, 128), 'float32')]


def kernel(**inputs):
    import numpy as _np
    import concourse.bacc as _bacc
    from concourse import mybir as _mybir
    from concourse.bass_utils import run_bass_kernel_spmd as _run

    nc = _bacc.Bacc("TRN2", target_bir_lowering=False, num_devices=1)
    arrays, args = {}, []
    for name in _INS:
        a = _np.ascontiguousarray(inputs[name])
        arrays[f"in_{name}_dram"] = a
        args.append(nc.dram_tensor(f"in_{name}_dram", a.shape, _mybir.dt.from_np(a.dtype), kind="ExternalInput").ap())
    for i, (shape, dtype) in enumerate(_OUTS):
        dt = _mybir.dt.from_np(_np.dtype(dtype))
        args.append(nc.dram_tensor(f"out_{i}_dram", shape, dt, kind="ExternalOutput").ap())
    adaln_program(nc, *args)
    r = _run(nc, [arrays], core_ids=[0])
    got = tuple(r.results[0][f"out_{i}_dram"] for i in range(len(_OUTS)))
    return got[0]
```
